# Optimizing a Trainium2 kernel written in Bass

```python
import numpy as np
import jax
import jax.numpy as jnp

def _softmax(x, axis=-1):
    return jax.nn.softmax(x, axis=axis)

def _gelu(x):
    return jax.nn.gelu(x, approximate=True)

def _silu(x):
    return jax.nn.silu(x)

def _sigmoid(x):
    return jax.nn.sigmoid(x)

def _layernorm(x, axis=-1, eps=1e-05):
    m = jnp.mean(x, axis=axis, keepdims=True)
    v = jnp.var(x, axis=axis, keepdims=True)
    return (x - m) / jnp.sqrt(v + eps)

def _scatter_add(tgt, idx, src, axis=0):
    return tgt.at[idx].add(src)

def _segment_sum(src, seg, n):
    return jax.ops.segment_sum(src, seg, n)
kernel_name = 'mk_decoder_postln_d2_seqx_r8_d0ede3'

def setup_inputs(seed: int=0):
    np.random.seed(seed)
    _w = jnp.asarray

    def _rec_inputs():
        import jax
        import jax.numpy as jnp
        _rk = jax.random.key(seed)
        x = 7.22e-05 + 1 * jax.random.normal(jax.random.fold_in(_rk, 1), (16, 64, 512), jnp.float32)
        _lenS = 64 - jax.random.randint(jax.random.fold_in(_rk, 7), (16,), 0, max(1, 64 // 4) + 1, jnp.int32)
        _lenS2 = 64 - jax.random.randint(jax.random.fold_in(_rk, 8), (16,), 0, max(1, 64 // 4) + 1, jnp.int32)
        _ctx_4096P = jax.random.normal(jax.random.fold_in(_rk, 11), (16, 16, 512), jnp.float32)
        _ctx_4096c = jax.random.dirichlet(jax.random.fold_in(_rk, 511), 0.3 * jnp.ones((16,), jnp.float32), (16, 64))
        _ctx_4096t = jnp.einsum('bsk,bkd->bsd', _ctx_4096c, _ctx_4096P)
        _ctx_4096t = _ctx_4096t * jax.lax.rsqrt(jnp.mean(jnp.square(_ctx_4096t)) + 1e-12) * 0.953939
        ctx_4096 = 4.13588e-05 + 0.999923 * (_ctx_4096t + 0.3 * jax.random.normal(jax.random.fold_in(_rk, 611), (16, 64, 512), jnp.float32))
        return (x, ctx_4096)
    x, ctx_4096 = _rec_inputs()

    def _L0_attn_setup():
        import jax, jax.numpy as jnp
        import numpy as np
        SEQ, BATCH, HIDDEN = (256, 1, 512)
        NUM_HEADS, NUM_KV_HEADS, HEAD_DIM = (32, 8, 128)
        Q_PER_GROUP = NUM_HEADS // NUM_KV_HEADS
        TOTAL_PROJ = NUM_KV_HEADS * (Q_PER_GROUP + 2) * HEAD_DIM
        key = jax.random.key(seed)
        k1, k2, k3 = jax.random.split(key, 3)
        tokens = jax.random.normal(k1, (SEQ, BATCH, HIDDEN), dtype=jnp.float32)
        weight_qkv = jax.random.normal(k2, (TOTAL_PROJ, HIDDEN), dtype=jnp.float32) * (2.0 / (TOTAL_PROJ + HIDDEN)) ** 0.5
        weight_proj = jax.random.normal(k3, (HIDDEN, NUM_HEADS * HEAD_DIM), dtype=jnp.float32) * (2.0 / (HIDDEN + NUM_HEADS * HEAD_DIM)) ** 0.5
        return {'tokens': tokens, 'weight_qkv': weight_qkv, 'weight_proj': weight_proj}
    _L0_attn_all = _L0_attn_setup()
    _L0_attn_in = {k: v for k, v in _L0_attn_all.items() if k in ('weight_qkv', 'weight_proj')}
    del _L0_attn_all

    def _L0_xattn_setup():
        import jax, jax.numpy as jnp
        import numpy as np
        import math
        D_MODEL = 128
        NHEAD = 16
        MAX_SUP = 4
        DK = D_MODEL // NHEAD
        DM = D_MODEL * MAX_SUP
        B, S = (2, 128)
        key = jax.random.key(seed)
        ks = jax.random.split(key, 12)
        std = 0.02
        inp = {'q': jax.random.normal(ks[0], (B, S, DM), jnp.float32), 'k': jax.random.normal(ks[1], (B, S, DM), jnp.float32), 'v': jax.random.normal(ks[2], (B, S, DM), jnp.float32), 'Wq': jax.random.normal(ks[3], (DM, DM), jnp.float32) * std, 'bq': jnp.zeros((DM,), jnp.float32), 'Wk': jax.random.normal(ks[4], (DM, DM), jnp.float32) * std, 'bk': jnp.zeros((DM,), jnp.float32), 'Wv': jax.random.normal(ks[5], (DM, DM), jnp.float32) * std, 'bv': jnp.zeros((DM,), jnp.float32), 'interference': jax.random.normal(ks[6], (NHEAD, MAX_SUP, MAX_SUP), jnp.float32), 'amp': jnp.ones((1,), jnp.float32), 'Wo': jax.random.normal(ks[7], (DM, DM), jnp.float32) * std, 'bo': jnp.zeros((DM,), jnp.float32)}
        return inp
    _L0_xattn_all = _L0_xattn_setup()
    _L0_xattn_in = {k: v for k, v in _L0_xattn_all.items() if k in ('Wq', 'bq', 'Wk', 'bk', 'Wv', 'bv', 'interference', 'amp', 'Wo', 'bo')}
    del _L0_xattn_all

    def _L0_ffn_setup():
        import jax, jax.numpy as jnp
        import numpy as np

        def sparsemax(z):
            E = z.shape[-1]
            z_sorted = -jnp.sort(-z, axis=-1)
            z_cum = jnp.cumsum(z_sorted, axis=-1)
            k = jnp.arange(1, E + 1, dtype=z.dtype)
            support = 1.0 + k * z_sorted > z_cum
            k_z = jnp.sum(support, axis=-1, keepdims=True)
            tau_sum = jnp.take_along_axis(z_cum, k_z.astype(jnp.int32) - 1, axis=-1)
            tau = (tau_sum - 1.0) / k_z.astype(z.dtype)
            return jnp.maximum(z - tau, 0.0)
        key = jax.random.key(seed)
        ks = jax.random.split(key, 6)
        B, S, D_IN, D_OUT, E, R = (8, 256, 512, 512, 8, 16)
        x = jax.random.normal(ks[0], (B, S, D_IN), dtype=jnp.float32)
        W_base = jax.random.normal(ks[1], (D_OUT, D_IN), dtype=jnp.float32) * D_IN ** (-0.5)
        b_base = jax.random.normal(ks[2], (D_OUT,), dtype=jnp.float32) * 0.01
        W_router = jax.random.normal(ks[3], (E, D_IN), dtype=jnp.float32) * D_IN ** (-0.5)
        b_router = jnp.zeros((E,), dtype=jnp.float32)
        lora_A = jax.random.normal(ks[4], (E, D_IN, R), dtype=jnp.float32) * D_IN ** (-0.5)
        lora_B = jnp.zeros((E, R, D_OUT), dtype=jnp.float32)
        return {'x': x, 'W_base': W_base, 'b_base': b_base, 'W_router': W_router, 'b_router': b_router, 'lora_A': lora_A, 'lora_B': lora_B}
    _L0_ffn_all = _L0_ffn_setup()
    _L0_ffn_in = {k: v for k, v in _L0_ffn_all.items() if k in ('W_base', 'b_base', 'W_router', 'b_router', 'lora_A', 'lora_B')}
    del _L0_ffn_all

    def _L1_attn_setup():
        import math
        import jax, jax.numpy as jnp
        import numpy as np
        NUM_HEADS = 32
        NUM_KV_HEADS = 8
        HEAD_DIM = 128
        HIDDEN = 512
        ROPE_THETA = 500000.0
        ROPE_FACTOR = 8.0
        HIGH_FF = 4.0
        LOW_FF = 1.0
        ORIG_MAX_POS = 1024

        def _llama3_inv_freq():
            inv = 1.0 / ROPE_THETA ** (np.arange(0, HEAD_DIM, 2, dtype=np.float32) / HEAD_DIM)
            wavelen = 2.0 * np.pi / inv
            low_wl = ORIG_MAX_POS / LOW_FF
            high_wl = ORIG_MAX_POS / HIGH_FF
            inv_scaled = np.where(wavelen > low_wl, inv / ROPE_FACTOR, inv)
            smooth = (ORIG_MAX_POS / wavelen - LOW_FF) / (HIGH_FF - LOW_FF)
            smoothed = (1.0 - smooth) / ROPE_FACTOR * inv + smooth * inv
            is_medium = (wavelen <= low_wl) & (wavelen >= high_wl)
            return jnp.asarray(np.where(is_medium, smoothed, inv_scaled), dtype=jnp.float32)

        def _rotate_half(x):
            h = x.shape[-1] // 2
            return jnp.concatenate([-x[..., h:], x[..., :h]], axis=-1)
        key = jax.random.key(seed)
        ks = jax.random.split(key, 5)
        s = 0.02
        return {'x': jax.random.normal(ks[0], (1, 256, HIDDEN), dtype=jnp.float32), 'Wq': jax.random.normal(ks[1], (NUM_HEADS * HEAD_DIM, HIDDEN), dtype=jnp.float32) * s, 'Wk': jax.random.normal(ks[2], (NUM_KV_HEADS * HEAD_DIM, HIDDEN), dtype=jnp.float32) * s, 'Wv': jax.random.normal(ks[3], (NUM_KV_HEADS * HEAD_DIM, HIDDEN), dtype=jnp.float32) * s, 'Wo': jax.random.normal(ks[4], (HIDDEN, NUM_HEADS * HEAD_DIM), dtype=jnp.float32) * s}
    _L1_attn_all = _L1_attn_setup()
    _L1_attn_in = {k: v for k, v in _L1_attn_all.items() if k in ('Wq', 'Wk', 'Wv', 'Wo')}
    del _L1_attn_all

    def _L1_xattn_setup():
        import jax, jax.numpy as jnp
        import numpy as np
        EMBED = 512
        NUM_Q = 32
        NUM_KV = 8
        GROUPS = NUM_Q // NUM_KV
        HEAD_DIM = EMBED // NUM_Q
        KV_DIM = HEAD_DIM * NUM_KV
        key = jax.random.key(seed)
        ks = jax.random.split(key, 12)
        B, S = (2, 256)
        s = 0.02
        return {'query': jax.random.normal(ks[0], (B, S, EMBED), jnp.float32), 'key': jax.random.normal(ks[1], (B, S, EMBED), jnp.float32), 'value': jax.random.normal(ks[2], (B, S, EMBED), jnp.float32), 'Wq': jax.random.normal(ks[3], (EMBED, EMBED), jnp.float32) * s, 'bq': jnp.zeros((EMBED,), jnp.float32), 'Wk': jax.random.normal(ks[4], (EMBED, KV_DIM), jnp.float32) * s, 'bk': jnp.zeros((KV_DIM,), jnp.float32), 'Wv': jax.random.normal(ks[5], (EMBED, KV_DIM), jnp.float32) * s, 'bv': jnp.zeros((KV_DIM,), jnp.float32), 'Wo': jax.random.normal(ks[6], (EMBED, EMBED), jnp.float32) * s, 'bo': jnp.zeros((EMBED,), jnp.float32)}
    _L1_xattn_all = _L1_xattn_setup()
    _L1_xattn_in = {k: v for k, v in _L1_xattn_all.items() if k in ('Wq', 'bq', 'Wk', 'bk', 'Wv', 'bv', 'Wo', 'bo')}
    del _L1_xattn_all

    def _L1_ffn_setup():
        import jax, jax.numpy as jnp
        import numpy as np
        DIM = 512
        INTER = 128
        E = 16
        GROUPS = 4
        LIM = 2
        K = 2
        SHARED_INTER = 2 * INTER
        SCALE = 1.0
        key = jax.random.key(seed)
        ks = jax.random.split(key, 16)

        def n(k, shape, s=0.02):
            return jax.random.normal(k, shape, jnp.float32) * s
        return {'x': jax.random.normal(ks[0], (1, 256, DIM), jnp.float32), 'router_w': n(ks[1], (DIM, E)), 'router_b': n(ks[2], (E,)), 'router_bias': n(ks[3], (E,), 1.0), 'ew1': n(ks[4], (E, DIM, INTER)), 'eb1': n(ks[5], (E, INTER)), 'ew2': n(ks[6], (E, DIM, INTER)), 'eb2': n(ks[7], (E, INTER)), 'ew3': n(ks[8], (E, INTER, DIM)), 'eb3': n(ks[9], (E, DIM)), 'sw1': n(ks[10], (DIM, SHARED_INTER)), 'sb1': n(ks[11], (SHARED_INTER,)), 'sw2': n(ks[12], (DIM, SHARED_INTER)), 'sb2': n(ks[13], (SHARED_INTER,)), 'sw3': n(ks[14], (SHARED_INTER, DIM)), 'sb3': n(ks[15], (DIM,))}
    _L1_ffn_all = _L1_ffn_setup()
    _L1_ffn_in = {k: v for k, v in _L1_ffn_all.items() if k in ('router_w', 'router_b', 'router_bias', 'ew1', 'eb1', 'ew2', 'eb2', 'ew3', 'eb3', 'sw1', 'sb1', 'sw2', 'sb2', 'sw3', 'sb3')}
    del _L1_ffn_all
    return {'x': x, 'ctx_4096': ctx_4096, 'L0_attn_weight_qkv': _L0_attn_in['weight_qkv'], 'L0_attn_weight_proj': _L0_attn_in['weight_proj'], 'L0_xattn_Wq': _L0_xattn_in['Wq'], 'L0_xattn_bq': _L0_xattn_in['bq'], 'L0_xattn_Wk': _L0_xattn_in['Wk'], 'L0_xattn_bk': _L0_xattn_in['bk'], 'L0_xattn_Wv': _L0_xattn_in['Wv'], 'L0_xattn_bv': _L0_xattn_in['bv'], 'L0_xattn_interference': _L0_xattn_in['interference'], 'L0_xattn_amp': _L0_xattn_in['amp'], 'L0_xattn_Wo': _L0_xattn_in['Wo'], 'L0_xattn_bo': _L0_xattn_in['bo'], 'L0_ffn_W_base': _L0_ffn_in['W_base'], 'L0_ffn_b_base': _L0_ffn_in['b_base'], 'L0_ffn_W_router': _L0_ffn_in['W_router'], 'L0_ffn_b_router': _L0_ffn_in['b_router'], 'L0_ffn_lora_A': _L0_ffn_in['lora_A'], 'L0_ffn_lora_B': _L0_ffn_in['lora_B'], 'L1_attn_Wq': _L1_attn_in['Wq'], 'L1_attn_Wk': _L1_attn_in['Wk'], 'L1_attn_Wv': _L1_attn_in['Wv'], 'L1_attn_Wo': _L1_attn_in['Wo'], 'L1_xattn_Wq': _L1_xattn_in['Wq'], 'L1_xattn_bq': _L1_xattn_in['bq'], 'L1_xattn_Wk': _L1_xattn_in['Wk'], 'L1_xattn_bk': _L1_xattn_in['bk'], 'L1_xattn_Wv': _L1_xattn_in['Wv'], 'L1_xattn_bv': _L1_xattn_in['bv'], 'L1_xattn_Wo': _L1_xattn_in['Wo'], 'L1_xattn_bo': _L1_xattn_in['bo'], 'L1_ffn_router_w': _L1_ffn_in['router_w'], 'L1_ffn_router_b': _L1_ffn_in['router_b'], 'L1_ffn_router_bias': _L1_ffn_in['router_bias'], 'L1_ffn_ew1': _L1_ffn_in['ew1'], 'L1_ffn_eb1': _L1_ffn_in['eb1'], 'L1_ffn_ew2': _L1_ffn_in['ew2'], 'L1_ffn_eb2': _L1_ffn_in['eb2'], 'L1_ffn_ew3': _L1_ffn_in['ew3'], 'L1_ffn_eb3': _L1_ffn_in['eb3'], 'L1_ffn_sw1': _L1_ffn_in['sw1'], 'L1_ffn_sb1': _L1_ffn_in['sb1'], 'L1_ffn_sw2': _L1_ffn_in['sw2'], 'L1_ffn_sb2': _L1_ffn_in['sb2'], 'L1_ffn_sw3': _L1_ffn_in['sw3'], 'L1_ffn_sb3': _L1_ffn_in['sb3']}

def reference(x, ctx_4096, L0_attn_weight_qkv, L0_attn_weight_proj, L0_xattn_Wq, L0_xattn_bq, L0_xattn_Wk, L0_xattn_bk, L0_xattn_Wv, L0_xattn_bv, L0_xattn_interference, L0_xattn_amp, L0_xattn_Wo, L0_xattn_bo, L0_ffn_W_base, L0_ffn_b_base, L0_ffn_W_router, L0_ffn_b_router, L0_ffn_lora_A, L0_ffn_lora_B, L1_attn_Wq, L1_attn_Wk, L1_attn_Wv, L1_attn_Wo, L1_xattn_Wq, L1_xattn_bq, L1_xattn_Wk, L1_xattn_bk, L1_xattn_Wv, L1_xattn_bv, L1_xattn_Wo, L1_xattn_bo, L1_ffn_router_w, L1_ffn_router_b, L1_ffn_router_bias, L1_ffn_ew1, L1_ffn_eb1, L1_ffn_ew2, L1_ffn_eb2, L1_ffn_ew3, L1_ffn_eb3, L1_ffn_sw1, L1_ffn_sb1, L1_ffn_sw2, L1_ffn_sb2, L1_ffn_sw3, L1_ffn_sb3):
    import jax
    import jax.numpy as jnp

    def _L0_attn_ref(tokens, weight_qkv, weight_proj):
        import jax, jax.numpy as jnp
        import numpy as np
        SEQ, BATCH, HIDDEN = (256, 1, 512)
        NUM_HEADS, NUM_KV_HEADS, HEAD_DIM = (32, 8, 128)
        Q_PER_GROUP = NUM_HEADS // NUM_KV_HEADS
        TOTAL_PROJ = NUM_KV_HEADS * (Q_PER_GROUP + 2) * HEAD_DIM
        S, B, H = tokens.shape
        scale = 1.0 / HEAD_DIM ** 0.5
        qkv = jnp.einsum('sbh,ph->sbp', tokens, weight_qkv)
        qkv = qkv.reshape(S, B, NUM_KV_HEADS, Q_PER_GROUP + 2, HEAD_DIM)
        q = qkv[:, :, :, :Q_PER_GROUP, :].reshape(S, B, NUM_HEADS, HEAD_DIM)
        k = qkv[:, :, :, Q_PER_GROUP, :]
        v = qkv[:, :, :, Q_PER_GROUP + 1, :]
        k = jnp.repeat(k, Q_PER_GROUP, axis=2)
        v = jnp.repeat(v, Q_PER_GROUP, axis=2)
        q = q.transpose(1, 2, 0, 3)
        k = k.transpose(1, 2, 0, 3)
        v = v.transpose(1, 2, 0, 3)
        scores = jnp.einsum('bhsd,bhtd->bhst', q, k) * scale
        causal = jnp.tril(jnp.ones((S, S), dtype=bool))
        scores = jnp.where(causal, scores, jnp.finfo(scores.dtype).min)
        attn = jax.nn.softmax(scores, axis=-1)
        out = jnp.einsum('bhst,bhtd->bhsd', attn, v)
        out = out.transpose(2, 0, 1, 3).reshape(S, B, NUM_HEADS * HEAD_DIM)
        return jnp.einsum('sbe,he->sbh', out, weight_proj)

    def _L0_xattn_ref(q, k, v, Wq, bq, Wk, bk, Wv, bv, interference, amp, Wo, bo):
        import jax, jax.numpy as jnp
        import numpy as np
        import math
        D_MODEL = 128
        NHEAD = 16
        MAX_SUP = 4
        DK = D_MODEL // NHEAD
        DM = D_MODEL * MAX_SUP
        B, S = (2, 128)
        b, s, dm = q.shape
        H, M = (interference.shape[0], interference.shape[1])
        dk = dm // (H * M)

        def proj(x, W, bias):
            y = x @ W.T + bias
            y = y.reshape(b, s, H, dk, M)
            return jnp.transpose(y, (0, 2, 1, 3, 4))
        qh = proj(q, Wq, bq)
        kh = proj(k, Wk, bk)
        vh = proj(v, Wv, bv)

        def interfere(x):
            return x + 0.1 * amp[0] * jnp.einsum('bhsdi,hij->bhsdj', x, interference)
        qh, kh, vh = (interfere(qh), interfere(kh), interfere(vh))
        scores = jnp.einsum('bhqdm,bhkdm->bhqkm', qh, kh) / math.sqrt(dk)
        weights = jax.nn.softmax(scores, axis=3)
        out = jnp.einsum('bhqkm,bhkdm->bhqdm', weights, vh)
        out = jnp.transpose(out, (0, 2, 1, 3, 4)).reshape(b, s, dm)
        return out @ Wo.T + bo

    def _L0_ffn_ref(x, W_base, b_base, W_router, b_router, lora_A, lora_B):
        import jax, jax.numpy as jnp
        import numpy as np

        def sparsemax(z):
            E = z.shape[-1]
            z_sorted = -jnp.sort(-z, axis=-1)
            z_cum = jnp.cumsum(z_sorted, axis=-1)
            k = jnp.arange(1, E + 1, dtype=z.dtype)
            support = 1.0 + k * z_sorted > z_cum
            k_z = jnp.sum(support, axis=-1, keepdims=True)
            tau_sum = jnp.take_along_axis(z_cum, k_z.astype(jnp.int32) - 1, axis=-1)
            tau = (tau_sum - 1.0) / k_z.astype(z.dtype)
            return jnp.maximum(z - tau, 0.0)
        base_out = jnp.einsum('bsd,od->bso', x, W_base) + b_base
        logits = jnp.einsum('bsd,ed->bse', x, W_router) + b_router
        weights = sparsemax(logits)
        h = jnp.einsum('bsd,edr->bser', x, lora_A)
        expert_out = jnp.einsum('bser,bse,ero->bso', h, weights, lora_B)
        return base_out + expert_out

    def _L1_attn_ref(x, Wq, Wk, Wv, Wo):
        import math
        import jax, jax.numpy as jnp
        import numpy as np
        NUM_HEADS = 32
        NUM_KV_HEADS = 8
        HEAD_DIM = 128
        HIDDEN = 512
        ROPE_THETA = 500000.0
        ROPE_FACTOR = 8.0
        HIGH_FF = 4.0
        LOW_FF = 1.0
        ORIG_MAX_POS = 1024

        def _llama3_inv_freq():
            inv = 1.0 / ROPE_THETA ** (np.arange(0, HEAD_DIM, 2, dtype=np.float32) / HEAD_DIM)
            wavelen = 2.0 * np.pi / inv
            low_wl = ORIG_MAX_POS / LOW_FF
            high_wl = ORIG_MAX_POS / HIGH_FF
            inv_scaled = np.where(wavelen > low_wl, inv / ROPE_FACTOR, inv)
            smooth = (ORIG_MAX_POS / wavelen - LOW_FF) / (HIGH_FF - LOW_FF)
            smoothed = (1.0 - smooth) / ROPE_FACTOR * inv + smooth * inv
            is_medium = (wavelen <= low_wl) & (wavelen >= high_wl)
            return jnp.asarray(np.where(is_medium, smoothed, inv_scaled), dtype=jnp.float32)

        def _rotate_half(x):
            h = x.shape[-1] // 2
            return jnp.concatenate([-x[..., h:], x[..., :h]], axis=-1)
        B, T, _ = x.shape
        G = NUM_HEADS // NUM_KV_HEADS
        q = jnp.einsum('bth,oh->bto', x, Wq).reshape(B, T, NUM_HEADS, HEAD_DIM).transpose(0, 2, 1, 3)
        k = jnp.einsum('bth,oh->bto', x, Wk).reshape(B, T, NUM_KV_HEADS, HEAD_DIM).transpose(0, 2, 1, 3)
        v = jnp.einsum('bth,oh->bto', x, Wv).reshape(B, T, NUM_KV_HEADS, HEAD_DIM).transpose(0, 2, 1, 3)
        inv_freq = _llama3_inv_freq()
        pos = jnp.arange(T, dtype=jnp.float32)
        freqs = pos[:, None] * inv_freq[None, :]
        emb = jnp.concatenate([freqs, freqs], axis=-1)
        cos, sin = (jnp.cos(emb), jnp.sin(emb))
        q = q * cos + _rotate_half(q) * sin
        k = k * cos + _rotate_half(k) * sin
        qg = q.reshape(B, NUM_KV_HEADS, G, T, HEAD_DIM)
        scale = 1.0 / math.sqrt(HEAD_DIM)
        scores = jnp.einsum('bkgtd,bksd->bkgts', qg, k) * scale
        causal = jnp.tril(jnp.ones((T, T), dtype=bool))
        scores = jnp.where(causal, scores, -jnp.inf)
        attn = jax.nn.softmax(scores, axis=-1)
        out = jnp.einsum('bkgts,bksd->bkgtd', attn, v)
        out = out.reshape(B, NUM_HEADS, T, HEAD_DIM).transpose(0, 2, 1, 3).reshape(B, T, NUM_HEADS * HEAD_DIM)
        return jnp.einsum('bto,ho->bth', out, Wo)

    def _L1_xattn_ref(query, key, value, Wq, bq, Wk, bk, Wv, bv, Wo, bo):
        import jax, jax.numpy as jnp
        import numpy as np
        EMBED = 512
        NUM_Q = 32
        NUM_KV = 8
        GROUPS = NUM_Q // NUM_KV
        HEAD_DIM = EMBED // NUM_Q
        KV_DIM = HEAD_DIM * NUM_KV
        B, S, _ = query.shape
        Q = query @ Wq + bq
        K = key @ Wk + bk
        V = value @ Wv + bv
        Q = Q.reshape(B, S, NUM_KV, GROUPS, HEAD_DIM).transpose(0, 2, 3, 1, 4)
        K = K.reshape(B, S, NUM_KV, HEAD_DIM).transpose(0, 2, 1, 3)
        V = V.reshape(B, S, NUM_KV, HEAD_DIM).transpose(0, 2, 1, 3)
        scale = 1.0 / jnp.sqrt(jnp.asarray(HEAD_DIM, query.dtype))
        scores = jnp.einsum('bhgqd,bhkd->bhgqk', Q, K) * scale
        w = jax.nn.softmax(scores, axis=-1)
        y = jnp.einsum('bhgqk,bhkd->bhgqd', w, V)
        y = y.transpose(0, 3, 1, 2, 4).reshape(B, S, EMBED)
        return y @ Wo + bo

    def _L1_ffn_ref(x, router_w, router_b, router_bias, ew1, eb1, ew2, eb2, ew3, eb3, sw1, sb1, sw2, sb2, sw3, sb3):
        import jax, jax.numpy as jnp
        import numpy as np
        DIM = 512
        INTER = 128
        E = 16
        GROUPS = 4
        LIM = 2
        K = 2
        SHARED_INTER = 2 * INTER
        SCALE = 1.0
        shape = x.shape
        xt = x.reshape(-1, DIM)
        T = xt.shape[0]
        logits = xt @ router_w + router_b
        scores = jax.nn.softmax(logits.astype(jnp.float32), axis=-1) + router_bias
        g = scores.reshape(T, GROUPS, E // GROUPS)
        _, gidx = jax.lax.top_k(g.max(axis=-1), LIM)
        keep = jnp.zeros((T, GROUPS), bool).at[jnp.arange(T)[:, None], gidx].set(True)
        masked = jnp.where(keep[:, :, None], g, -jnp.inf).reshape(T, E)
        _, idx = jax.lax.top_k(masked, K)
        vals = (jnp.take_along_axis(scores, idx, axis=1) * SCALE).astype(x.dtype)
        gate = jnp.zeros((T, E), x.dtype).at[jnp.arange(T)[:, None], idx].add(vals)

        def step(y, p):
            w1, b1, w2, b2, w3, b3, ge = p
            h = jax.nn.silu(xt @ w1 + b1) * (xt @ w2 + b2)
            return (y + ge[:, None] * (h @ w3 + b3), None)
        y, _ = jax.lax.scan(step, jnp.zeros_like(xt), (ew1, eb1, ew2, eb2, ew3, eb3, gate.T))
        z = jax.nn.silu(xt @ sw1 + sb1) * (xt @ sw2 + sb2) @ sw3 + sb3
        return (y + z).reshape(shape)
    x = _layernorm(x + _L0_attn_ref(x, L0_attn_weight_qkv, L0_attn_weight_proj), axis=-1)
    x = _layernorm(x + _L0_xattn_ref(x, ctx_4096, ctx_4096, L0_xattn_Wq, L0_xattn_bq, L0_xattn_Wk, L0_xattn_bk, L0_xattn_Wv, L0_xattn_bv, L0_xattn_interference, L0_xattn_amp, L0_xattn_Wo, L0_xattn_bo), axis=-1)
    x = _layernorm(x + _L0_ffn_ref(x, L0_ffn_W_base, L0_ffn_b_base, L0_ffn_W_router, L0_ffn_b_router, L0_ffn_lora_A, L0_ffn_lora_B), axis=-1)
    x = _layernorm(x + _L1_attn_ref(x, L1_attn_Wq, L1_attn_Wk, L1_attn_Wv, L1_attn_Wo), axis=-1)
    x = _layernorm(x + _L1_xattn_ref(x, ctx_4096, ctx_4096, L1_xattn_Wq, L1_xattn_bq, L1_xattn_Wk, L1_xattn_bk, L1_xattn_Wv, L1_xattn_bv, L1_xattn_Wo, L1_xattn_bo), axis=-1)
    x = _layernorm(x + _L1_ffn_ref(x, L1_ffn_router_w, L1_ffn_router_b, L1_ffn_router_bias, L1_ffn_ew1, L1_ffn_eb1, L1_ffn_ew2, L1_ffn_eb2, L1_ffn_ew3, L1_ffn_eb3, L1_ffn_sw1, L1_ffn_sb1, L1_ffn_sw2, L1_ffn_sb2, L1_ffn_sw3, L1_ffn_sb3), axis=-1)
    return x

_drawn_inputs = setup_inputs


def setup_inputs(seed=0):
    import zlib

    import numpy as np

    out = dict(_drawn_inputs(seed))
    spreads = {'L0_xattn_bq': (0.0, 0.8),
     'L0_xattn_bk': (0.0, 2.0),
     'L0_xattn_bv': (0.0, 0.1),
     'L0_xattn_bo': (0.0, 0.1),
     'L0_ffn_b_router': (0.0, 0.52),
     'L0_ffn_lora_B': (0.0, 0.1),
     'L1_xattn_bq': (0.0, 0.8),
     'L1_xattn_bk': (0.0, 2.0),
     'L1_xattn_bv': (0.0, 0.1),
     'L1_xattn_bo': (0.0, 0.1)}
    factors = {'L0_xattn_Wq': 6.306,
     'L0_xattn_Wk': 6.038,
     'L0_ffn_b_base': 7.821,
     'L1_xattn_Wq': 6.952,
     'L1_xattn_Wk': 6.677,
     'L1_ffn_router_w': 8.0,
     'L1_ffn_router_b': 141.559,
     'L1_ffn_eb1': 8.0,
     'L1_ffn_eb2': 8.0,
     'L1_ffn_sb1': 34.591,
     'L1_ffn_sb2': 32.691,
     'L1_ffn_sb3': 2.859}
    for name, (base, spread) in spreads.items():
        noise = np.random.default_rng([zlib.crc32(name.encode()), seed]).standard_normal(out[name].shape)
        drawn = base * np.exp(spread * noise) if base else spread * noise
        out[name] = jnp.asarray(drawn.astype(out[name].dtype))
    for name, factor in factors.items():
        out[name] = (out[name] * factor).astype(out[name].dtype)
    return out
```

```python
from contextlib import ExitStack

import numpy as np

import concourse.bass as bass
from concourse import mybir

F32 = mybir.dt.float32
F32R = mybir.dt.float32r
BF16 = mybir.dt.bfloat16
ALU = mybir.AluOpType
ACT = mybir.ActivationFunctionType
AX = mybir.AxisListType

P = 128
SEQ_A, SEQ_B, DM = 16, 64, 512
TOK = SEQ_A * SEQ_B
KC = DM // P
NT = TOK // P
HALF = TOK // 2
GROUPS, QPG, HD = 8, 4, 128
CH = QPG + 2
EPS = 1e-5
MASKED = -1e30




def wait(engine, semaphore, value):
    if isinstance(value, int) and value <= 0:
        return
    engine.wait_ge(semaphore, value)


def three_pass(pe, out, w_hi, w_lo, x_hi, x_lo, start, stop):
    pe.matmul(out, w_hi, x_hi, start=start, stop=False, skip_group_check=True)
    pe.matmul(out, w_hi, x_lo, start=False, stop=False, skip_group_check=True)
    return pe.matmul(out, w_lo, x_hi, start=False, stop=stop, skip_group_check=True)


class Phase:

    def __init__(self, nc, ctx, name):
        self.nc, self.ctx, self.name = nc, ctx, name
        self.semaphores = []

    def sb(self, name, shape, dt=F32):
        return self.ctx.enter_context(self.nc.sbuf_tensor(f"{self.name}_{name}", shape, dt))

    def ps(self, name, shape, dt=F32):
        return self.ctx.enter_context(self.nc.psum_tensor(f"{self.name}_{name}", shape, dt))

    def sem(self, name):
        self.semaphores.append(self.nc.alloc_semaphore(name=f"{self.name}_{name}"))
        return self.semaphores[-1]

    def close(self):
        self.nc.clear_and_free_semaphores(self.semaphores)
        self.nc.all_engine_barrier()


def attention_phase(nc, name, S, w_dram, wo_dram, mask_dram, layer0, xT_raw_dram=None, rope_dram=None):
    scale = float(HD) ** -0.5
    with ExitStack() as ctx:
        ph = Phase(nc, ctx, name)
        sb, ps, sem = ph.sb, ph.ps, ph.sem
        QT = sb("QT", [P, 2, QPG, HALF])
        KT = sb("KT", [P, 2, HALF])
        VT = sb("VT", [P, HALF])
        V = sb("V", [P, 2, 4, HD])
        W_raw = sb("W_raw", [P, CH, KC, P])
        W_hi = sb("W_hi", [P, CH, KC, P], F32R)
        W_lo = sb("W_lo", [P, CH, KC, P], F32R)
        Wo_raw = sb("Wo_raw", [P, QPG, DM])
        Wo_hi = sb("Wo_hi", [P, QPG, DM], F32R)
        Wo_lo = sb("Wo_lo", [P, QPG, DM], F32R)
        O_hi = sb("O_hi", [P, 2, QPG, HALF], F32R)
        O_lo = sb("O_lo", [P, 2, QPG, HALF], F32R)
        prob = sb("prob", [P, 2, QPG, P])
        probT = sb("probT", [P, 2, QPG, P])
        top = sb("top", [P, 2, QPG])
        total = sb("total", [P, 2, QPG])
        inv = sb("inv", [P, 2, QPG])
        mask = sb("mask", [P, P], BF16)
        if not layer0:
            cos = sb("cos", [P, SEQ_B])
            sin = sb("sin", [P, SEQ_B])
            r_cos = sb("r_cos", [P, 2, HALF])
            r_sin = sb("r_sin", [P, 2, HALF])
        pA = ps("pA", [P, 2, HALF])
        pS = ps("pS", [P, QPG, P])
        pP = ps("pP", [P, QPG, P])
        pV = ps("pV", [P, 4, HD])
        pO = ps("pO", [P, QPG, P])
        pC = ps("pC", [P, 2, DM])
        mask_loaded = sem("mask_loaded")
        xT_loaded = sem("xT_loaded")
        xT_hi_done = sem("xT_hi_done")
        xT_lo_done = sem("xT_lo_done")
        w_loaded = sem("w_loaded")
        wo_loaded = sem("wo_loaded")
        w_hi_done = sem("w_hi_done")
        w_lo_done = sem("w_lo_done")
        wo_hi_done = sem("wo_hi_done")
        wo_lo_done = sem("wo_lo_done")
        proj_done = sem("proj_done")
        chunk_read = [sem("chunk_read0"), sem("chunk_read1")]
        cos_done = sem("cos_done")
        rope_done = sem("rope_done")
        v_turned = sem("v_turned")
        v_ready = sem("v_ready")
        scores_done = sem("scores_done")
        top_done = sem("top_done")
        shifted = sem("shifted")
        exp_done = sem("exp_done")
        total_done = sem("total_done")
        inv_done = sem("inv_done")
        prob_ready = sem("prob_ready")
        prob_turned = sem("prob_turned")
        probT_ready = sem("probT_ready")
        av_done = sem("av_done")
        o_hi_done = sem("o_hi_done")
        o_lo_done = sem("o_lo_done")
        out_done = sem("out_done")
        summed = sem("summed")

        def o_tile(O, u2, t):
            if layer0:
                return O[:, u2].rearrange("p h (a t b) -> p h t b a", t=4, b=8)[:, :, t]
            return O[:, u2, :, t * P:(t + 1) * P]

        def po_view():
            if layer0:
                return pO[:, :, :].rearrange("p h (b a) -> p h b a", a=SEQ_A)
            return pO[:, :, :]

        def o_columns(O, u2, h, t):
            return O[:, u2, h, t * P:(t + 1) * P]

        def head_sum(ap):
            return ap.unsqueeze(2).broadcast_to([P, QPG, P])

        def loop(engine, body):
            body(0)
            with engine.Fori(1, GROUPS - 1) as g:
                body(g)
            body(GROUPS - 1)

        def is_last(g, hf):
            return isinstance(g, int) and g == GROUPS - 1 and hf == 1

        def is_first(g, hf):
            return isinstance(g, int) and g == 0 and hf == 0

        with nc.Block() as block:

            @block.sync
            def _(sp):
                sp.dma_start(W_raw[:].rearrange("p c k n -> p (c k n)"), w_dram[0]).then_inc(w_loaded, 16)
                if layer0:
                    sp.dma_start(QT[:].rearrange("p u h n -> p (u h n)"), xT_raw_dram).then_inc(xT_loaded, 16)
                sp.dma_start(mask[:], mask_dram).then_inc(mask_loaded, 16)
                if not layer0:
                    sp.dma_start(cos[:], rope_dram[0]).then_inc(mask_loaded, 16)
                    sp.dma_start(sin[:], rope_dram[1]).then_inc(mask_loaded, 16)
                sp.dma_start(Wo_raw[:].rearrange("p h n -> p (h n)"), wo_dram[0]).then_inc(wo_loaded, 16)

                def body(g):
                    sp.wait_ge(w_hi_done, CH * g)
                    sp.wait_ge(w_lo_done, CH * g)
                    sp.dma_start(W_raw[:].rearrange("p c k n -> p (c k n)"), w_dram[g]).then_inc(w_loaded, 16)
                    sp.wait_ge(wo_hi_done, QPG * g)
                    sp.wait_ge(wo_lo_done, QPG * g)
                    sp.dma_start(Wo_raw[:].rearrange("p h n -> p (h n)"), wo_dram[g]).then_inc(wo_loaded, 16)

                with sp.Fori(1, GROUPS) as g:
                    body(g)

            @block.tensor
            def _(pe):
                def project(u, g, hf, c):
                    pe.wait_ge(w_hi_done, CH * g + c + 1)
                    pe.wait_ge(w_lo_done, CH * g + c + 1)
                    wait(pe, chunk_read[c % 2], 3 * u + c // 2)
                    tok = slice(hf * HALF, (hf + 1) * HALF)
                    for k in range(KC):
                        mm = three_pass(pe, pA[:, c % 2, :], W_hi[:, c, k, :], W_lo[:, c, k, :],
                                        S.xT_hi[:, k, tok], S.xT_lo[:, k, tok], k == 0, k == KC - 1)
                    mm.then_inc(proj_done, 1)

                def turn_v(u, hf):
                    wait(pe, v_ready, u)
                    pe.wait_ge(chunk_read[1], 3 * u + 1)
                    for t in range(4):
                        mm = pe.transpose(pV[:, t, :], VT[:, t * P:(t + 1) * P], S.ident[:])
                    mm.then_inc(v_turned, 1)

                def scores(u, hf, t):
                    wait(pe, shifted, 4 * u + t)
                    if t == 0:
                        if layer0:
                            pe.wait_ge(chunk_read[0], 3 * u + 3)
                            pe.wait_ge(chunk_read[1], 3 * u + 3)
                        else:
                            pe.wait_ge(rope_done, 5 * u + 5)
                    pe.matmul(pS[:, :, :], S.ident_bf[:], mask[:].unsqueeze(1).broadcast_to([P, QPG, P]),
                              start=True, stop=False, skip_group_check=True)
                    cols = slice(t * P, (t + 1) * P)
                    for h in range(QPG):
                        mm = pe.matmul(pS[:, h, :], QT[:, hf, h, cols], KT[:, hf, cols],
                                       start=False, stop=h == QPG - 1, skip_group_check=True)
                    mm.then_inc(scores_done, 1)

                def turn_probs(u, t):
                    n = 4 * u + t
                    pe.wait_ge(prob_ready, n + 1)
                    wait(pe, probT_ready, n)
                    for h in range(QPG):
                        mm = pe.transpose(pP[:, h, :], prob[:, t % 2, h, :], S.ident[:])
                    mm.then_inc(prob_turned, 1)

                def attend(u, hf, t):
                    n = 4 * u + t
                    pe.wait_ge(probT_ready, n + 1)
                    if t == 0:
                        pe.wait_ge(v_ready, u + 1)
                    wait(pe, o_lo_done, n)
                    pe.matmul(pO[:, :, :], V[:, hf, t, :], probT[:, t % 2, :, :],
                              start=True, stop=True).then_inc(av_done, 1)

                def out_project(u, g, hf, t):
                    n = 4 * u + t
                    if t == 0:
                        pe.wait_ge(o_lo_done, 4 * u + 4)
                        if hf == 0:
                            pe.wait_ge(wo_hi_done, QPG * (g + 1))
                            pe.wait_ge(wo_lo_done, QPG * (g + 1))
                    wait(pe, summed, n - 1)
                    for h in range(QPG):
                        mm = three_pass(pe, pC[:, t % 2, :], o_columns(O_hi, hf, h, t), o_columns(O_lo, hf, h, t),
                                        Wo_hi[:, h, :], Wo_lo[:, h, :], h == 0, h == QPG - 1)
                    mm.then_inc(out_done, 1)

                if layer0:
                    pe.wait_ge(xT_hi_done, KC)
                    pe.wait_ge(xT_lo_done, KC)
                for c in range(CH):
                    project(0, 0, 0, c)
                turn_v(0, 0)
                pe.wait_ge(mask_loaded, 16 if layer0 else 48)
                scores(0, 0, 0)

                def body(g):
                    for hf in range(2):
                        u = 2 * g + hf
                        last = is_last(g, hf)
                        for t in range(4):
                            if t == 3:
                                if not is_first(g, hf):
                                    out_project(u - 1, g - 1 + hf, 1 - hf, t)
                                if not last:
                                    scores(u + 1, 1 - hf, 0)
                                turn_probs(u, t)
                                if not last:
                                    turn_v(u + 1, 1 - hf)
                            else:
                                scores(u, hf, t + 1)
                                turn_probs(u, t)
                                if not last:
                                    for c in (2 * t, 2 * t + 1):
                                        project(u + 1, g + hf, 1 - hf, c)
                                if not is_first(g, hf):
                                    out_project(u - 1, g - 1 + hf, 1 - hf, t)
                            attend(u, hf, t)

                loop(pe, body)
                for t in range(4):
                    out_project(2 * GROUPS - 1, GROUPS - 1, 1, t)

            @block.scalar
            def _(act):
                def split_w(g, c):
                    if c == 0:
                        act.wait_ge(w_loaded, 16 * (g + 1))
                    if not (isinstance(g, int) and g == 0):
                        act.wait_ge(proj_done, CH * (2 * g - 1) + c + 1)
                    nc.scalar.copy(W_hi[:, c], W_raw[:, c]).then_inc(w_hi_done, 1)

                def split_wo(g):
                    act.wait_ge(wo_loaded, 16 * (g + 1))
                    if not (isinstance(g, int) and g == 0):
                        act.wait_ge(out_done, 8 * g)
                    for h in range(QPG):
                        nc.scalar.copy(Wo_hi[:, h], Wo_raw[:, h]).then_inc(wo_hi_done, 1)

                def read_chunk(u, hf, c):
                    if not layer0 and c != 1:
                        return
                    act.wait_ge(proj_done, CH * u + c + 1)
                    if c == 1:
                        wait(act, v_turned, u)
                        dst = VT[:, :]
                    else:
                        wait(act, scores_done, 4 * u - 4)
                        dst = KT[:, hf, :] if c == 0 else QT[:, hf, c - 2, :]
                    nc.scalar.copy(dst, pA[:, c % 2, :]).then_inc(chunk_read[c % 2], 1)

                def read_v(u, hf):
                    act.wait_ge(v_turned, u + 1)
                    wait(act, av_done, 4 * u - 4)
                    nc.scalar.copy(V[:, hf], pV[:, :, :]).then_inc(v_ready, 1)

                def exponent(u, t):
                    n = 4 * u + t
                    act.wait_ge(shifted, n + 1)
                    nc.scalar.activation(prob[:, t % 2], prob[:, t % 2], ACT.Exp, scale=scale).then_inc(exp_done, 1)

                def read_probT(u, t):
                    n = 4 * u + t
                    act.wait_ge(prob_turned, n + 1)
                    wait(act, av_done, n - 1)
                    nc.scalar.copy(probT[:, t % 2], pP[:, :, :]).then_inc(probT_ready, 1)

                def read_o(u, hf, t):
                    n = 4 * u + t
                    act.wait_ge(av_done, n + 1)
                    wait(act, out_done, 4 * u - 4)
                    nc.scalar.copy(o_tile(O_hi, hf, t), po_view()).then_inc(o_hi_done, 1)

                if layer0:
                    act.wait_ge(xT_loaded, 16)
                    for k in range(KC):
                        nc.scalar.copy(S.xT_hi[:, k], QT[:].rearrange("p u h n -> p (u h n)")[:, k * TOK:(k + 1) * TOK]
                                       ).then_inc(xT_hi_done, 1)
                for c in range(CH):
                    split_w(0, c)
                if layer0:
                    act.wait_ge(xT_lo_done, KC)
                for c in range(CH):
                    read_chunk(0, 0, c)
                read_v(0, 0)
                exponent(0, 0)

                def body(g):
                    for hf in range(2):
                        u = 2 * g + hf
                        last = is_last(g, hf)
                        for t in range(4):
                            read_probT(u, t)
                            if t < 3:
                                exponent(u, t + 1)
                                if not last:
                                    for c in (2 * t, 2 * t + 1):
                                        read_chunk(u + 1, 1 - hf, c)
                                        if hf == 0 and not (isinstance(g, int) and g == GROUPS - 1):
                                            split_w(g + 1, c)
                            elif not last:
                                exponent(u + 1, 0)
                                read_v(u + 1, 1 - hf)
                            read_o(u, hf, t)
                        if hf == 0:
                            split_wo(g)

                loop(act, body)

            @block.vector
            def _(dve):
                def soften(u, t):
                    n = 4 * u + t
                    dve.wait_ge(scores_done, n + 1)
                    nc.vector.tensor_reduce(top[:, t % 2], pS[:, :, :], AX.X, ALU.max).then_inc(top_done, 1)
                    dve.wait_ge(top_done, n + 1)
                    wait(dve, prob_turned, n - 1)
                    nc.vector.tensor_tensor(prob[:, t % 2], pS[:, :, :], head_sum(top[:, t % 2]),
                                            ALU.subtract).then_inc(shifted, 1)

                def row_totals(u, t):
                    n = 4 * u + t
                    dve.wait_ge(exp_done, n + 1)
                    nc.vector.tensor_reduce(total[:, t % 2], prob[:, t % 2], AX.X, ALU.add).then_inc(total_done, 1)
                    dve.wait_ge(total_done, n + 1)
                    wait(dve, prob_ready, n - 1)
                    nc.vector.reciprocal(inv[:, t % 2], total[:, t % 2]).then_inc(inv_done, 1)

                def rope(u, c):
                    if layer0 or c == 1:
                        return
                    i = 0 if c == 0 else c - 1
                    m = 5 * u + i
                    slot = RS[0]
                    RS[0] = 1 - RS[0]
                    dve.wait_ge(proj_done, CH * u + c + 1)
                    wait(dve, rope_done, m - 1)
                    src = pA[:, c % 2, :].rearrange("p (a b) -> p a b", b=SEQ_B)
                    rc = r_cos[:, slot].rearrange("p (a b) -> p a b", b=SEQ_B)
                    rs = r_sin[:, slot].rearrange("p (a b) -> p a b", b=SEQ_B)
                    n_a = HALF // SEQ_B
                    h = HD // 2
                    nc.vector.tensor_tensor(rc, src, cos[:].unsqueeze(1).broadcast_to([P, n_a, SEQ_B]), ALU.mult)
                    nc.vector.tensor_tensor(rs[0:h], src[h:P], sin[h:P].unsqueeze(1).broadcast_to([h, n_a, SEQ_B]), ALU.mult)
                    nc.vector.tensor_tensor(rs[h:P], src[0:h], sin[0:h].unsqueeze(1).broadcast_to([h, n_a, SEQ_B]),
                                            ALU.mult).then_inc(chunk_read[c % 2], 1)

                def read_o_lo(u, hf, t):
                    n = 4 * u + t
                    dve.wait_ge(o_hi_done, n + 1)
                    nc.vector.tensor_tensor(o_tile(O_lo, hf, t), po_view(), o_tile(O_hi, hf, t).bitcast(F32),
                                            ALU.subtract).then_inc(o_lo_done, 1)

                def add_out(u, hf, t):
                    n = 4 * u + t
                    dve.wait_ge(out_done, n + 1)
                    wait(dve, summed, n - 3)
                    T = 4 * hf + t
                    nc.vector.tensor_tensor(S.x[:, T], pC[:, t % 2, :], S.x[:, T], ALU.add).then_inc(summed, 1)

                RS = [0]
                if layer0:
                    for k in range(KC):
                        dve.wait_ge(xT_hi_done, k + 1)
                        nc.vector.tensor_tensor(S.xT_lo[:, k],
                                                QT[:].rearrange("p u h n -> p (u h n)")[:, k * TOK:(k + 1) * TOK],
                                                S.xT_hi[:, k].bitcast(F32), ALU.subtract).then_inc(xT_lo_done, 1)
                else:
                    dve.wait_ge(mask_loaded, 48)
                for c in range(CH):
                    rope(0, c)
                soften(0, 0)
                row_totals(0, 0)

                def body(g):
                    for hf in range(2):
                        u = 2 * g + hf
                        last = is_last(g, hf)
                        for t in range(4):
                            if t < 3:
                                soften(u, t + 1)
                                if not last:
                                    rope(u + 1, 2 * t)
                                row_totals(u, t + 1)
                                if not last:
                                    rope(u + 1, 2 * t + 1)
                                if not is_first(g, hf):
                                    add_out(u - 1, 1 - hf, t)
                            else:
                                if not is_first(g, hf):
                                    add_out(u - 1, 1 - hf, t)
                                if not last:
                                    soften(u + 1, 0)
                                    row_totals(u + 1, 0)
                            read_o_lo(u, hf, t)

                loop(dve, body)
                for t in range(4):
                    add_out(2 * GROUPS - 1, 1, t)

            @block.gpsimd
            def _(pool):
                def split_w(g, c):
                    pool.wait_ge(w_hi_done, CH * g + c + 1)
                    if not (isinstance(g, int) and g == 0):
                        pool.wait_ge(proj_done, CH * (2 * g - 1) + c + 1)
                    nc.gpsimd.tensor_tensor(W_lo[:, c], W_raw[:, c], W_hi[:, c].bitcast(F32),
                                            ALU.subtract).then_inc(w_lo_done, 1)

                def split_wo(g):
                    if not (isinstance(g, int) and g == 0):
                        pool.wait_ge(out_done, 8 * g)
                    for h in range(QPG):
                        pool.wait_ge(wo_hi_done, QPG * g + h + 1)
                        nc.gpsimd.tensor_tensor(Wo_lo[:, h], Wo_raw[:, h], Wo_hi[:, h].bitcast(F32),
                                                ALU.subtract).then_inc(wo_lo_done, 1)

                def divide(u, t):
                    n = 4 * u + t
                    pool.wait_ge(inv_done, n + 1)
                    nc.gpsimd.tensor_tensor(prob[:, t % 2], prob[:, t % 2], head_sum(inv[:, t % 2]),
                                            ALU.mult).then_inc(prob_ready, 1)

                def rope_add(u, hf, c):
                    if layer0 or c == 1:
                        return
                    slot = RS[0]
                    RS[0] = 1 - RS[0]
                    pool.wait_ge(chunk_read[c % 2], 3 * u + c // 2 + 1)
                    wait(pool, scores_done, 4 * u - 4)
                    dst = KT[:, hf, :] if c == 0 else QT[:, hf, c - 2, :]
                    nc.gpsimd.tensor_tensor(dst, r_cos[:, slot], r_sin[:, slot], ALU.add).then_inc(rope_done, 1)

                RS = [0]
                for c in range(CH):
                    split_w(0, c)
                for c in range(CH):
                    rope_add(0, 0, c)
                divide(0, 0)

                def body(g):
                    for hf in range(2):
                        u = 2 * g + hf
                        last = is_last(g, hf)
                        for t in range(4):
                            if t < 3:
                                if not last:
                                    rope_add(u + 1, 1 - hf, 2 * t)
                                divide(u, t + 1)
                                if not last:
                                    rope_add(u + 1, 1 - hf, 2 * t + 1)
                                    if hf == 0 and not (isinstance(g, int) and g == GROUPS - 1):
                                        split_w(g + 1, 2 * t)
                                        split_w(g + 1, 2 * t + 1)
                            elif not last:
                                divide(u + 1, 0)
                        if hf == 0:
                            split_wo(g)

                loop(pool, body)
        ph.close()


class State:
    pass


def norm_phase(nc, name, S, out_dram=None, split_rows=False):
    turn = out_dram is None or split_rows

    with ExitStack() as ctx:
        ph = Phase(nc, ctx, name)
        stats = ph.sb("stats", [P, NT, 6])
        mv = ph.sb("mv", [P, NT, 2])
        var = ph.sb("var", [P, NT])
        dev = ph.sb("dev", [P, NT])
        rstd = ph.sb("rstd", [P, NT])
        newton = ph.sb("newton", [P, NT])
        pT = ph.ps("pT", [P, 4, KC, P])
        names = ("stats_done", "mv_done", "dev_done", "step", "normed", "turned", "hi_done", "lo_done", "stored")
        stats_done, mv_done, dev_done, step, normed, turned, hi_done, lo_done, stored = map(ph.sem, names)

        def parts(xT, T):
            if not split_rows:
                return [(xT[:, :, T * P:(T + 1) * P], pT[:, T % 4])]
            hb, r = divmod(T, 4)
            to = xT[:].rearrange("p k (r a h b) -> p k r h a b", r=4, a=4, h=2)[:, :, r, hb]
            return [(to[:, k], pT[:, T % 4, k].rearrange("p (a b) -> p a b", a=4)) for k in range(KC)]

        with nc.Block() as block:

            @block.vector
            def _(dve):
                def small(n, instruction):
                    instruction.then_inc(step, 1)
                    dve.wait_ge(step, n)

                for T in range(NT):
                    nc.vector.bn_stats(stats[:, T], S.x[:, T]).then_inc(stats_done, 1)
                for T in range(NT):
                    dve.wait_ge(stats_done, T + 1)
                    nc.vector.bn_aggr(mv[:, T], stats[:, T]).then_inc(mv_done, 1)
                dve.wait_ge(mv_done, NT)
                small(1, nc.vector.tensor_scalar(var[:], mv[:, :, 1], EPS, None, ALU.add))
                dve.wait_ge(dev_done, 1)
                small(2, nc.vector.reciprocal(rstd[:], dev[:]))
                small(3, nc.vector.tensor_tensor(newton[:], rstd[:], rstd[:], ALU.mult))
                small(4, nc.vector.tensor_tensor(newton[:], newton[:], var[:], ALU.mult))
                small(5, nc.vector.tensor_scalar(newton[:], newton[:], -0.5, 1.5, ALU.mult, ALU.add))
                small(6, nc.vector.tensor_tensor(rstd[:], rstd[:], newton[:], ALU.mult))

                def scale_rows(T):
                    nc.vector.tensor_scalar(S.x[:, T], S.x[:, T], mv[:, T, 0:1], rstd[:, T:T + 1], ALU.subtract,
                                            ALU.mult).then_inc(normed, 1)

                def low(T):
                    dve.wait_ge(hi_done, T + 1)
                    for (lo, bank), (hi, _) in zip(parts(S.xT_lo, T), parts(S.xT_hi, T)):
                        ins = nc.vector.tensor_tensor(lo, bank, hi.bitcast(F32), ALU.subtract)
                    ins.then_inc(lo_done, 1)

                for T in range(NT + 2):
                    if T < NT:
                        scale_rows(T)
                    if T >= 2 and turn:
                        low(T - 2)

            @block.scalar
            def _(act):
                act.wait_ge(step, 1)
                nc.scalar.activation(dev[:], var[:], ACT.Sqrt).then_inc(dev_done, 1)
                if turn:
                    for T in range(NT):
                        act.wait_ge(turned, T + 1)
                        for hi, bank in parts(S.xT_hi, T):
                            ins = nc.scalar.copy(hi, bank)
                        ins.then_inc(hi_done, 1)

            if turn:
                @block.tensor
                def _(pe):
                    for T in range(NT):
                        pe.wait_ge(normed, T + 1)
                        wait(pe, lo_done, T - 3)
                        for k in range(KC):
                            mm = pe.transpose(pT[:, T % 4, k], S.x[:, T, k * P:(k + 1) * P], S.ident[:])
                        mm.then_inc(turned, 1)

            if out_dram is not None:
                @block.sync
                def _(sp):
                    for T in range(NT):
                        sp.wait_ge(normed, T + 1)
                        if split_rows:
                            hb, r = divmod(T, 4)
                            dst = out_dram.rearrange("t (a h b) n -> h t a b n", a=2, h=2)[hb, 2 * r:2 * r + 2]
                            for t2 in range(2):
                                for a2 in range(2):
                                    a4 = 2 * t2 + a2
                                    sp.dma_start(dst[t2, a2], S.x[32 * a4:32 * a4 + 32, T]).then_inc(stored, 16)
                        else:
                            sp.dma_start(out_dram[T], S.x[:, T]).then_inc(stored, 16)
                    sp.wait_ge(stored, 16 * NT * (4 if split_rows else 1))
        ph.close()


def cross_attention_phase(nc, name, S, d, rows_per_unit, x_dram=None):
    mixed = rows_per_unit == 32
    units = DM // rows_per_unit
    W = units // 2
    scale = float(8 if mixed else 16) ** -0.5
    fills = 2 if mixed else 1
    SB = SEQ_B
    with ExitStack() as ctx:
        ph = Phase(nc, ctx, name)
        sb, ps, sem = ph.sb, ph.ps, ph.sem
        with ExitStack() as early:
            ph_early = Phase(nc, early, name)
            ctx_hi = ph_early.sb("ctx_hi", [P, KC, TOK], F32R)
            ctx_lo = ph_early.sb("ctx_lo", [P, KC, TOK], F32R)
        Kmask = sb("Kmask", [P, 2, KC, 4, P])
        Vmask = sb("Vmask", [P, 2, 2, 2, DM])
        W_raw = sb("W_raw", [P, KC, DM])
        W_hi = sb("W_hi", [P, KC, DM], F32R)
        W_lo = sb("W_lo", [P, KC, DM], F32R)
        QT = sb("QT", [P, KC, TOK])
        KT = sb("KT", [P, KC, TOK])
        VT = sb("VT", [P, KC, TOK])
        Qtile = sb("Qtile", [P, 2, KC, P])
        Vtile = sb("Vtile", [P, KC, P])
        prob = sb("prob", [P, 4, 8, SB])
        probT = sb("probT", [P, 2, 4, P])
        top = sb("top", [P, 4, 8])
        total = sb("total", [P, 4, 8])
        inv = sb("inv", [P, 4, 8])
        kmask = sb("kmask", [P, 4])
        vmask = sb("vmask", [P, 2, DM], BF16)
        biases = sb("biases", [P, 3, KC])
        bo = sb("bo", [P, DM])
        if mixed:
            inter = sb("inter", [P, KC, 4])
            amp = sb("amp", [P, 1])
            same = sb("same", [P, 32])
            mix = sb("mix", [P, KC, P])
        pM = ps("pM", [P, 2, DM])
        pS = ps("pS", [P, 2, DM])
        pP = ps("pP", [P, 4, P])
        pO = ps("pO", [P, 2, KC, P])
        small_loaded = sem("small_loaded")
        ctx_loaded = sem("ctx_loaded")
        x_loaded = sem("x_loaded")
        x_biased = sem("x_biased")
        ctx_hi_done = sem("ctx_hi_done")
        ctx_lo_done = sem("ctx_lo_done")
        w_loaded = sem("w_loaded")
        w_hi_done = sem("w_hi_done")
        w_lo_done = sem("w_lo_done")
        mix_step = sem("mix_step")
        proj_done = sem("proj_done")
        bank_read = [sem("bank_read0"), sem("bank_read1")]
        q_mixed = sem("q_mixed")
        k_mixed = sem("k_mixed")
        v_copied = sem("v_copied")
        v_doubled = sem("v_doubled")
        q_ready = sem("q_ready")
        k_ready = sem("k_ready")
        scores_done = sem("scores_done")
        top_done = sem("top_done")
        shifted = sem("shifted")
        exp_done = sem("exp_done")
        total_done = sem("total_done")
        inv_done = sem("inv_done")
        prob_ready = sem("prob_ready")
        prob_turned = sem("prob_turned")
        probT_ready = sem("probT_ready")
        av_done = sem("av_done")
        o_hi_done = sem("o_hi_done")
        o_lo_done = sem("o_lo_done")
        out_done = sem("out_done")
        n_small = 7 if mixed else 4
        PAIRS = NT // 2

        def softmax_rows(ap):
            return ap.unsqueeze(2).broadcast_to([P, 8, SB])

        def loop(engine, body):
            body(0)
            with engine.Fori(1, PAIRS - 1) as i:
                body(i)
            body(PAIRS - 1)

        def is_last(i, e):
            return isinstance(i, int) and i == PAIRS - 1 and e == 1

        with nc.Block() as block:

            @block.sync
            def _(sp):
                sp.dma_start(W_raw[:].rearrange("p k n -> p (k n)"), d["w"][0]).then_inc(w_loaded, 16)
                sp.dma_start(QT[:].rearrange("p k n -> p (k n)"), d["ctxT"]).then_inc(ctx_loaded, 16)
                sp.dma_start(biases[:], d["biases"]).then_inc(small_loaded, 16)
                sp.dma_start(kmask[:], d["kmask"]).then_inc(small_loaded, 16)
                sp.dma_start(vmask[:], d["vmask"]).then_inc(small_loaded, 16)
                sp.dma_start(bo[:], d["bo"].broadcast_to([P, DM])).then_inc(small_loaded, 16)
                if mixed:
                    sp.dma_start(inter[:], d["inter"]).then_inc(small_loaded, 16)
                    sp.dma_start(amp[:], d["amp"].broadcast_to([P, 1])).then_inc(small_loaded, 16)
                    sp.dma_start(same[:], d["same"]).then_inc(small_loaded, 16)
                for T in range(NT if x_dram is not None else 0):
                    sp.dma_start(S.x[:, T], x_dram[T]).then_inc(x_loaded, 16)
                for m in range(1, 4):
                    sp.wait_ge(w_hi_done, KC * m)
                    sp.wait_ge(w_lo_done, KC * m)
                    sp.dma_start(W_raw[:].rearrange("p k n -> p (k n)"), d["w"][m]).then_inc(w_loaded, 16)

            @block.tensor
            def _(pe):
                for m in range(3):
                    hi, lo = (S.xT_hi, S.xT_lo) if m == 2 else (ctx_hi, ctx_lo)
                    for c in range(KC):
                        pe.wait_ge(w_hi_done, KC * m + c + 1)
                        pe.wait_ge(w_lo_done, KC * m + c + 1)
                        for hf in range(2):
                            if m == 0 and c == 0:
                                pe.wait_ge(ctx_lo_done, 2 * KC if hf else KC)
                            wait(pe, bank_read[hf], KC * m + c)
                            tok = slice(hf * HALF, (hf + 1) * HALF)
                            for k in range(KC):
                                wk = slice(k * P, (k + 1) * P)
                                mm = three_pass(pe, pM[:, hf, :], W_hi[:, c, wk], W_lo[:, c, wk],
                                                hi[:, k, tok], lo[:, k, tok], k == 0, k == KC - 1)
                            mm.then_inc(proj_done, 1)

                def mix_rows(j, src, bank, nth, semaphore):
                    pe.wait_ge(bank_read[bank], 3 * KC + fills * j + nth)
                    for c in range(KC):
                        mm = pe.matmul(pM[:, bank, c * P:(c + 1) * P], mix[:, c, :],
                                       src[:, c, bass.ds(j * P, P)], start=True, stop=True,
                                       skip_group_check=True)
                    mm.then_inc(semaphore, 1)

                def double_v(j, b):
                    pe.wait_ge(bank_read[b], 3 * KC + fills * j + fills - 1)
                    pe.wait_ge(v_copied, j + 1)
                    for c in range(KC):
                        v = Vtile[:, c, b * SB:(b + 1) * SB]
                        w = mix[:, c, :] if mixed else S.ident[:]
                        for half in range(2):
                            mm = pe.matmul(pM[half * SB:(half + 1) * SB, b, c * P:(c + 1) * P], v, w,
                                           start=True, stop=True, skip_group_check=True)
                    mm.then_inc(v_doubled, 1)

                def rows(w, i):
                    r0 = w // 2 * rows_per_unit
                    return slice(r0, r0 + rows_per_unit), 2 * (w % 2) + i

                def wait_qk(j):
                    if mixed:
                        pe.wait_ge(bank_read[0], 3 * KC + fills * j + 1)
                        pe.wait_ge(bank_read[1], 3 * KC + fills * j + 1)
                    else:
                        pe.wait_ge(q_ready, j + 1)
                        pe.wait_ge(k_ready, j + 1)

                def scores(j, e, w):
                    for i in range(2):
                        r, c = rows(w, i)
                        for b in range(2):
                            mm = pe.matmul(pS[b * SB:(b + 1) * SB, w % 2, i * 4 * SB:(i + 1) * 4 * SB],
                                           Qtile[r, e, c, b * SB:(b + 1) * SB],
                                           Kmask[r, e, c, :, b * SB:(b + 1) * SB],
                                           start=True, stop=True, skip_group_check=True)
                    mm.then_inc(scores_done, 1)

                def turn_probs(j, w):
                    n = W * j + w
                    pe.wait_ge(prob_ready, n + 1)
                    wait(pe, probT_ready, n)
                    for i in range(4):
                        mm = pe.transpose(pP[:, i, :], prob[:, w % 4, 2 * i:2 * i + 2, :], S.ident[:])
                    mm.then_inc(prob_turned, 1)

                def attend(j, e, w):
                    n = W * j + w
                    pe.wait_ge(probT_ready, n + 1)
                    if w == 0:
                        for b in range(2):
                            pe.wait_ge(bank_read[b], 3 * KC + fills * (j + 1))
                        wait(pe, o_lo_done, j - 1)
                    for i in range(2):
                        r, c = rows(w, i)
                        cols = slice(c * P + r.start, c * P + r.stop)
                        for b in range(2):
                            for pair in range(2):
                                mm = pe.matmul(pO[r, e, c, b * SB:(b + 1) * SB], Vmask[:, e, b, pair, cols],
                                               probT[:, w % 2, 2 * i + pair, b * SB:(b + 1) * SB],
                                               start=pair == 0, stop=pair == 1, skip_group_check=True,
                                               tile_position=(0, r.start))
                    mm.then_inc(av_done, 1)

                if mixed:
                    pe.wait_ge(mix_step, 1 + 2 * KC)

                def prepare(j, step):
                    if mixed:
                        if step == 0:
                            mix_rows(j, QT, 0, 0, q_mixed)
                        if step == 1:
                            mix_rows(j, KT, 1, 0, k_mixed)
                        if step in (2, 3):
                            double_v(j, step - 2)
                    elif step in (0, 1):
                        double_v(j, step)

                for step in range(4):
                    prepare(0, step)
                wait_qk(0)
                scores(0, 0, 0)
                scores(0, 0, 1)

                def body(i):
                    for e in range(2):
                        j = 2 * i + e
                        last = is_last(i, e)
                        for w in range(W):
                            if w + 2 == W and not last:
                                wait_qk(j + 1)
                            turn_probs(j, w)
                            if w + 2 < W:
                                scores(j, e, w + 2)
                            elif not last:
                                scores(j + 1, 1 - e, w + 2 - W)
                            if not last:
                                prepare(j + 1, w)
                            if w > 0:
                                attend(j, e, w - 1)
                        attend(j, e, W - 1)

                loop(pe, body)
                for T in range(NT):
                    if T == 0:
                        pe.wait_ge(w_hi_done, 4 * KC)
                        pe.wait_ge(w_lo_done, 4 * KC)
                        pe.wait_ge(o_lo_done, NT)
                    pe.wait_ge(bank_read[T % 2], 3 * KC + fills * NT + T // 2)
                    cols = slice(T * P, (T + 1) * P)
                    for c in range(KC):
                        mm = three_pass(pe, pM[:, T % 2, :], S.xT_hi[:, c, cols], S.xT_lo[:, c, cols],
                                        W_hi[:, c, :], W_lo[:, c, :], c == 0, c == KC - 1)
                    mm.then_inc(out_done, 1)

            @block.scalar
            def _(act):
                def split_w(m, c):
                    if c == 0:
                        act.wait_ge(w_loaded, 16 * (m + 1))
                    wait(act, proj_done, 2 * (KC * (m - 1) + c + 1))
                    nc.scalar.copy(W_hi[:, c], W_raw[:, c]).then_inc(w_hi_done, 1)

                act.wait_ge(ctx_loaded, 16)
                for hf in range(2):
                    for k in range(KC):
                        tok = slice(hf * HALF, (hf + 1) * HALF)
                        nc.scalar.copy(ctx_hi[:, k, tok], QT[:, k, tok]).then_inc(ctx_hi_done, 1)
                        if hf == 0:
                            split_w(0, k)
                act.wait_ge(small_loaded, 16 * n_small)
                for m in range(3):
                    dst = (KT, VT, QT)[m]
                    if m == 2:
                        act.wait_ge(ctx_lo_done, 2 * KC)
                    for c in range(KC):
                        for hf in range(2):
                            act.wait_ge(proj_done, 2 * (KC * m + c) + hf + 1)
                            nc.scalar.activation(dst[:, c, hf * HALF:(hf + 1) * HALF], pM[:, hf, :], ACT.Identity,
                                                 bias=biases[:, m, c:c + 1]).then_inc(bank_read[hf], 1)
                        split_w(m + 1, c)

                def read_probT(j, w):
                    n = W * j + w
                    act.wait_ge(prob_turned, n + 1)
                    wait(act, av_done, n - 1)
                    nc.scalar.copy(probT[:, w % 2], pP[:, :, :]).then_inc(probT_ready, 1)

                def exponent(j, w):
                    n = W * j + w
                    act.wait_ge(shifted, n + 1)
                    nc.scalar.activation(prob[:, w % 4], prob[:, w % 4], ACT.Exp, scale=scale).then_inc(exp_done, 1)

                def prepare(j, e, step):
                    if not mixed:
                        return
                    if step == 0:
                        act.wait_ge(q_mixed, j + 1)
                        wait(act, scores_done, W * (j - 1))
                        nc.scalar.copy(Qtile[:, e], pM[:, 0, :].rearrange("p (c n) -> p c n", c=KC)).then_inc(bank_read[0], 1)
                    if step == 1:
                        act.wait_ge(k_mixed, j + 1)
                        wait(act, scores_done, W * (j - 1))
                        for m in range(4):
                            ins = nc.scalar.activation(Kmask[:, e, :, m, :], pM[:, 1, :].rearrange("p (c n) -> p c n", c=KC),
                                                       ACT.Copy, scale=kmask[:, m:m + 1])
                        ins.then_inc(bank_read[1], 1)

                for step in range(2):
                    prepare(0, 0, step)
                exponent(0, 0)
                exponent(0, 1)

                def body(i):
                    for e in range(2):
                        j = 2 * i + e
                        last = is_last(i, e)
                        for w in range(W):
                            read_probT(j, w)
                            if w + 2 < W:
                                exponent(j, w + 2)
                            elif not last:
                                exponent(j + 1, w + 2 - W)
                            if not last:
                                prepare(j + 1, 1 - e, w)

                loop(act, body)

            @block.vector
            def _(dve):
                for hf in range(2):
                    for k in range(KC):
                        tok = slice(hf * HALF, (hf + 1) * HALF)
                        dve.wait_ge(ctx_hi_done, KC * hf + k + 1)
                        nc.vector.tensor_tensor(ctx_lo[:, k, tok], QT[:, k, tok], ctx_hi[:, k, tok].bitcast(F32),
                                                ALU.subtract).then_inc(ctx_lo_done, 1)
                dve.wait_ge(small_loaded, 16 * n_small)
                if mixed:
                    nc.vector.tensor_scalar(inter[:], inter[:], amp[:, 0:1], 0.1, ALU.mult, ALU.mult).then_inc(mix_step, 1)
                    dve.wait_ge(mix_step, 1)
                    for c in range(KC):
                        nc.vector.tensor_tensor(mix[:, c, :].rearrange("p (h j) -> p h j", j=4),
                                                same[:].unsqueeze(2).broadcast_to([P, 32, 4]),
                                                inter[:, c].unsqueeze(1).broadcast_to([P, 32, 4]),
                                                ALU.mult).then_inc(mix_step, 1)
                        dve.wait_ge(mix_step, 2 + 2 * c)
                        nc.vector.tensor_tensor(mix[:, c, :], mix[:, c, :], S.ident[:], ALU.add).then_inc(mix_step, 1)

                def copy_v(j):
                    if isinstance(j, int) and j == 0:
                        dve.wait_ge(bank_read[0], 2 * KC)
                        dve.wait_ge(bank_read[1], 2 * KC)
                    wait(dve, v_doubled, 2 * j)
                    nc.vector.tensor_scalar(Vtile[:], VT[:, :, bass.ds(j * P, P)], 1.0, None, ALU.mult).then_inc(v_copied, 1)

                def copy_qk(j, e):
                    if mixed:
                        return
                    if isinstance(j, int) and j == 0:
                        dve.wait_ge(bank_read[0], 3 * KC)
                        dve.wait_ge(bank_read[1], 3 * KC)
                    wait(dve, scores_done, W * (j - 1))
                    nc.vector.tensor_scalar(Qtile[:, e], QT[:, :, bass.ds(j * P, P)], 1.0, None, ALU.mult).then_inc(q_ready, 1)
                    for m in range(4):
                        ins = nc.vector.tensor_scalar(Kmask[:, e, :, m, :], KT[:, :, bass.ds(j * P, P)], kmask[:, m:m + 1],
                                                      None, ALU.mult)
                    ins.then_inc(k_ready, 1)

                def mask_v(j, e, b):
                    dve.wait_ge(v_doubled, 2 * j + b + 1)
                    wait(dve, av_done, W * (j - 1))
                    for pair in range(2):
                        ins = nc.vector.tensor_tensor(Vmask[:, e, b, pair, :], pM[:, b, :], vmask[:, pair, :], ALU.mult)
                    ins.then_inc(bank_read[b], 1)

                def soften(j, w):
                    n = W * j + w
                    dve.wait_ge(scores_done, n + 1)
                    bank = pS[:, w % 2, :].rearrange("p (u k) -> p u k", u=8)
                    nc.vector.tensor_reduce(top[:, w % 4], bank, AX.X, ALU.max).then_inc(top_done, 1)
                    dve.wait_ge(top_done, n + 1)
                    wait(dve, prob_turned, n - 3)
                    nc.vector.tensor_tensor(prob[:, w % 4], bank, softmax_rows(top[:, w % 4]),
                                            ALU.subtract).then_inc(shifted, 1)

                def row_totals(j, w):
                    n = W * j + w
                    dve.wait_ge(exp_done, n + 1)
                    nc.vector.tensor_reduce(total[:, w % 4], prob[:, w % 4], AX.X, ALU.add).then_inc(total_done, 1)
                    dve.wait_ge(total_done, n + 1)
                    wait(dve, prob_ready, n - 3)
                    nc.vector.reciprocal(inv[:, w % 4], total[:, w % 4]).then_inc(inv_done, 1)

                def read_o(j, e):
                    dve.wait_ge(av_done, W * (j + 1))
                    nc.vector.tensor_scalar(S.xT_hi[:, :, bass.ds(j * P, P)], pO[:, e], 1.0, None, ALU.mult).then_inc(o_hi_done, 1)
                    dve.wait_ge(o_hi_done, j + 1)
                    nc.vector.tensor_tensor(S.xT_lo[:, :, bass.ds(j * P, P)], pO[:, e],
                                            S.xT_hi[:, :, bass.ds(j * P, P)].bitcast(F32), ALU.subtract).then_inc(o_lo_done, 1)

                copy_v(0)
                copy_qk(0, 0)
                for b in range(2):
                    mask_v(0, 0, b)
                for w in range(2):
                    soften(0, w)
                    row_totals(0, w)
                dve.wait_ge(proj_done, 6 * KC)

                def body(i):
                    for e in range(2):
                        j = 2 * i + e
                        last = is_last(i, e)
                        for w in range(W):
                            nj, nw = (j, w + 2) if w + 2 < W else (j + 1, w + 2 - W)
                            todo = w + 2 < W or not last
                            if w == 0 and not last:
                                copy_v(j + 1)
                                copy_qk(j + 1, 1 - e)
                            if todo:
                                soften(nj, nw)
                            if not last and mixed and w in (2, 3):
                                mask_v(j + 1, 1 - e, w - 2)
                            if not last and not mixed and w in (0, 1):
                                if w == 1:
                                    mask_v(j + 1, 1 - e, 0)
                            if not last and not mixed and w == 2:
                                mask_v(j + 1, 1 - e, 1)
                            if todo:
                                row_totals(nj, nw)
                        read_o(j, e)

                loop(dve, body)
                for T in range(NT):
                    dve.wait_ge(out_done, T + 1)
                    dve.wait_ge(x_biased, T + 1)
                    nc.vector.tensor_tensor(S.x[:, T], pM[:, T % 2, :], S.x[:, T], ALU.add).then_inc(bank_read[T % 2], 1)

            @block.gpsimd
            def _(pool):
                def split_w(m, c):
                    pool.wait_ge(w_hi_done, KC * m + c + 1)
                    wait(pool, proj_done, 2 * (KC * (m - 1) + c + 1))
                    nc.gpsimd.tensor_tensor(W_lo[:, c], W_raw[:, c], W_hi[:, c].bitcast(F32),
                                            ALU.subtract).then_inc(w_lo_done, 1)

                for c in range(KC):
                    split_w(0, c)
                pool.wait_ge(small_loaded, 16 * n_small)
                if x_dram is not None:
                    pool.wait_ge(x_loaded, 16 * NT)
                for T in range(NT):
                    nc.gpsimd.tensor_tensor(S.x[:, T], S.x[:, T], bo[:], ALU.add).then_inc(x_biased, 1)
                for m in range(1, 4):
                    for c in range(KC):
                        split_w(m, c)

                def divide(j, w):
                    n = W * j + w
                    pool.wait_ge(inv_done, n + 1)
                    nc.gpsimd.tensor_tensor(prob[:, w % 4], prob[:, w % 4], softmax_rows(inv[:, w % 4]),
                                            ALU.mult).then_inc(prob_ready, 1)

                divide(0, 0)
                divide(0, 1)

                def body(i):
                    for e in range(2):
                        j = 2 * i + e
                        last = is_last(i, e)
                        for w in range(W):
                            if w + 2 < W:
                                divide(j, w + 2)
                            elif not last:
                                divide(j + 1, w + 2 - W)

                loop(pool, body)
        ph.close()


def lora_phase(nc, name, S, d):
    E, R = 8, 16
    with ExitStack() as ctx:
        ph = Phase(nc, ctx, name)
        sb, ps, sem = ph.sb, ph.ps, ph.sem
        raw = sb("raw", [P, 7, DM])
        w_hi = sb("w_hi", [P, 7, DM], F32R)
        w_lo = sb("w_lo", [P, 7, DM], F32R)
        A, ROUTER, B, BASE = 0, 1, 2, 3
        base_bias = sb("base_bias", [P, DM])
        router_bias = sb("router_bias", [P, 1])
        inv_k = sb("inv_k", [P, E])
        hT = sb("hT", [P, TOK])
        gT = sb("gT", [P, TOK])
        z = sb("z", [P, NT, E])
        top = sb("top", [P, NT, E])
        run = sb("run", [P, NT, E])
        tau = sb("tau", [P, NT])
        weight = sb("weight", [P, NT, E, R])
        hw = sb("hw", [P, TOK])
        hw_hi = sb("hw_hi", [P, TOK], F32R)
        hw_lo = sb("hw_lo", [P, TOK], F32R)
        pA = ps("pA", [P, 2, HALF])
        pL = ps("pL", [P, NT, P])
        pB = ps("pB", [P, 4, DM])
        names = ("small_loaded", "w_hi_done", "w_lo_done", "x_biased", "proj_done", "h_read", "logits_turned",
                 "z_done", "sorted_done", "step", "weight_turned", "hw_done", "hw_hi_done", "hw_lo_done", "out_done", "summed")
        (small_loaded, w_hi_done, w_lo_done, x_biased, proj_done, h_read, logits_turned,
         z_done, sorted_done, step, weight_turned, hw_done, hw_hi_done, hw_lo_done, out_done, summed) = map(sem, names)
        w_loaded = [sem(f"w_loaded{i}") for i in range(2)]

        with nc.Block() as block:

            @block.sync
            def _(sp):
                sp.dma_start(raw[:, 0:BASE].rearrange("p k n -> p (k n)"), d["small_w"]).then_inc(w_loaded[0], 16)
                sp.dma_start(raw[:, BASE:7].rearrange("p k n -> p (k n)"), d["base_w"]).then_inc(w_loaded[1], 16)
                sp.dma_start(base_bias[:], d["base_bias"].broadcast_to([P, DM])).then_inc(small_loaded, 16)
                sp.dma_start(router_bias[:], d["router_bias"]).then_inc(small_loaded, 16)
                sp.dma_start(inv_k[:], d["inv_k"].broadcast_to([P, E])).then_inc(small_loaded, 16)

            @block.tensor
            def _(pe):
                for i, w in enumerate((ROUTER, A)):
                    for hf in range(2):
                        pe.wait_ge(w_lo_done, 2)
                        if i == 1:
                            pe.wait_ge(h_read, hf + 1)
                        tok = slice(hf * HALF, (hf + 1) * HALF)
                        for k in range(KC):
                            wk = slice(k * P, (k + 1) * P)
                            mm = three_pass(pe, pA[:, hf, :], w_hi[:, w, wk], w_lo[:, w, wk],
                                            S.xT_hi[:, k, tok], S.xT_lo[:, k, tok], k == 0, k == KC - 1)
                        mm.then_inc(proj_done, 1)
                pe.wait_ge(h_read, 2)
                for T in range(NT):
                    mm = pe.transpose(pL[:, T, :], gT[:, T * P:(T + 1) * P], S.ident[:])
                mm.then_inc(logits_turned, 1)

                def base(T):
                    wait(pe, summed, T - 3)
                    cols = slice(T * P, (T + 1) * P)
                    for k in range(KC):
                        pe.wait_ge(w_lo_done, BASE + k + 1)
                        three_pass(pe, pB[:, T % 4, :], S.xT_hi[:, k, cols], S.xT_lo[:, k, cols],
                                   w_hi[:, BASE + k, :], w_lo[:, BASE + k, :], k == 0, False)

                def lora(T):
                    if T % 4 == 0:
                        pe.wait_ge(hw_lo_done, T // 4 + 1)
                    cols = slice(T * P, (T + 1) * P)
                    three_pass(pe, pB[:, T % 4, :], hw_hi[:, cols], hw_lo[:, cols], w_hi[:, B, :], w_lo[:, B, :],
                               False, True).then_inc(out_done, 1)

                for T in range(4):
                    base(T)
                pe.wait_ge(step, E + 4)
                for T in range(NT):
                    mm = pe.transpose(pL[:, T, :], weight[:, T].rearrange("p e r -> p (e r)"), S.ident[:])
                mm.then_inc(weight_turned, 1)
                for T in range(4):
                    lora(T)
                for T in range(4, NT):
                    base(T)
                    lora(T)

            @block.scalar
            def _(act):
                for n, i in enumerate((ROUTER, A, B, BASE, BASE + 1, BASE + 2, BASE + 3)):
                    act.wait_ge(w_loaded[i >= BASE], 16)
                    nc.scalar.copy(w_hi[:, i], raw[:, i]).then_inc(w_hi_done, 1)
                act.wait_ge(small_loaded, 48)
                for hf in range(2):
                    act.wait_ge(proj_done, hf + 1)
                    nc.scalar.activation(gT[:, hf * HALF:(hf + 1) * HALF], pA[:, hf, :], ACT.Identity,
                                         bias=router_bias[:, 0:1]).then_inc(h_read, 1)
                for hf in range(2):
                    act.wait_ge(proj_done, 3 + hf)
                    nc.scalar.copy(hT[:, hf * HALF:(hf + 1) * HALF], pA[:, hf, :]).then_inc(h_read, 1)
                for hf in range(2):
                    act.wait_ge(hw_done, hf + 1)
                    nc.scalar.copy(hw_hi[:, hf * HALF:(hf + 1) * HALF], hw[:, hf * HALF:(hf + 1) * HALF]).then_inc(hw_hi_done, 1)

            @block.vector
            def _(dve):
                dve.wait_ge(small_loaded, 48)
                dve.wait_ge(logits_turned, 1)
                nc.vector.tensor_copy(z[:], pL[:, :, :].rearrange("p t (e r) -> p t e r", r=R)[:, :, :, 0]).then_inc(z_done, 1)
                dve.wait_ge(z_done, 1)
                for T in range(NT):
                    nc.vector.max(top[:, T], z[:, T]).then_inc(sorted_done, 1)
                dve.wait_ge(sorted_done, NT)

                def link(n, instruction):
                    instruction.then_inc(step, 1)
                    dve.wait_ge(step, n)

                link(1, nc.vector.tensor_scalar(run[:, :, 0:1], top[:, :, 0:1], -1.0, None, ALU.add))
                for k in range(1, E):
                    link(k + 1, nc.vector.tensor_tensor(run[:, :, k:k + 1], run[:, :, k - 1:k], top[:, :, k:k + 1], ALU.add))
                link(E + 1, nc.vector.tensor_tensor(run[:], run[:], inv_k[:].unsqueeze(1).broadcast_to([P, NT, E]), ALU.mult))
                link(E + 2, nc.vector.tensor_reduce(tau[:], run[:], AX.X, ALU.max))
                link(E + 3, nc.vector.tensor_tensor(z[:], z[:], tau[:].unsqueeze(2).broadcast_to([P, NT, E]), ALU.subtract))
                link(E + 4, nc.vector.tensor_scalar(weight[:], z[:].unsqueeze(3).broadcast_to([P, NT, E, R]), 0.0, None, ALU.max))
                dve.wait_ge(h_read, 4)
                dve.wait_ge(weight_turned, 1)
                for hf in range(2):
                    tok = slice(hf * HALF, (hf + 1) * HALF)
                    nc.vector.tensor_tensor(hw[:, tok], hT[:, tok], pL[:, 4 * hf:4 * hf + 4, :].rearrange("p t n -> p (t n)"),
                                            ALU.mult).then_inc(hw_done, 1)
                for hf in range(2):
                    tok = slice(hf * HALF, (hf + 1) * HALF)
                    dve.wait_ge(hw_hi_done, hf + 1)
                    nc.vector.tensor_tensor(hw_lo[:, tok], hw[:, tok], hw_hi[:, tok].bitcast(F32),
                                            ALU.subtract).then_inc(hw_lo_done, 1)
                for T in range(NT):
                    dve.wait_ge(out_done, T + 1)
                    dve.wait_ge(x_biased, T + 1)
                    nc.vector.tensor_tensor(S.x[:, T], pB[:, T % 4, :], S.x[:, T], ALU.add).then_inc(summed, 1)

            @block.gpsimd
            def _(pool):
                for n, i in enumerate((ROUTER, A, B, BASE, BASE + 1, BASE + 2, BASE + 3)):
                    pool.wait_ge(w_hi_done, n + 1)
                    nc.gpsimd.tensor_tensor(w_lo[:, i], raw[:, i], w_hi[:, i].bitcast(F32), ALU.subtract).then_inc(w_lo_done, 1)
                pool.wait_ge(small_loaded, 48)
                for T in range(NT):
                    nc.gpsimd.tensor_tensor(S.x[:, T], S.x[:, T], base_bias[:], ALU.add).then_inc(x_biased, 1)
        ph.close()


def experts_phase(nc, name, S, d):
    E, G, X = 16, 4, 18
    with ExitStack() as ctx:
        ph = Phase(nc, ctx, name)
        sb, ps, sem = ph.sb, ph.ps, ph.sem
        raw = sb("raw", [P, 2, 3 * DM + 2])
        w12_hi = sb("w12_hi", [P, 2, 2 * DM], F32R)
        w12_lo = sb("w12_lo", [P, 2, 2 * DM], F32R)
        w3_hi = sb("w3_hi", [P, 2, DM], F32R)
        w3_lo = sb("w3_lo", [P, 2, DM], F32R)
        r_raw = sb("r_raw", [P, DM])
        r_hi = sb("r_hi", [P, DM], F32R)
        r_lo = sb("r_lo", [P, DM], F32R)
        r_bias = sb("r_bias", [P, 1])
        s_bias = sb("s_bias", [P, E])
        before = sb("before", [P, E, E])
        b3 = sb("b3", [X, DM])
        gT = sb("gT", [P, TOK])
        score = sb("score", [P, NT, E])
        masked = sb("masked", [P, NT, E])
        stat = sb("stat", [P, NT])
        gmax = sb("gmax", [P, NT, G])
        keep = sb("keep", [P, NT, G])
        cmp = sb("cmp", [P, NT, E, E])
        same = sb("same", [P, NT, E, E])
        rank = sb("rank", [P, NT, E])
        gate = sb("gate", [P, NT, X])
        gateT = sb("gateT", [X, TOK])
        act_out = sb("act_out", [P, 2, HALF])
        hid = sb("hid", [P, 2, HALF])
        hid_hi = sb("hid_hi", [P, 2, 2, HALF], F32R)
        hid_lo = sb("hid_lo", [P, 2, 2, HALF], F32R)
        pH = ps("pH", [P, 2, 2, HALF])
        pY = ps("pY", [P, 4, DM])
        names = ("small_loaded", "r_hi_done", "r_lo_done", "r_done", "r_read", "r_turned", "step", "exp_done", "gate_set",
                 "gate_turned", "gateT_read", "b3_done", "w12_hi_done", "w12_lo_done", "w3_hi_done", "w3_lo_done",
                 "hid_done", "silu_done", "hid_ready", "hid_hi_done", "hid_lo_done", "y_done", "summed")
        (small_loaded, r_hi_done, r_lo_done, r_done, r_read, r_turned, step, exp_done, gate_set,
         gate_turned, gateT_read, b3_done, w12_hi_done, w12_lo_done, w3_hi_done, w3_lo_done,
         hid_done, silu_done, hid_ready, hid_hi_done, hid_lo_done, y_done, summed) = map(sem, names)
        w_loaded = [sem(f"w_loaded{i}") for i in range(2)]
        STEPS = 18

        def bcast(ap, dim, n):
            shape = list(ap.shape)
            shape.insert(dim, n)
            return ap.unsqueeze(dim).broadcast_to(shape)

        def loop(engine, body):
            body(0)
            with engine.Fori(1, X // 2 - 1) as i:
                body(i)
            body(X // 2 - 1)

        def exists(i, e2, ahead):
            return not (isinstance(i, int) and 2 * i + e2 + ahead >= X)

        with nc.Block() as block:

            @block.sync
            def _(sp):
                for dst, src in ((r_raw, d["r_w"]), (r_bias, d["r_bias"]), (s_bias, d["s_bias"].broadcast_to([P, E])),
                                 (before, d["before"].broadcast_to([P, E * E])), (b3, d["b3"])):
                    to = dst[:].rearrange("p i j -> p (i j)") if dst is before else dst[:]
                    sp.dma_start(to, src).then_inc(small_loaded, 16)
                for e in range(2):
                    sp.dma_start(raw[:, e], d["w"][e]).then_inc(w_loaded[e], 16)

                def body(i):
                    for e2 in range(2):
                        e = 2 * i + e2
                        sp.wait_ge(hid_ready, 2 * (e - 1))
                        sp.wait_ge(w3_hi_done, e - 1)
                        sp.wait_ge(w3_lo_done, e - 1)
                        sp.dma_start(raw[:, e2], d["w"][e]).then_inc(w_loaded[e2], 16)

                with sp.Fori(1, X // 2) as i:
                    body(i)

            @block.tensor
            def _(pe):
                pe.wait_ge(r_hi_done, 1)
                pe.wait_ge(r_lo_done, 1)
                for hf in range(2):
                    tok = slice(hf * HALF, (hf + 1) * HALF)
                    for k in range(KC):
                        wk = slice(k * P, (k + 1) * P)
                        mm = three_pass(pe, pY[:, hf, :], r_hi[:, wk], r_lo[:, wk],
                                        S.xT_hi[:, k, tok], S.xT_lo[:, k, tok], k == 0, k == KC - 1)
                    mm.then_inc(r_done, 1)
                pe.wait_ge(r_read, 2)
                for T in range(NT):
                    mm = pe.transpose(pY[:, 2 + T // 4, (T % 4) * P:(T % 4 + 1) * P], gT[:, T * P:(T + 1) * P], S.ident[:])
                mm.then_inc(r_turned, 1)

                def hidden(e, slot, hf):
                    if hf == 0:
                        pe.wait_ge(w12_hi_done, e + 1)
                        pe.wait_ge(w12_lo_done, e + 1)
                    wait(pe, silu_done, 2 * e - 1 + hf)
                    wait(pe, hid_ready, 2 * e - 1 + hf)
                    tok = slice(hf * HALF, (hf + 1) * HALF)
                    for m in range(2):
                        for k in range(KC):
                            wk = slice(m * DM + k * P, m * DM + (k + 1) * P)
                            mm = three_pass(pe, pH[:, m, hf, :], w12_hi[:, slot, wk], w12_lo[:, slot, wk],
                                            S.xT_hi[:, k, tok], S.xT_lo[:, k, tok], k == 0, k == KC - 1)
                    mm.then_inc(hid_done, 1)

                def output(e, slot, hf):
                    pe.wait_ge(hid_lo_done, 2 * e + hf + 1)
                    if hf == 0:
                        pe.wait_ge(w3_hi_done, e + 1)
                        pe.wait_ge(w3_lo_done, e + 1)
                    for t in range(4):
                        wait(pe, summed, 8 * (e + 1) + 4 * hf + t - 3)
                        cols = slice(t * P, (t + 1) * P)
                        three_pass(pe, pY[:, t, :], hid_hi[:, slot, hf, cols], hid_lo[:, slot, hf, cols],
                                   w3_hi[:, slot, :], w3_lo[:, slot, :], True, True).then_inc(y_done, 1)

                for hf in range(2):
                    hidden(0, 0, hf)
                pe.wait_ge(step, STEPS)
                for T in range(NT):
                    bank = pY[0:X, T // 4, (T % 4) * P:(T % 4 + 1) * P]
                    mm = pe.transpose(bank, gate[:, T, :], S.ident[:])
                mm.then_inc(gate_turned, 1)
                pe.wait_ge(gateT_read, 1)
                for T in range(NT):
                    wait(pe, summed, T - 3)
                    pe.matmul(pY[:, T % 4, :], gateT[:, T * P:(T + 1) * P], b3[:, :],
                              start=True, stop=True, skip_group_check=True).then_inc(b3_done, 1)

                def body(i):
                    for e2 in range(2):
                        e = 2 * i + e2
                        for hf in range(2):
                            if exists(i, e2, 1):
                                hidden(e + 1, 1 - e2, hf)
                            output(e, e2, hf)

                loop(pe, body)

            @block.scalar
            def _(act):
                act.wait_ge(small_loaded, 80)
                nc.scalar.copy(r_hi[:], r_raw[:]).then_inc(r_hi_done, 1)

                def split(e, slot, i, n12):
                    act.wait_ge(w_loaded[slot], 16 * (i + 1))
                    if n12:
                        wait(act, hid_done, 2 * (e - 1))
                        nc.scalar.copy(w12_hi[:, slot], raw[:, slot, 0:2 * DM]).then_inc(w12_hi_done, 1)
                    else:
                        wait(act, y_done, 8 * (e - 1))
                        nc.scalar.copy(w3_hi[:, slot], raw[:, slot, 2 * DM:3 * DM]).then_inc(w3_hi_done, 1)

                def silu(e, slot, hf):
                    act.wait_ge(hid_done, 2 * e + hf + 1)
                    wait(act, hid_ready, 2 * e - 1 + hf)
                    nc.scalar.activation(act_out[:, hf], pH[:, 0, hf, :], ACT.Silu,
                                         bias=raw[:, slot, 3 * DM:3 * DM + 1]).then_inc(silu_done, 1)

                def high(e, slot, hf):
                    act.wait_ge(hid_ready, 2 * e + hf + 1)
                    wait(act, y_done, 8 * (e - 1))
                    nc.scalar.copy(hid_hi[:, slot, hf], hid[:, hf]).then_inc(hid_hi_done, 1)

                split(0, 0, 0, True)
                for hf in range(2):
                    act.wait_ge(r_done, hf + 1)
                    nc.scalar.activation(gT[:, hf * HALF:(hf + 1) * HALF], pY[:, hf, :], ACT.Identity,
                                         bias=r_bias[:, 0:1]).then_inc(r_read, 1)
                split(1, 1, 0, True)
                split(0, 0, 0, False)
                act.wait_ge(step, 2)
                nc.scalar.activation(score[:], score[:], ACT.Exp).then_inc(exp_done, 1)
                for hf in range(2):
                    silu(0, 0, hf)
                    high(0, 0, hf)
                act.wait_ge(gate_turned, 1)
                nc.scalar.copy(gateT[:], pY[0:X, 0:2, :].rearrange("p t n -> p (t n)")).then_inc(gateT_read, 1)

                def body(i):
                    for e2 in range(2):
                        e = 2 * i + e2
                        if exists(i, e2, 1):
                            split(e + 1, 1 - e2, i + e2, False)
                            silu(e + 1, 1 - e2, 0)
                            high(e + 1, 1 - e2, 0)
                        if exists(i, e2, 2):
                            split(e + 2, e2, i + 1, True)
                        if exists(i, e2, 1):
                            silu(e + 1, 1 - e2, 1)
                            high(e + 1, 1 - e2, 1)

                loop(act, body)

            @block.vector
            def _(dve):
                dve.wait_ge(small_loaded, 80)

                def link(n, instruction):
                    instruction.then_inc(step, 1)
                    dve.wait_ge(step, n)

                def hidden_product(e, slot, hf):
                    dve.wait_ge(silu_done, 2 * e + hf + 1)
                    wait(dve, hid_lo_done, 2 * e - 1 + hf)
                    nc.vector.scalar_tensor_tensor(out=hid[:, hf], in0=pH[:, 1, hf, :], scalar=raw[:, slot, 3 * DM + 1:3 * DM + 2],
                                                   in1=act_out[:, hf], op0=ALU.add, op1=ALU.mult).then_inc(hid_ready, 1)

                def low(e, slot, hf):
                    dve.wait_ge(hid_hi_done, 2 * e + hf + 1)
                    nc.vector.tensor_tensor(hid_lo[:, slot, hf], hid[:, hf], hid_hi[:, slot, hf].bitcast(F32),
                                            ALU.subtract).then_inc(hid_lo_done, 1)

                def add_output(e, hf):
                    for t in range(4):
                        T = 4 * hf + t
                        dve.wait_ge(y_done, 8 * e + T + 1)
                        dve.wait_ge(summed, 8 * e + T + 1)
                        nc.vector.scalar_tensor_tensor(out=S.x[:, T], in0=pY[:, t, :], scalar=gate[:, T, bass.ds(e, 1)],
                                                       in1=S.x[:, T], op0=ALU.mult, op1=ALU.add).then_inc(summed, 1)

                dve.wait_ge(r_turned, 1)
                logits = pY[:, 2:4, :].rearrange("p a (t e r) -> p (a t) e r", t=4, r=P // E)[:, :, :, 0]
                link(1, nc.vector.tensor_reduce(stat[:], logits, AX.X, ALU.max))
                link(2, nc.vector.tensor_tensor(score[:], logits, bcast(stat[:], 2, E), ALU.subtract))
                dve.wait_ge(exp_done, 1)
                link(3, nc.vector.tensor_reduce(stat[:], score[:], AX.X, ALU.add))
                link(4, nc.vector.reciprocal(stat[:], stat[:]))
                link(5, nc.vector.tensor_tensor(score[:], score[:], bcast(stat[:], 2, E), ALU.mult))
                link(6, nc.vector.tensor_tensor(score[:], score[:], bcast(s_bias[:], 1, NT), ALU.add))

                def ranks(n, values, m, out):
                    c, s = cmp[:, :, 0:m, 0:m], same[:, :, 0:m, 0:m]
                    mine, other = bcast(values, 3, m), bcast(values, 2, m)
                    nc.vector.tensor_tensor(c, other, mine, ALU.is_gt)
                    link(n, nc.vector.tensor_tensor(s, other, mine, ALU.is_equal))
                    link(n + 1, nc.vector.tensor_tensor(s, s, bcast(before[:, 0:m, 0:m], 1, NT), ALU.mult))
                    link(n + 2, nc.vector.tensor_tensor(c, c, s, ALU.add))
                    link(n + 3, nc.vector.tensor_reduce(out, c, AX.X, ALU.add))

                link(7, nc.vector.tensor_reduce(gmax[:], score[:].rearrange("p t (g i) -> p t g i", g=G), AX.X, ALU.max))
                ranks(8, gmax[:], G, keep[:])
                link(12, nc.vector.tensor_scalar(keep[:], keep[:], 1.5, None, ALU.is_lt))
                grouped = lambda a: a[:].rearrange("p t (g i) -> p t g i", g=G)
                nc.vector.tensor_tensor(grouped(masked), grouped(score), bcast(keep[:], 3, G), ALU.mult)
                link(13, nc.vector.tensor_scalar(gmax[:], keep[:], -MASKED, MASKED, ALU.mult, ALU.add))
                nc.vector.tensor_tensor(grouped(masked), grouped(masked), bcast(gmax[:], 3, G), ALU.add).then_inc(gate_set, 1)
                dve.wait_ge(gate_set, 1)
                ranks(14, masked[:], E, rank[:])
                nc.vector.memset(gate[:, :, 0:2], 1.0)
                nc.vector.scalar_tensor_tensor(out=gate[:, :, 2:X], in0=rank[:], scalar=1.5, in1=score[:],
                                               op0=ALU.is_lt, op1=ALU.mult).then_inc(step, 1)
                for hf in range(2):
                    hidden_product(0, 0, hf)
                    low(0, 0, hf)
                for T in range(NT):
                    dve.wait_ge(b3_done, T + 1)
                    nc.vector.tensor_tensor(S.x[:, T], pY[:, T % 4, :], S.x[:, T], ALU.add).then_inc(summed, 1)

                def body(i):
                    for e2 in range(2):
                        e = 2 * i + e2
                        for hf in range(2):
                            if exists(i, e2, 1):
                                hidden_product(e + 1, 1 - e2, hf)
                                low(e + 1, 1 - e2, hf)
                            add_output(e, hf)

                loop(dve, body)

            @block.gpsimd
            def _(pool):
                pool.wait_ge(r_hi_done, 1)
                nc.gpsimd.tensor_tensor(r_lo[:], r_raw[:], r_hi[:].bitcast(F32), ALU.subtract).then_inc(r_lo_done, 1)

                def split(e, slot, n12):
                    if n12:
                        pool.wait_ge(w12_hi_done, e + 1)
                        wait(pool, hid_done, 2 * (e - 1))
                        nc.gpsimd.tensor_tensor(w12_lo[:, slot], raw[:, slot, 0:2 * DM], w12_hi[:, slot].bitcast(F32),
                                                ALU.subtract).then_inc(w12_lo_done, 1)
                    else:
                        pool.wait_ge(w3_hi_done, e + 1)
                        wait(pool, y_done, 8 * (e - 1))
                        nc.gpsimd.tensor_tensor(w3_lo[:, slot], raw[:, slot, 2 * DM:3 * DM], w3_hi[:, slot].bitcast(F32),
                                                ALU.subtract).then_inc(w3_lo_done, 1)

                split(0, 0, True)
                split(1, 1, True)
                split(0, 0, False)

                def body(i):
                    for e2 in range(2):
                        e = 2 * i + e2
                        if exists(i, e2, 1):
                            split(e + 1, 1 - e2, False)
                        if exists(i, e2, 2):
                            split(e + 2, e2, True)

                loop(pool, body)
        ph.close()


def decoder(nc, d, out):
    with ExitStack() as ctx:
        S = State()
        sb = lambda name, shape, dt=F32: ctx.enter_context(nc.sbuf_tensor(name, shape, dt))
        S.x = sb("x", [P, NT, DM])
        S.xT_hi = sb("xT_hi", [P, KC, TOK], F32R)
        S.xT_lo = sb("xT_lo", [P, KC, TOK], F32R)
        S.ident = sb("ident", [P, P])
        S.ident_bf = sb("ident_bf", [P, P], BF16)
        loaded = ctx.enter_context(nc.semaphore("constants_loaded"))

        with nc.Block() as block:
            @block.sync
            def _(sp):
                sp.dma_start(S.ident[:], d["ident"]).then_inc(loaded, 16)
                sp.dma_start(S.ident_bf[:], d["ident_bf"]).then_inc(loaded, 16)
                for T in range(NT):
                    sp.dma_start(S.x[:, T], d["x_rows"][T]).then_inc(loaded, 16)
                sp.wait_ge(loaded, 16 * (NT + 2))

        run_phases(nc, d, out, S)


def run_phases(nc, d, out, S):
    scratch = nc.dram_tensor("x_natural", (NT, P, DM), F32).ap()
    sub = lambda prefix: {k[len(prefix):]: v for k, v in d.items() if k.startswith(prefix)}
    steps = [
        lambda: attention_phase(nc, "l0a", S, d["l0_wqkv"], d["l0_wo"], d["mask0"], True, xT_raw_dram=d["xT_perm"]),
        lambda: norm_phase(nc, "n1", S, scratch, split_rows=True),
        lambda: cross_attention_phase(nc, "l0x", S, sub("x0_"), 32, scratch),
        lambda: norm_phase(nc, "n2", S),
        lambda: lora_phase(nc, "l0f", S, sub("f0_")),
        lambda: norm_phase(nc, "n3", S),
        lambda: attention_phase(nc, "l1a", S, d["l1_wqkv"], d["l1_wo"], d["mask1"], False, rope_dram=d["rope"]),
        lambda: norm_phase(nc, "n4", S),
        lambda: cross_attention_phase(nc, "l1x", S, sub("x1_"), 64),
        lambda: norm_phase(nc, "n5", S),
        lambda: experts_phase(nc, "l1f", S, sub("f1_")),
        lambda: norm_phase(nc, "n6", S, out),
    ]
    for step in steps:
        step()


def _rows(a):
    return a.reshape(4, 4, 2, 32, -1).transpose(2, 0, 1, 3, 4).reshape(NT, P, -1)


def _k_major(w):
    K, n = w.shape
    return w.reshape(K // P, P, n).transpose(1, 0, 2).reshape(P, -1)


def _group_weights(w):
    return w.reshape(GROUPS, CH, P, KC, P).transpose(0, 4, 1, 3, 2).reshape(GROUPS, P, -1)


def _out_weights(w):
    return w.reshape(DM, GROUPS, QPG, HD).transpose(1, 3, 2, 0).reshape(GROUPS, P, -1)


def _constants():
    bf = np.dtype("bfloat16")
    i = np.arange(P)
    causal = i[:, None] >= i[None, :]
    mask0 = causal & (i[:, None] // SEQ_A == i[None, :] // SEQ_A)
    mask1 = causal & (i[:, None] // SEQ_B == i[None, :] // SEQ_B)
    inv = 1.0 / 500000.0 ** (np.arange(0, HD, 2, dtype=np.float32) / HD)
    wavelen = 2.0 * np.pi / inv
    low, high = 1024 / 1.0, 1024 / 4.0
    scaled = np.where(wavelen > low, inv / 8.0, inv)
    smooth = (1024 / wavelen - 1.0) / (4.0 - 1.0)
    smoothed = (1.0 - smooth) / 8.0 * inv + smooth * inv
    freq = np.where((wavelen <= low) & (wavelen >= high), smoothed, scaled).astype(np.float32)
    angle = (np.arange(SEQ_B, dtype=np.float32)[None, :] * np.concatenate([freq, freq])[:, None]).astype(np.float32)
    sign = np.where(i[:, None] < HD // 2, 1.0, -1.0)
    rope = np.stack([np.cos(angle.astype(np.float64)), sign * np.sin(angle.astype(np.float64))]).astype(np.float32)
    vmask = lambda m: (m == 2 * np.arange(2)[:, None] + (i // SEQ_B)[:, None, None]).astype(np.float32)
    return {
        "ident": np.eye(P, dtype=np.float32),
        "ident_bf": np.eye(P, dtype=np.float32).astype(bf),
        "mask0": np.where(mask0, 0.0, MASKED).astype(np.float32).astype(bf),
        "mask1": np.where(mask1, 0.0, MASKED).astype(np.float32).astype(bf),
        "rope": rope,
        "f0_inv_k": (1.0 / np.arange(1, 9, dtype=np.float32)).reshape(1, 8),
        "f1_before": (np.arange(16)[:, None] > np.arange(16)[None, :]).astype(np.float32).reshape(1, 256),
        "x0_kmask": (i[:, None] % 4 == np.arange(4)).astype(np.float32),
        "x1_kmask": (i[:, None] // 16 % 4 == np.arange(4)).astype(np.float32),
        "x0_vmask": vmask(np.arange(DM) % 4).astype(bf),
        "x1_vmask": vmask(np.arange(DM) // 16 % 4).astype(bf),
        "x0_same": (i[:, None] // 4 == np.arange(32)).astype(np.float32),
    }


def _lay_out(i):
    n = {k: np.asarray(v) for k, v in i.items()}
    a = _constants()
    x = n["x"]
    a["x_rows"] = _rows(x)
    a["xT_perm"] = _k_major(x.transpose(2, 1, 0).reshape(DM, TOK))
    w = n["L0_attn_weight_qkv"].reshape(GROUPS, CH, P, DM)
    a["l0_wqkv"] = _group_weights(np.concatenate([w[:, 4:6], w[:, 0:4]], axis=1))
    a["l0_wo"] = _out_weights(n["L0_attn_weight_proj"])
    w = np.concatenate([n["L1_attn_Wk"].reshape(GROUPS, 1, P, DM), n["L1_attn_Wv"].reshape(GROUPS, 1, P, DM),
                        n["L1_attn_Wq"].reshape(GROUPS, QPG, P, DM)], axis=1)
    a["l1_wqkv"] = _group_weights(w)
    a["l1_wo"] = _out_weights(n["L1_attn_Wo"])
    for layer in range(2):
        o, x = f"L{layer}_xattn_", f"x{layer}_"
        if layer == 0:
            wk, wv, wq, wo = [n[o + k].T for k in ("Wk", "Wv", "Wq", "Wo")]
            bk, bv, bq = n[o + "bk"], n[o + "bv"], n[o + "bq"]
            a[x + "inter"] = np.repeat(n[o + "interference"].reshape(KC, 4, 1, 4, 4), 8, axis=2).reshape(KC, P, 4).transpose(1, 0, 2)
            a[x + "amp"] = n[o + "amp"].reshape(1, 1)
        else:
            share = lambda w: np.repeat(w.reshape(-1, 8, 1, 16), 4, axis=2).reshape(w.shape[0] if w.ndim > 1 else 1, DM)
            wk, wv, wq, wo = share(n[o + "Wk"]), share(n[o + "Wv"]), n[o + "Wq"], n[o + "Wo"]
            bk, bv, bq = share(n[o + "bk"]), share(n[o + "bv"]), n[o + "bq"]
        by_chunk = lambda w: w.reshape(KC, P, KC, P).transpose(1, 2, 0, 3).reshape(P, -1)
        a[x + "w"] = np.stack([by_chunk(wk), by_chunk(wv), by_chunk(wq), _k_major(wo)])
        a[x + "biases"] = np.stack([b.reshape(KC, P).T for b in (bk, bv, bq)], axis=1)
        a[x + "bo"] = n[o + "bo"].reshape(1, DM)
        a[x + "ctxT"] = _k_major(n["ctx_4096"].reshape(TOK, DM).T)
    f = "L0_ffn_"
    lora_a = n[f + "lora_A"].transpose(1, 0, 2).reshape(DM, P)
    router = np.repeat(n[f + "W_router"].T, P // 8, axis=1)
    a["f0_small_w"] = np.concatenate([_k_major(lora_a), _k_major(router), n[f + "lora_B"].reshape(P, DM)], axis=1)
    a["f0_base_w"] = _k_major(n[f + "W_base"].T)
    a["f0_base_bias"] = n[f + "b_base"].reshape(1, DM)
    a["f0_router_bias"] = np.repeat(n[f + "b_router"], P // 8).reshape(P, 1)
    f = "L1_ffn_"
    two = lambda w: w.reshape(DM, 2, P).transpose(1, 0, 2)
    w1 = np.concatenate([two(n[f + "sw1"]), n[f + "ew1"]])
    w2 = np.concatenate([two(n[f + "sw2"]), n[f + "ew2"]])
    w3 = np.concatenate([n[f + "sw3"].reshape(2, P, DM), n[f + "ew3"]])
    b1 = np.concatenate([n[f + "sb1"].reshape(2, P), n[f + "eb1"]])
    b2 = np.concatenate([n[f + "sb2"].reshape(2, P), n[f + "eb2"]])
    a["f1_w"] = np.concatenate([np.stack([_k_major(w) for w in w1]), np.stack([_k_major(w) for w in w2]), w3,
                                b1[:, :, None], b2[:, :, None]], axis=2)
    a["f1_b3"] = np.concatenate([n[f + "sb3"].reshape(1, DM), np.zeros((1, DM), np.float32), n[f + "eb3"]])
    a["f1_r_w"] = _k_major(np.repeat(n[f + "router_w"], P // 16, axis=1))
    a["f1_r_bias"] = np.repeat(n[f + "router_b"], P // 16).reshape(P, 1)
    a["f1_s_bias"] = n[f + "router_bias"].reshape(1, 16)
    return {k: np.ascontiguousarray(v) for k, v in a.items()}


def kernel(**inputs):
    import concourse.bacc as _bacc
    from concourse.bass_utils import run_bass_kernel_spmd as _run

    nc = _bacc.Bacc("TRN2", target_bir_lowering=False, num_devices=1)
    arrays = _lay_out(inputs)
    d = {k: nc.dram_tensor(f"in_{k}_dram", v.shape, mybir.dt.from_np(v.dtype), kind="ExternalInput").ap()
         for k, v in arrays.items()}
    out = nc.dram_tensor("out_0_dram", (NT, P, DM), F32, kind="ExternalOutput").ap()
    decoder(nc, d, out)
    r = _run(nc, [{f"in_{k}_dram": v for k, v in arrays.items()}], core_ids=[0])
    rows = r.results[0]["out_0_dram"]
    return rows.reshape(SEQ_A, SEQ_B, DM)
```

```python
from contextlib import ExitStack

import numpy as np

import concourse.bass as bass
from concourse import mybir

F32 = mybir.dt.float32
F32R = mybir.dt.float32r
BF16 = mybir.dt.bfloat16
ALU = mybir.AluOpType
ACT = mybir.ActivationFunctionType
AX = mybir.AxisListType

P = 128
SEQ_A, SEQ_B, DM = 16, 64, 512
TOK = SEQ_A * SEQ_B
KC = DM // P
NT = TOK // P
HALF = TOK // 2
GROUPS, QPG, HD = 8, 4, 128
CH = QPG + 2
EPS = 1e-5
EW = 3 * DM + 2
MASKED = -1e30




def wait(engine, semaphore, value):
    if isinstance(value, int) and value <= 0:
        return
    engine.wait_ge(semaphore, value)


def three_pass(pe, out, w_hi, w_lo, x_hi, x_lo, start, stop):
    pe.matmul(out, w_hi, x_hi, start=start, stop=False, skip_group_check=True)
    pe.matmul(out, w_hi, x_lo, start=False, stop=False, skip_group_check=True)
    return pe.matmul(out, w_lo, x_hi, start=False, stop=stop, skip_group_check=True)


class Phase:

    def __init__(self, nc, ctx, name):
        self.nc, self.ctx, self.name = nc, ctx, name
        self.semaphores = []

    def sb(self, name, shape, dt=F32):
        return self.ctx.enter_context(self.nc.sbuf_tensor(f"{self.name}_{name}", shape, dt))

    def ps(self, name, shape, dt=F32):
        return self.ctx.enter_context(self.nc.psum_tensor(f"{self.name}_{name}", shape, dt))

    def sem(self, name):
        self.semaphores.append(self.nc.alloc_semaphore(name=f"{self.name}_{name}"))
        return self.semaphores[-1]

    def close(self):
        self.nc.clear_and_free_semaphores(self.semaphores)
        self.nc.all_engine_barrier()


def attention_phase(nc, name, S, w_dram, wo_dram, mask_dram, layer0, next_loads, xT_raw_dram=None, rope_dram=None,
                    x_rows_dram=None, ident_dram=None):
    scale = float(HD) ** -0.5
    n_small = 32 if layer0 else 48
    S.begin_phase()
    with ExitStack() as ctx:
        ph = Phase(nc, ctx, name)
        sb, ps, sem = ph.sb, ph.ps, ph.sem
        QT = sb("QT", [P, 2, QPG, HALF])
        KT = sb("KT", [P, 2, HALF])
        VT = sb("VT", [P, HALF])
        V = sb("V", [P, 2, 4, HD])
        W_raw = S.raw[:, 0:CH * DM].rearrange("p (c k n) -> p c k n", c=CH, k=KC)
        W_hi = sb("W_hi", [P, CH, KC, P], F32R)
        W_lo = sb("W_lo", [P, CH, KC, P], F32R)
        Wo_raw = S.raw[:, CH * DM:(CH + QPG) * DM].rearrange("p (h n) -> p h n", h=QPG)
        Wo_hi = sb("Wo_hi", [P, QPG, DM], F32R)
        Wo_lo = sb("Wo_lo", [P, QPG, DM], F32R)
        O_hi = sb("O_hi", [P, 2, QPG, HALF], F32R)
        O_lo = sb("O_lo", [P, 2, QPG, HALF], F32R)
        prob = sb("prob", [P, 2, QPG, P])
        probT = sb("probT", [P, 2, QPG, P])
        top = sb("top", [P, 2, QPG])
        total = sb("total", [P, 2, QPG])
        inv = sb("inv", [P, 2, QPG])
        mask = sb("mask", [P, P], BF16)
        if not layer0:
            cos = sb("cos", [P, SEQ_B])
            sin = sb("sin", [P, SEQ_B])
            r_cos = sb("r_cos", [P, 2, HALF])
            r_sin = sb("r_sin", [P, 2, HALF])
        pA = ps("pA", [P, 2, HALF])
        pS = ps("pS", [P, QPG, P])
        pP = ps("pP", [P, QPG, P])
        pV = ps("pV", [P, 4, HD])
        pO = ps("pO", [P, QPG, P])
        pC = ps("pC", [P, 2, DM])
        mask_loaded = sem("mask_loaded")
        x_loaded = sem("x_loaded")
        first_loaded = [sem(f"first_loaded{i}") for i in range(3 if layer0 else 0)]
        xT_loaded = [sem(f"xT_loaded{hf}") for hf in range(2)]
        xT_hi_done = sem("xT_hi_done")
        xT_lo_done = sem("xT_lo_done")
        w_loaded = sem("w_loaded")
        wo_loaded = sem("wo_loaded")
        w_hi_done = sem("w_hi_done")
        w_lo_done = sem("w_lo_done")
        wo_hi_done = sem("wo_hi_done")
        wo_lo_done = sem("wo_lo_done")
        proj_done = sem("proj_done")
        chunk_read = [sem("chunk_read0"), sem("chunk_read1")]
        cos_done = sem("cos_done")
        rope_done = sem("rope_done")
        v_turned = sem("v_turned")
        v_ready = sem("v_ready")
        scores_done = sem("scores_done")
        masked = sem("masked")
        top_done = sem("top_done")
        shifted = sem("shifted")
        exp_done = sem("exp_done")
        total_done = sem("total_done")
        inv_done = sem("inv_done")
        prob_ready = sem("prob_ready")
        prob_turned = sem("prob_turned")
        probT_ready = sem("probT_ready")
        av_done = sem("av_done")
        o_hi_done = sem("o_hi_done")
        o_lo_done = sem("o_lo_done")
        out_done = sem("out_done")
        summed = sem("summed")

        AHEAD = ((0, 1, 2), (3, 4), (5,), ())

        def o_tile(O, u2, t):
            if layer0:
                return O[:, u2].rearrange("p h (a t b) -> p h t b a", t=4, b=8)[:, :, t]
            return O[:, u2, :, t * P:(t + 1) * P]

        def po_view():
            if layer0:
                return pO[:, :, :].rearrange("p h (b a) -> p h b a", a=SEQ_A)
            return pO[:, :, :]

        def o_columns(O, u2, h, t):
            return O[:, u2, h, t * P:(t + 1) * P]

        def head_sum(ap):
            return ap.unsqueeze(2).broadcast_to([P, QPG, P])

        def loop(engine, body):
            body(0)
            with engine.Fori(1, GROUPS - 1) as g:
                body(g)
            body(GROUPS - 1)

        def is_last(g, hf):
            return isinstance(g, int) and g == GROUPS - 1 and hf == 1

        def is_first(g, hf):
            return isinstance(g, int) and g == 0 and hf == 0

        with nc.Block() as block:

            @block.sync
            def _(sp):
                if layer0:
                    half = lambda hf: QT[:, hf].rearrange("p k n -> p (k n)")
                    sp.dma_start(S.raw[:, 0:DM], w_dram[0][:, 0:DM]).then_inc(first_loaded[0], 16)
                    sp.dma_start(half(0), xT_raw_dram[0]).then_inc(xT_loaded[0], 16)
                    sp.dma_start(S.raw[:, DM:CH * DM], w_dram[0][:, DM:CH * DM]).then_inc(first_loaded[1], 16)
                    sp.dma_start(half(1), xT_raw_dram[1]).then_inc(xT_loaded[1], 16)
                    sp.dma_start(S.ident[:], ident_dram).then_inc(mask_loaded, 16)
                sp.dma_start(mask[:], mask_dram).then_inc(mask_loaded, 16)
                if not layer0:
                    sp.dma_start(cos[:], rope_dram[0]).then_inc(mask_loaded, 16)
                    sp.dma_start(sin[:], rope_dram[1]).then_inc(mask_loaded, 16)
                if layer0:
                    sp.dma_start(S.raw[:, CH * DM:(CH + QPG) * DM], wo_dram[0]).then_inc(first_loaded[2], 16)
                    for T in range(NT):
                        sp.dma_start(S.x[:, T], x_rows_dram[T]).then_inc(x_loaded, 16)

                with sp.Fori(1, GROUPS) as g:
                    sp.wait_ge(w_hi_done, CH * g)
                    sp.wait_ge(w_lo_done, CH * g)
                    sp.dma_start(W_raw.rearrange("p c k n -> p (c k n)"), w_dram[g]).then_inc(w_loaded, 16)
                    sp.wait_ge(wo_hi_done, QPG * g)
                    sp.wait_ge(wo_lo_done, QPG * g)
                    sp.dma_start(Wo_raw.rearrange("p h n -> p (h n)"), wo_dram[g]).then_inc(wo_loaded, 16)
                sp.wait_ge(w_lo_done, CH * GROUPS)
                sp.wait_ge(wo_lo_done, QPG * GROUPS)
                S.prefetch(sp, next_loads)

            @block.tensor
            def _(pe):
                def project(u, g, hf, c):
                    pe.wait_ge(w_hi_done, CH * g + c + 1)
                    pe.wait_ge(w_lo_done, CH * g + c + 1)
                    wait(pe, chunk_read[c % 2], 3 * u + c // 2)
                    if layer0 and c == 0 and isinstance(u, int) and u < 2:
                        pe.wait_ge(xT_lo_done, KC * (u + 1))
                    tok = slice(hf * HALF, (hf + 1) * HALF)
                    for k in range(KC):
                        mm = three_pass(pe, pA[:, c % 2, :], W_hi[:, c, k, :], W_lo[:, c, k, :],
                                        S.xT_hi[:, k, tok], S.xT_lo[:, k, tok], k == 0, k == KC - 1)
                    mm.then_inc(proj_done, 1)

                def turn_v(u, hf):
                    wait(pe, v_ready, u)
                    pe.wait_ge(chunk_read[1], 3 * u + 1)
                    for t in range(4):
                        mm = pe.transpose(pV[:, t, :], VT[:, t * P:(t + 1) * P], S.ident[:])
                    mm.then_inc(v_turned, 1)

                def scores(u, hf, t):
                    wait(pe, masked, 4 * u + t)
                    if t == 0:
                        if layer0:
                            pe.wait_ge(chunk_read[0], 3 * u + 3)
                            pe.wait_ge(chunk_read[1], 3 * u + 3)
                        else:
                            pe.wait_ge(rope_done, 5 * u + 5)
                    cols = slice(t * P, (t + 1) * P)
                    for h in range(QPG):
                        mm = pe.matmul(pS[:, h, :], QT[:, hf, h, cols], KT[:, hf, cols],
                                       start=True, stop=True, skip_group_check=True)
                    mm.then_inc(scores_done, 1)

                def turn_probs(u, t):
                    n = 4 * u + t
                    pe.wait_ge(prob_ready, n + 1)
                    wait(pe, probT_ready, n)
                    for h in range(QPG):
                        mm = pe.transpose(pP[:, h, :], prob[:, t % 2, h, :], S.ident[:])
                    mm.then_inc(prob_turned, 1)

                def attend(u, hf, t):
                    n = 4 * u + t
                    pe.wait_ge(probT_ready, n + 1)
                    if t == 0:
                        pe.wait_ge(v_ready, u + 1)
                    wait(pe, o_lo_done, n)
                    pe.matmul(pO[:, :, :], V[:, hf, t, :], probT[:, t % 2, :, :],
                              start=True, stop=True).then_inc(av_done, 1)

                def out_project(u, g, hf, t):
                    n = 4 * u + t
                    if t == 0:
                        pe.wait_ge(o_lo_done, 4 * u + 4)
                        if hf == 0:
                            pe.wait_ge(wo_hi_done, QPG * (g + 1))
                            pe.wait_ge(wo_lo_done, QPG * (g + 1))
                    wait(pe, summed, n - 1)
                    for h in range(QPG):
                        mm = three_pass(pe, pC[:, t % 2, :], o_columns(O_hi, hf, h, t), o_columns(O_lo, hf, h, t),
                                        Wo_hi[:, h, :], Wo_lo[:, h, :], h == 0, h == QPG - 1)
                    mm.then_inc(out_done, 1)

                for c in range(CH):
                    project(0, 0, 0, c)
                pe.wait_ge(mask_loaded, n_small)
                turn_v(0, 0)
                scores(0, 0, 0)

                def body(g):
                    for hf in range(2):
                        u = 2 * g + hf
                        last = is_last(g, hf)
                        for t in range(4):
                            if t < 3:
                                scores(u, hf, t + 1)
                            elif not last:
                                scores(u + 1, 1 - hf, 0)
                            turn_probs(u, t)
                            if not last:
                                for c in AHEAD[t]:
                                    project(u + 1, g + hf, 1 - hf, c)
                                if t == 3:
                                    turn_v(u + 1, 1 - hf)
                            if t == 3 and not is_first(g, hf):
                                out_project(u - 1, g - 1 + hf, 1 - hf, t)
                            attend(u, hf, t)
                            if t < 3 and not is_first(g, hf):
                                out_project(u - 1, g - 1 + hf, 1 - hf, t)

                loop(pe, body)
                for t in range(4):
                    out_project(2 * GROUPS - 1, GROUPS - 1, 1, t)

            @block.scalar
            def _(act):
                def split_w(g, c):
                    if isinstance(g, int) and g == 0:
                        if not layer0:
                            S.wait_prefetched(act)
                        elif c < 2:
                            act.wait_ge(first_loaded[c], 16)
                    elif c == 0:
                        act.wait_ge(w_loaded, 16 * g)
                    if not (isinstance(g, int) and g == 0):
                        act.wait_ge(proj_done, CH * (2 * g - 1) + c + 1)
                    nc.scalar.copy(W_hi[:, c], W_raw[:, c]).then_inc(w_hi_done, 1)

                def split_wo(g):
                    if layer0 and isinstance(g, int) and g == 0:
                        act.wait_ge(first_loaded[2], 16)
                    wait(act, wo_loaded, 16 * g)
                    if not (isinstance(g, int) and g == 0):
                        act.wait_ge(out_done, 8 * g)
                    for h in range(QPG):
                        nc.scalar.copy(Wo_hi[:, h], Wo_raw[:, h]).then_inc(wo_hi_done, 1)

                def read_chunk(u, hf, c):
                    if not layer0 and c != 1:
                        return
                    act.wait_ge(proj_done, CH * u + c + 1)
                    if c == 1:
                        wait(act, v_turned, u)
                        dst = VT[:, :]
                    else:
                        wait(act, scores_done, 4 * u - 4)
                        dst = KT[:, hf, :] if c == 0 else QT[:, hf, c - 2, :]
                    nc.scalar.copy(dst, pA[:, c % 2, :]).then_inc(chunk_read[c % 2], 1)

                def read_v(u, hf):
                    act.wait_ge(v_turned, u + 1)
                    wait(act, av_done, 4 * u - 4)
                    nc.scalar.copy(V[:, hf], pV[:, :, :]).then_inc(v_ready, 1)

                def exponent(u, t):
                    n = 4 * u + t
                    act.wait_ge(shifted, n + 1)
                    nc.scalar.activation(prob[:, t % 2], prob[:, t % 2], ACT.Exp, scale=scale).then_inc(exp_done, 1)

                def read_probT(u, t):
                    n = 4 * u + t
                    act.wait_ge(prob_turned, n + 1)
                    wait(act, av_done, n - 1)
                    nc.scalar.copy(probT[:, t % 2], pP[:, :, :]).then_inc(probT_ready, 1)

                def read_o(u, hf, t):
                    n = 4 * u + t
                    act.wait_ge(av_done, n + 1)
                    wait(act, out_done, 4 * u - 4)
                    nc.scalar.copy(o_tile(O_hi, hf, t), po_view()).then_inc(o_hi_done, 1)

                split_w(0, 0)
                if layer0:
                    for hf in range(2):
                        act.wait_ge(xT_loaded[hf], 16)
                        for k in range(KC):
                            nc.scalar.copy(S.xT_hi[:, k, hf * HALF:(hf + 1) * HALF], QT[:, hf, k, :]).then_inc(xT_hi_done, 1)
                        if hf == 0:
                            for c in range(1, CH):
                                split_w(0, c)
                    act.wait_ge(xT_lo_done, 2 * KC)
                else:
                    for c in range(1, CH):
                        split_w(0, c)
                for c in range(CH):
                    read_chunk(0, 0, c)
                read_v(0, 0)
                exponent(0, 0)

                def body(g):
                    for hf in range(2):
                        u = 2 * g + hf
                        last = is_last(g, hf)
                        for t in range(4):
                            read_probT(u, t)
                            if t < 3:
                                exponent(u, t + 1)
                            elif not last:
                                exponent(u + 1, 0)
                            if not last:
                                for c in AHEAD[t]:
                                    read_chunk(u + 1, 1 - hf, c)
                                    if hf == 0 and not (isinstance(g, int) and g == GROUPS - 1):
                                        split_w(g + 1, c)
                                if t == 3:
                                    read_v(u + 1, 1 - hf)
                            read_o(u, hf, t)
                        if hf == 0:
                            split_wo(g)

                loop(act, body)

            @block.vector
            def _(dve):
                def soften(u, t):
                    n = 4 * u + t
                    dve.wait_ge(scores_done, n + 1)
                    wait(dve, prob_turned, n - 1)
                    nc.vector.tensor_tensor(prob[:, t % 2], pS[:, :, :], mask[:].unsqueeze(1).broadcast_to([P, QPG, P]),
                                            ALU.add).then_inc(masked, 1)
                    dve.wait_ge(masked, n + 1)
                    nc.vector.tensor_reduce(top[:, t % 2], prob[:, t % 2], AX.X, ALU.max).then_inc(top_done, 1)
                    dve.wait_ge(top_done, n + 1)
                    nc.vector.tensor_tensor(prob[:, t % 2], prob[:, t % 2], head_sum(top[:, t % 2]),
                                            ALU.subtract).then_inc(shifted, 1)

                def row_totals(u, t):
                    n = 4 * u + t
                    dve.wait_ge(exp_done, n + 1)
                    nc.vector.tensor_reduce(total[:, t % 2], prob[:, t % 2], AX.X, ALU.add).then_inc(total_done, 1)
                    dve.wait_ge(total_done, n + 1)
                    wait(dve, prob_ready, n - 1)
                    nc.vector.reciprocal(inv[:, t % 2], total[:, t % 2]).then_inc(inv_done, 1)

                def rope(u, c):
                    if layer0 or c == 1:
                        return
                    i = 0 if c == 0 else c - 1
                    m = 5 * u + i
                    slot = RS[0]
                    RS[0] = 1 - RS[0]
                    dve.wait_ge(proj_done, CH * u + c + 1)
                    wait(dve, rope_done, m - 1)
                    src = pA[:, c % 2, :].rearrange("p (a b) -> p a b", b=SEQ_B)
                    rc = r_cos[:, slot].rearrange("p (a b) -> p a b", b=SEQ_B)
                    rs = r_sin[:, slot].rearrange("p (a b) -> p a b", b=SEQ_B)
                    n_a = HALF // SEQ_B
                    h = HD // 2
                    nc.vector.tensor_tensor(rc, src, cos[:].unsqueeze(1).broadcast_to([P, n_a, SEQ_B]), ALU.mult)
                    nc.vector.tensor_tensor(rs[0:h], src[h:P], sin[h:P].unsqueeze(1).broadcast_to([h, n_a, SEQ_B]), ALU.mult)
                    nc.vector.tensor_tensor(rs[h:P], src[0:h], sin[0:h].unsqueeze(1).broadcast_to([h, n_a, SEQ_B]),
                                            ALU.mult).then_inc(chunk_read[c % 2], 1)

                def read_o_lo(u, hf, t):
                    n = 4 * u + t
                    dve.wait_ge(o_hi_done, n + 1)
                    nc.vector.tensor_tensor(o_tile(O_lo, hf, t), po_view(), o_tile(O_hi, hf, t).bitcast(F32),
                                            ALU.subtract).then_inc(o_lo_done, 1)

                def add_out(u, hf, t):
                    n = 4 * u + t
                    dve.wait_ge(out_done, n + 1)
                    wait(dve, summed, n - 3)
                    T = 4 * hf + t
                    nc.vector.tensor_tensor(S.x[:, T], pC[:, t % 2, :], S.x[:, T], ALU.add).then_inc(summed, 1)

                RS = [0]
                if layer0:
                    for hf in range(2):
                        for k in range(KC):
                            tok = slice(hf * HALF, (hf + 1) * HALF)
                            dve.wait_ge(xT_hi_done, KC * hf + k + 1)
                            nc.vector.tensor_tensor(S.xT_lo[:, k, tok], QT[:, hf, k, :], S.xT_hi[:, k, tok].bitcast(F32),
                                                    ALU.subtract).then_inc(xT_lo_done, 1)
                    dve.wait_ge(x_loaded, 16 * NT)
                dve.wait_ge(mask_loaded, n_small)
                for c in range(CH):
                    rope(0, c)
                soften(0, 0)
                row_totals(0, 0)

                def body(g):
                    for hf in range(2):
                        u = 2 * g + hf
                        last = is_last(g, hf)
                        for t in range(4):
                            nu, nt = (u, t + 1) if t < 3 else (u + 1, 0)
                            todo = t < 3 or not last
                            if todo:
                                soften(nu, nt)
                            if not last:
                                for c in AHEAD[t][:1]:
                                    rope(u + 1, c)
                            if todo:
                                row_totals(nu, nt)
                            if not last:
                                for c in AHEAD[t][1:]:
                                    rope(u + 1, c)
                            if t == 3 and not is_first(g, hf):
                                add_out(u - 1, 1 - hf, t)
                            read_o_lo(u, hf, t)
                            if t < 3 and not is_first(g, hf):
                                add_out(u - 1, 1 - hf, t)

                loop(dve, body)
                for t in range(4):
                    add_out(2 * GROUPS - 1, 1, t)

            @block.gpsimd
            def _(pool):
                def split_w(g, c):
                    pool.wait_ge(w_hi_done, CH * g + c + 1)
                    if not (isinstance(g, int) and g == 0):
                        pool.wait_ge(proj_done, CH * (2 * g - 1) + c + 1)
                    nc.gpsimd.tensor_tensor(W_lo[:, c], W_raw[:, c], W_hi[:, c].bitcast(F32),
                                            ALU.subtract).then_inc(w_lo_done, 1)

                def split_wo(g):
                    if not (isinstance(g, int) and g == 0):
                        pool.wait_ge(out_done, 8 * g)
                    for h in range(QPG):
                        pool.wait_ge(wo_hi_done, QPG * g + h + 1)
                        nc.gpsimd.tensor_tensor(Wo_lo[:, h], Wo_raw[:, h], Wo_hi[:, h].bitcast(F32),
                                                ALU.subtract).then_inc(wo_lo_done, 1)

                def divide(u, t):
                    n = 4 * u + t
                    pool.wait_ge(inv_done, n + 1)
                    nc.gpsimd.tensor_tensor(prob[:, t % 2], prob[:, t % 2], head_sum(inv[:, t % 2]),
                                            ALU.mult).then_inc(prob_ready, 1)

                def rope_add(u, hf, c):
                    if layer0 or c == 1:
                        return
                    slot = RS[0]
                    RS[0] = 1 - RS[0]
                    pool.wait_ge(chunk_read[c % 2], 3 * u + c // 2 + 1)
                    wait(pool, scores_done, 4 * u - 4)
                    dst = KT[:, hf, :] if c == 0 else QT[:, hf, c - 2, :]
                    nc.gpsimd.tensor_tensor(dst, r_cos[:, slot], r_sin[:, slot], ALU.add).then_inc(rope_done, 1)

                RS = [0]
                for c in range(CH):
                    split_w(0, c)
                for c in range(CH):
                    rope_add(0, 0, c)
                divide(0, 0)

                def body(g):
                    for hf in range(2):
                        u = 2 * g + hf
                        last = is_last(g, hf)
                        for t in range(4):
                            if not last:
                                for c in AHEAD[t][:1]:
                                    rope_add(u + 1, 1 - hf, c)
                            if t < 3:
                                divide(u, t + 1)
                            elif not last:
                                divide(u + 1, 0)
                            if not last:
                                for c in AHEAD[t][1:]:
                                    rope_add(u + 1, 1 - hf, c)
                                if hf == 0 and not (isinstance(g, int) and g == GROUPS - 1):
                                    for c in AHEAD[t]:
                                        split_w(g + 1, c)
                        if hf == 0:
                            split_wo(g)

                loop(pool, body)
        ph.close()


class State:

    def __init__(self, nc, ctx):
        sb = lambda name, shape, dt=F32: ctx.enter_context(nc.sbuf_tensor(name, shape, dt))
        self.x = sb("x", [P, NT, DM])
        self.xT_hi = sb("xT_hi", [P, KC, TOK], F32R)
        self.xT_lo = sb("xT_lo", [P, KC, TOK], F32R)
        self.ident = sb("ident", [P, P])
        self.raw = sb("raw", [P, (CH + QPG) * DM])
        self.prefetched = ctx.enter_context(nc.semaphore("prefetched"))
        self.loads = 0

    def prefetch(self, sp, loads):
        for dst, src in loads:
            sp.dma_start(dst, src).then_inc(self.prefetched, 16)
        self.loads += len(loads)

    def wait_prefetched(self, engine):
        engine.wait_ge(self.prefetched, 16 * self.loads_before)

    def begin_phase(self):
        self.loads_before = self.loads


class Norm:

    def __init__(self, nc, ph, tag, S, groups, banks=None, ring=4, split_rows=False):
        self.nc, self.S, self.groups, self.banks, self.ring, self.split_rows = nc, S, groups, banks, ring, split_rows
        self.stats = ph.sb(tag + "_stats", [P, NT, 6])
        self.mv = ph.sb(tag + "_mv", [P, NT, 2])
        self.var, self.dev, self.rstd, self.newton = [ph.sb(f"{tag}_{n}", [P, NT]) for n in ("var", "dev", "rstd", "newton")]
        names = ("stats_done", "mv_done", "var_done", "dev_done", "newton_step", "normed", "turned", "x_hi_done", "x_lo_done")
        (self.stats_done, self.mv_done, self.var_done, self.dev_done, self.newton_step,
         self.normed, self.turned, self.x_hi_done, self.x_lo_done) = [ph.sem(f"{tag}_{n}") for n in names]

    def variances(self, dve, i):
        nc, (a, b) = self.nc, self.groups[i]
        for T in range(a, b):
            nc.vector.bn_stats(self.stats[:, T], self.S.x[:, T]).then_inc(self.stats_done, 1)
        for T in range(a, b):
            dve.wait_ge(self.stats_done, T + 1)
            nc.vector.bn_aggr(self.mv[:, T], self.stats[:, T]).then_inc(self.mv_done, 1)
        dve.wait_ge(self.mv_done, b)
        nc.vector.tensor_scalar(self.var[:, a:b], self.mv[:, a:b, 1], EPS, None, ALU.add).then_inc(self.var_done, 1)

    def scale_rows(self, dve, i):
        nc, (a, b) = self.nc, self.groups[i]
        var, dev, r, t = self.var[:, a:b], self.dev[:, a:b], self.rstd[:, a:b], self.newton[:, a:b]
        dve.wait_ge(self.dev_done, i + 1)
        dve.wait_ge(self.var_done, i + 1)
        steps = (lambda: nc.vector.reciprocal(r, dev),
                 lambda: nc.vector.tensor_tensor(t, r, r, ALU.mult),
                 lambda: nc.vector.tensor_tensor(t, t, var, ALU.mult),
                 lambda: nc.vector.tensor_scalar(t, t, -0.5, 1.5, ALU.mult, ALU.add),
                 lambda: nc.vector.tensor_tensor(r, r, t, ALU.mult))
        for n, step in enumerate(steps):
            step().then_inc(self.newton_step, 1)
            dve.wait_ge(self.newton_step, len(steps) * i + n + 1)
        for T in range(a, b):
            nc.vector.tensor_scalar(self.S.x[:, T], self.S.x[:, T], self.mv[:, T, 0:1], self.rstd[:, T:T + 1],
                                    ALU.subtract, ALU.mult).then_inc(self.normed, 1)

    def low(self, dve, T):
        dve.wait_ge(self.x_hi_done, T + 1)
        for (lo, bank), (hi, _) in zip(self.parts(self.S.xT_lo, T), self.parts(self.S.xT_hi, T)):
            ins = self.nc.vector.tensor_tensor(lo, bank, hi.bitcast(F32), ALU.subtract)
        ins.then_inc(self.x_lo_done, 1)

    def root(self, act, i):
        a, b = self.groups[i]
        act.wait_ge(self.var_done, i + 1)
        self.nc.scalar.activation(self.dev[:, a:b], self.var[:, a:b], ACT.Sqrt).then_inc(self.dev_done, 1)

    def high(self, act, T):
        act.wait_ge(self.turned, T + 1)
        for hi, bank in self.parts(self.S.xT_hi, T):
            ins = self.nc.scalar.copy(hi, bank)
        ins.then_inc(self.x_hi_done, 1)

    def turn(self, pe, T):
        pe.wait_ge(self.normed, T + 1)
        wait(pe, self.x_lo_done, T - self.ring + 1)
        for k in range(KC):
            mm = pe.transpose(self.banks(T)[:, k], self.S.x[:, T, k * P:(k + 1) * P], self.S.ident[:])
        mm.then_inc(self.turned, 1)

    def parts(self, xT, T):
        if not self.split_rows:
            return [(xT[:, :, T * P:(T + 1) * P], self.banks(T))]
        hb, r = divmod(T, 4)
        to = xT[:].rearrange("p k (r a h b) -> p k r h a b", r=4, a=4, h=2)[:, :, r, hb]
        return [(to[:, k], self.banks(T)[:, k].rearrange("p (a b) -> p a b", a=4)) for k in range(KC)]


def cross_attention_phase(nc, name, S, d, rows_per_unit, ctx_half, next_loads, x_dram=None):
    mixed = rows_per_unit == 32
    W = DM // rows_per_unit // 2
    U = P // rows_per_unit
    D = 1 if mixed else 16
    scale = float(8 if mixed else 16) ** -0.5
    SB = SEQ_B
    FILLS = 2 * KC
    LEFT = 3 * FILLS // 2
    S.begin_phase()
    with ExitStack() as ctx:
        ph = Phase(nc, ctx, name)
        sb, ps, sem = ph.sb, ph.ps, ph.sem
        with ExitStack() as early:
            ph_early = Phase(nc, early, name)
            ctx_hi = ph_early.sb("ctx_hi", [P, KC, TOK], F32R)
            ctx_lo = ph_early.sb("ctx_lo", [P, KC, TOK], F32R)
        Kmask = sb("Kmask", [P, 2, KC, 4, P])
        Vmask = sb("Vmask", [P, 2, 2, 2 * DM + 5 * D])
        W_raw = S.raw[:, 0:KC * DM].rearrange("p (k n) -> p k n", k=KC)
        W_hi = sb("W_hi", [P, KC, DM], F32R)
        W_lo = sb("W_lo", [P, KC, DM], F32R)
        QT = sb("QT", [P, KC, TOK])
        KT = sb("KT", [P, KC, TOK])
        VT = sb("VT", [P, KC, TOK])
        ctx_raw = [S.raw[:, KC * DM:2 * KC * DM].rearrange("p (k n) -> p k n", k=KC),
                   QT[:, 0:2, :].rearrange("p a (b n) -> p (a b) n", n=HALF)]
        Qunit = sb("Qunit", [P, 2, KC, U, P])
        Ktile = sb("Ktile", [P, KC, P])
        Vtile = sb("Vtile", [P, KC, P])
        prob = sb("prob", [P, 4, 8, SB])
        probT = sb("probT", [P, 2, 4, P])
        top = sb("top", [P, 4, 8])
        total = sb("total", [P, 4, 8])
        inv = sb("inv", [P, 4, 8])
        row_mask = sb("row_mask", [P, 4])
        biases = sb("biases", [P, 3, KC])
        bo = sb("bo", [P, DM])
        if mixed:
            inter = sb("inter", [P, KC, 4])
            amp = sb("amp", [P, 1])
            same = sb("same", [P, 32])
            mix = sb("mix", [P, KC, P])
        pM = ps("pM", [P, 2, DM])
        pN = ps("pN", [P, 4, DM])
        pS = pN[:, 0:2, :]
        pO = pN[:, 2:4, :].rearrange("p e (c n) -> p e c n", c=KC)
        pP = ps("pP", [P, 4, P])
        pV = ps("pV", [P, DM])
        pX = [pP[:, :, :].rearrange("p i n -> p (i n)"), pV[:, :]]
        norm_bank = lambda T: pN[:, T % 4, :].rearrange("p (k n) -> p k n", k=KC)
        norm_in = Norm(nc, ph, "in", S, [(0, NT)], norm_bank, split_rows=mixed)
        norm_out = Norm(nc, ph, "out", S, [(T, T + 2) for T in range(0, NT, 2)], norm_bank)
        small_loaded = sem("small_loaded")
        ctx_loaded = sem("ctx_loaded")
        x_stored = sem("x_stored")
        x_loaded = sem("x_loaded")
        x_biased = sem("x_biased")
        ctx_hi_done = sem("ctx_hi_done")
        ctx_lo_done = sem("ctx_lo_done")
        w_loaded = sem("w_loaded")
        w_hi_done = sem("w_hi_done")
        w_lo_done = sem("w_lo_done")
        mix_step = sem("mix_step")
        proj_done = sem("proj_done")
        bank_read = [sem("bank_read0"), sem("bank_read1")]
        mixed_done = sem("mixed_done")
        mixed_read = sem("mixed_read")
        k_copied = sem("k_copied")
        v_copied = sem("v_copied")
        v_turned = sem("v_turned")
        zeroed = sem("zeroed")
        v_masked = [sem("v_masked0"), sem("v_masked1")]
        q_ready = sem("q_ready")
        k_ready = sem("k_ready")
        scores_done = sem("scores_done")
        top_done = sem("top_done")
        shifted = sem("shifted")
        exp_done = sem("exp_done")
        total_done = sem("total_done")
        inv_done = sem("inv_done")
        prob_ready = sem("prob_ready")
        prob_turned = sem("prob_turned")
        probT_ready = sem("probT_ready")
        av_done = sem("av_done")
        o_hi_done = sem("o_hi_done")
        o_lo_done = sem("o_lo_done")
        out_done = sem("out_done")
        n_small = 6 if mixed else 3
        PAIRS = NT // 2
        AHEAD = 3

        def softmax_rows(ap):
            return ap.unsqueeze(2).broadcast_to([P, 8, SB])

        def half(hf):
            return slice(hf * HALF, (hf + 1) * HALF)

        def split_after(m, c):
            return FILLS * (m - 1) + KC + c + 1

        def loop(engine, body):
            body(0)
            with engine.Fori(1, PAIRS - 1) as i:
                body(i)
            body(PAIRS - 1)

        def is_first(i, e):
            return isinstance(i, int) and i == 0 and e == 0

        def is_last(i, e):
            return isinstance(i, int) and i == PAIRS - 1 and e == 1

        def two_ahead(i):
            return not (isinstance(i, int) and i == PAIRS - 1)

        def wait_whole(engine, m):
            if mixed:
                engine.wait_ge(mixed_read, FILLS * (m + 1))
            else:
                for bank in bank_read:
                    engine.wait_ge(bank, FILLS // 2 * (m + 1))

        def step_ahead(i, e, w, n):
            j = 2 * i + e
            if w + n < W:
                return True, j, e, w + n
            return not is_last(i, e), j + 1, 1 - e, w + n - W

        def masked_v(slot, b, m2):
            width = DM + 2 * D
            rows = Vmask[m2 * SB:(m2 + 1) * SB, slot, b, D * m2:D * m2 + 2 * width]
            to = rows.rearrange("p (pair q) -> p pair q", pair=2)[:, :, 0:DM].rearrange("p pair (k r) -> p pair k r", r=4 * D)
            src = pV[b * SB:(b + 1) * SB, :].rearrange("p (k pair m d) -> p pair k m d", pair=2, m=2, d=D)
            return to[:, :, :, 0:D], src[:, :, :, m2]

        with nc.Block() as block:

            @block.sync
            def _(sp):
                sp.dma_start(QT[:, 0:2, :].rearrange("p a n -> p (a n)"), ctx_half).then_inc(ctx_loaded, 16)
                sp.dma_start(biases[:], d["biases"]).then_inc(small_loaded, 16)
                sp.dma_start(row_mask[:], d["row_mask"]).then_inc(small_loaded, 16)
                sp.dma_start(bo[:], d["bo"].broadcast_to([P, DM])).then_inc(small_loaded, 16)
                if mixed:
                    sp.dma_start(inter[:], d["inter"]).then_inc(small_loaded, 16)
                    sp.dma_start(amp[:], d["amp"].broadcast_to([P, 1])).then_inc(small_loaded, 16)
                    sp.dma_start(same[:], d["same"]).then_inc(small_loaded, 16)

                def load_w(m):
                    sp.wait_ge(w_hi_done, KC * m)
                    sp.wait_ge(w_lo_done, KC * m)
                    sp.dma_start(W_raw.rearrange("p k n -> p (k n)"), d["w"][m]).then_inc(w_loaded, 16)

                load_w(1)
                if mixed:
                    rows = x_dram.rearrange("t (a h b) n -> h t a b n", a=2, h=2)
                    for T in range(NT):
                        sp.wait_ge(norm_in.normed, T + 1)
                        hb, r = divmod(T, 4)
                        for a4 in range(4):
                            sp.dma_start(rows[hb, 2 * r + a4 // 2, a4 % 2], S.x[32 * a4:32 * a4 + 32, T]).then_inc(x_stored, 16)
                load_w(2)
                if mixed:
                    sp.wait_ge(x_stored, 16 * NT * 4)
                    sp.wait_ge(norm_in.turned, NT)
                    for T in range(NT):
                        sp.dma_start(S.x[:, T], x_dram[T]).then_inc(x_loaded, 16)
                load_w(3)
                sp.wait_ge(w_hi_done, 4 * KC)
                sp.wait_ge(w_lo_done, 4 * KC)
                S.prefetch(sp, next_loads)

            @block.tensor
            def _(pe):
                def mix_chunk(n):
                    m, hf, c = n // FILLS, n // KC % 2, n % KC
                    if n == 0:
                        pe.wait_ge(mix_step, 1 + 2 * KC)
                    pe.wait_ge(bank_read[c % 2], n // 2 + 1)
                    wait(pe, mixed_read, n - 1)
                    pe.matmul(pX[n % 2], mix[:, c, :], (KT, VT, QT)[m][:, c, half(hf)],
                              start=True, stop=True, skip_group_check=True).then_inc(mixed_done, 1)

                for m in range(3):
                    hi, lo = (S.xT_hi, S.xT_lo) if m == 2 else (ctx_hi, ctx_lo)
                    for hf in range(2):
                        if m == 0:
                            pe.wait_ge(ctx_lo_done, KC * (hf + 1))
                        if m == 2 and hf == 0:
                            pe.wait_ge(norm_in.x_lo_done, NT)
                        for c in range(KC):
                            if hf == 0:
                                pe.wait_ge(w_hi_done, KC * m + c + 1)
                                pe.wait_ge(w_lo_done, KC * m + c + 1)
                            n = FILLS * m + KC * hf + c
                            wait(pe, bank_read[c % 2], n // 2)
                            for k in range(KC):
                                wk = slice(k * P, (k + 1) * P)
                                mm = three_pass(pe, pM[:, c % 2, :], W_hi[:, c, wk], W_lo[:, c, wk],
                                                hi[:, k, half(hf)], lo[:, k, half(hf)], k == 0, k == KC - 1)
                            mm.then_inc(proj_done, 1)
                            if mixed and n > 0:
                                mix_chunk(n - 1)
                            if m == 1:
                                norm_in.turn(pe, KC * hf + c)

                def turn_v(j):
                    pe.wait_ge(v_copied, j + 1)
                    for b in range(2):
                        wait(pe, v_masked[b], j)
                    for c in range(KC):
                        mm = pe.transpose(pV[:, c * P:(c + 1) * P], Vtile[:, c, :], S.ident[:])
                    mm.then_inc(v_turned, 1)

                def unit(w, i):
                    return w // 2, slice(w // 2 * rows_per_unit, (w // 2 + 1) * rows_per_unit), 2 * (w % 2) + i

                def wait_qk(j):
                    pe.wait_ge(q_ready, j + 1)
                    pe.wait_ge(k_ready, j + 1)

                def scores(j, slot, w):
                    for i in range(2):
                        place, _, c = unit(w, i)
                        for b in range(2):
                            mm = pe.matmul(pS[b * SB:(b + 1) * SB, w % 2, i * 4 * SB:(i + 1) * 4 * SB],
                                           Qunit[:, slot, c, place, b * SB:(b + 1) * SB],
                                           Kmask[:, slot, c, :, b * SB:(b + 1) * SB],
                                           start=True, stop=True, skip_group_check=True)
                    mm.then_inc(scores_done, 1)

                def turn_probs(j, w):
                    n = W * j + w
                    pe.wait_ge(prob_ready, n + 1)
                    wait(pe, probT_ready, n)
                    for i in range(4):
                        mm = pe.transpose(pP[:, i, :], prob[:, w % 4, 2 * i:2 * i + 2, :], S.ident[:])
                    mm.then_inc(prob_turned, 1)

                def attend(j, slot, w):
                    n = W * j + w
                    pe.wait_ge(probT_ready, n + 1)
                    if w == 0:
                        for b in range(2):
                            pe.wait_ge(v_masked[b], j + 1)
                        wait(pe, o_lo_done, j - 1)
                    for i in range(2):
                        _, r, c = unit(w, i)
                        for b in range(2):
                            for pair in range(2):
                                col = pair * DM + c * P
                                mm = pe.matmul(pO[r, slot, c, b * SB:(b + 1) * SB],
                                               Vmask[:, slot, b, col + r.start:col + r.stop],
                                               probT[:, w % 2, 2 * i + pair, b * SB:(b + 1) * SB],
                                               start=pair == 0, stop=pair == 1, skip_group_check=True,
                                               tile_position=(0, r.start))
                    mm.then_inc(av_done, 1)

                if mixed:
                    mix_chunk(3 * FILLS - 1)
                    pe.wait_ge(mixed_read, 3 * FILLS)
                turn_v(0)
                wait_qk(0)
                for w in range(AHEAD):
                    if w == 2:
                        pe.wait_ge(shifted, 1)
                    scores(0, 0, w)

                def body(i):
                    for e in range(2):
                        j = 2 * i + e
                        for w in range(W):
                            exists, nj, slot, nw = step_ahead(i, e, w, AHEAD)
                            if exists:
                                if nw == 0:
                                    wait_qk(nj)
                                pe.wait_ge(shifted, W * j + w + 2)
                                scores(nj, slot, nw)
                            turn_probs(j, w)
                            if w == 1 and not is_last(i, e):
                                turn_v(j + 1)
                            if w > 0:
                                attend(j, e, w - 1)
                            elif not is_first(i, e):
                                attend(j - 1, 1 - e, W - 1)

                loop(pe, body)
                attend(NT - 1, 1, W - 1)
                pe.wait_ge(w_hi_done, 4 * KC)
                pe.wait_ge(w_lo_done, 4 * KC)
                for T in range(NT):
                    if T in (0, NT - 1):
                        pe.wait_ge(o_lo_done, NT - 1 if T == 0 else NT)
                    pe.wait_ge(bank_read[T % 2], LEFT + T // 2)
                    cols = slice(T * P, (T + 1) * P)
                    for c in range(KC):
                        mm = three_pass(pe, pM[:, T % 2, :], S.xT_hi[:, c, cols], S.xT_lo[:, c, cols],
                                        W_hi[:, c, :], W_lo[:, c, :], c == 0, c == KC - 1)
                    mm.then_inc(out_done, 1)
                    for turned in {5: (0, 1), 6: (2, 3), 7: (4, 5, 6, 7)}.get(T, ()):
                        norm_out.turn(pe, turned)

            @block.scalar
            def _(act):
                def split_w(m, c):
                    if m == 0:
                        S.wait_prefetched(act)
                    else:
                        if c == 0:
                            act.wait_ge(w_loaded, 16 * m)
                        act.wait_ge(proj_done, split_after(m, c))
                    nc.scalar.copy(W_hi[:, c], W_raw[:, c]).then_inc(w_hi_done, 1)

                def ctx_high(hf, k):
                    nc.scalar.copy(ctx_hi[:, k, half(hf)], ctx_raw[hf][:, k]).then_inc(ctx_hi_done, 1)

                for k in range(KC):
                    split_w(0, k)
                    ctx_high(0, k)
                act.wait_ge(small_loaded, 16 * n_small)

                def read_mixed(n):
                    m, hf, c = n // FILLS, n // KC % 2, n % KC
                    act.wait_ge(mixed_done, n + 1)
                    nc.scalar.copy((KT, VT, QT)[m][:, c, half(hf)], pX[n % 2]).then_inc(mixed_read, 1)

                for m in range(3):
                    for hf in range(2):
                        for c in range(KC):
                            act.wait_ge(proj_done, FILLS * m + KC * hf + c + 1)
                            if m == 2 and hf == 0 and c == 0:
                                act.wait_ge(ctx_lo_done, 2 * KC)
                            nc.scalar.activation((KT, VT, QT)[m][:, c, half(hf)], pM[:, c % 2, :], ACT.Identity,
                                                 bias=biases[:, m, c:c + 1]).then_inc(bank_read[c % 2], 1)
                            if m == 0 and hf == 0 and c == 1:
                                act.wait_ge(ctx_loaded, 16)
                                for k in range(KC):
                                    ctx_high(1, k)
                            if m == 0 and hf == 0 and c == 3:
                                norm_in.root(act, 0)
                            if m == 1 and KC * hf + c > 0:
                                norm_in.high(act, KC * hf + c - 1)
                            if m == 1 and KC * hf + c == NT - 1:
                                norm_in.high(act, NT - 1)
                            if hf == 1:
                                split_w(m + 1, c)
                            n = FILLS * m + KC * hf + c
                            if mixed and n > 0:
                                read_mixed(n - 1)
                if mixed:
                    read_mixed(3 * FILLS - 1)

                def read_probT(j, w):
                    n = W * j + w
                    act.wait_ge(prob_turned, n + 1)
                    wait(act, av_done, n - 1)
                    nc.scalar.copy(probT[:, w % 2], pP[:, :, :]).then_inc(probT_ready, 1)

                def exponent(j, w):
                    n = W * j + w
                    act.wait_ge(shifted, n + 1)
                    nc.scalar.activation(prob[:, w % 4], prob[:, w % 4], ACT.Exp, scale=scale).then_inc(exp_done, 1)

                def mask_k(j, slot, softmaxes):
                    act.wait_ge(k_copied, j + 1)
                    wait(act, scores_done, W * (j - 1))
                    for m in softmaxes:
                        ins = nc.scalar.activation(Kmask[:, slot, :, m, :], Ktile[:], ACT.Copy, scale=row_mask[:, m:m + 1])
                    if m == 3:
                        ins.then_inc(k_ready, 1)

                def mask_v(j, slot):
                    act.wait_ge(v_turned, j + 1)
                    wait(act, av_done, W * (j - 1))
                    for m2 in range(2):
                        to, src = masked_v(slot, 0, m2)
                        ins = nc.scalar.copy(to, src)
                    ins.then_inc(v_masked[0], 1)

                mask_k(0, 0, range(4))
                exponent(0, 0)
                act.wait_ge(zeroed, 2)
                mask_v(0, 0)
                exponent(0, 1)
                mask_k(1, 1, range(4))
                exponent(0, 2)

                def body(i):
                    for e in range(2):
                        j = 2 * i + e
                        for w in range(W):
                            read_probT(j, w)
                            exists, nj, slot, nw = step_ahead(i, e, w, AHEAD)
                            if exists:
                                exponent(nj, nw)
                            if w == W - 2 and two_ahead(i):
                                mask_k(j + 2, e, (0,))
                            if w == W - 1 and two_ahead(i):
                                mask_k(j + 2, e, (1, 2, 3))
                            if w == 2 and not is_last(i, e):
                                mask_v(j + 1, 1 - e)

                loop(act, body)
                for i in range(PAIRS):
                    norm_out.root(act, i)
                    for T in range(2 * (i - 1), 2 * i):
                        if T >= 0:
                            norm_out.high(act, T)
                for T in range(NT - 2, NT):
                    norm_out.high(act, T)

            @block.vector
            def _(dve):
                def ctx_low(hf):
                    for k in range(KC):
                        dve.wait_ge(ctx_hi_done, KC * hf + k + 1)
                        nc.vector.tensor_tensor(ctx_lo[:, k, half(hf)], ctx_raw[hf][:, k], ctx_hi[:, k, half(hf)].bitcast(F32),
                                                ALU.subtract).then_inc(ctx_lo_done, 1)

                def build_mix():
                    nc.vector.tensor_scalar(inter[:], inter[:], amp[:, 0:1], 0.1, ALU.mult, ALU.mult).then_inc(mix_step, 1)
                    dve.wait_ge(mix_step, 1)
                    for c in range(KC):
                        nc.vector.tensor_tensor(mix[:, c, :].rearrange("p (h j) -> p h j", j=4),
                                                same[:].unsqueeze(2).broadcast_to([P, 32, 4]),
                                                inter[:, c].unsqueeze(1).broadcast_to([P, 32, 4]),
                                                ALU.mult).then_inc(mix_step, 1)
                        dve.wait_ge(mix_step, 2 + 2 * c)
                        nc.vector.tensor_tensor(mix[:, c, :], mix[:, c, :], S.ident[:], ALU.add).then_inc(mix_step, 1)

                ctx_low(0)
                dve.wait_ge(small_loaded, 16 * n_small)
                if mixed:
                    build_mix()
                norm_in.variances(dve, 0)
                ctx_low(1)
                norm_in.scale_rows(dve, 0)
                for T in range(NT):
                    norm_in.low(dve, T)
                def copy_v(j):
                    wait(dve, v_turned, j)
                    nc.vector.tensor_scalar(Vtile[:], VT[:, :, bass.ds(j * P, P)], 1.0, None, ALU.mult).then_inc(v_copied, 1)

                def copy_qk(j, slot):
                    wait(dve, scores_done, W * (j - 1))
                    for place in range(U):
                        r = slice(place * rows_per_unit, (place + 1) * rows_per_unit)
                        ins = nc.vector.tensor_scalar(Qunit[r, slot, :, place], QT[r, :, bass.ds(j * P, P)], 1.0, None, ALU.mult)
                    ins.then_inc(q_ready, 1)
                    wait(dve, k_ready, j)
                    nc.vector.tensor_scalar(Ktile[:], KT[:, :, bass.ds(j * P, P)], 1.0, None, ALU.mult).then_inc(k_copied, 1)

                def mask_v(j, slot):
                    dve.wait_ge(v_turned, j + 1)
                    wait(dve, av_done, W * (j - 1))
                    for m2 in range(2):
                        to, src = masked_v(slot, 1, m2)
                        ins = nc.vector.tensor_copy(to, src)
                    ins.then_inc(v_masked[1], 1)

                def soften(ahead, behind):
                    if ahead is not None:
                        j, w = ahead
                        n = W * j + w
                        bank = pS[:, w % 2, :].rearrange("p (u k) -> p u k", u=8)
                        dve.wait_ge(scores_done, n + 1)
                        nc.vector.tensor_reduce(top[:, w % 4], bank, AX.X, ALU.max).then_inc(top_done, 1)
                    if behind is not None:
                        j2, w2 = behind
                        n2 = W * j2 + w2
                        dve.wait_ge(exp_done, n2 + 1)
                        nc.vector.tensor_reduce(total[:, w2 % 4], prob[:, w2 % 4], AX.X, ALU.add).then_inc(total_done, 1)
                    if ahead is not None:
                        dve.wait_ge(top_done, n + 1)
                        wait(dve, prob_turned, n - 3)
                        nc.vector.tensor_tensor(prob[:, w % 4], bank, softmax_rows(top[:, w % 4]),
                                                ALU.subtract).then_inc(shifted, 1)
                    if behind is not None:
                        dve.wait_ge(total_done, n2 + 1)
                        wait(dve, prob_ready, n2 - 3)
                        nc.vector.reciprocal(inv[:, w2 % 4], total[:, w2 % 4]).then_inc(inv_done, 1)

                def read_o(j, slot):
                    dve.wait_ge(av_done, W * (j + 1))
                    nc.vector.tensor_scalar(S.xT_hi[:, :, bass.ds(j * P, P)], pO[:, slot], 1.0, None, ALU.mult).then_inc(o_hi_done, 1)
                    dve.wait_ge(o_hi_done, j + 1)
                    nc.vector.tensor_tensor(S.xT_lo[:, :, bass.ds(j * P, P)], pO[:, slot],
                                            S.xT_hi[:, :, bass.ds(j * P, P)].bitcast(F32), ALU.subtract).then_inc(o_lo_done, 1)

                wait_whole(dve, 1)
                copy_v(0)
                wait_whole(dve, 2)
                dve.wait_ge(zeroed, 2)
                copy_qk(0, 0)
                soften((0, 0), None)
                copy_qk(1, 1)
                soften((0, 1), (0, 0))
                mask_v(0, 0)
                soften((0, 2), (0, 1))
                dve.wait_ge(proj_done, 3 * FILLS)

                def body(i):
                    for e in range(2):
                        j = 2 * i + e
                        for w in range(W):
                            steps = [step_ahead(i, e, w, n) for n in (AHEAD, AHEAD - 1)]
                            soften(*[(nj, nw) if exists else None for exists, nj, _, nw in steps])
                            if w == 0 and not is_last(i, e):
                                copy_v(j + 1)
                            if w == W - 3 and two_ahead(i):
                                copy_qk(j + 2, e)
                            if w == 2 and not is_first(i, e):
                                read_o(j - 1, 1 - e)
                            if w == 3 and not is_last(i, e):
                                mask_v(j + 1, 1 - e)

                loop(dve, body)
                read_o(NT - 1, 1)
                for T in range(NT + 2):
                    if T < NT:
                        dve.wait_ge(out_done, T + 1)
                        dve.wait_ge(x_biased, T + 1)
                        nc.vector.tensor_tensor(S.x[:, T], pM[:, T % 2, :], S.x[:, T], ALU.add).then_inc(bank_read[T % 2], 1)
                        dve.wait_ge(bank_read[T % 2], LEFT + T // 2 + 1)
                    if T % 2 == 1 and T < NT:
                        norm_out.variances(dve, T // 2)
                    if T % 2 == 0 and T >= 2:
                        norm_out.scale_rows(dve, T // 2 - 1)
                    if T >= 6:
                        for low in range(2 * (T - 6), 2 * (T - 5)):
                            norm_out.low(dve, low)
                        
            @block.gpsimd
            def _(pool):
                def split_w(m, c):
                    pool.wait_ge(w_hi_done, KC * m + c + 1)
                    if m > 0:
                        pool.wait_ge(proj_done, split_after(m, c))
                    nc.gpsimd.tensor_tensor(W_lo[:, c], W_raw[:, c], W_hi[:, c].bitcast(F32),
                                            ALU.subtract).then_inc(w_lo_done, 1)

                for c in range(KC):
                    split_w(0, c)
                nc.gpsimd.memset(Qunit[:], 0.0).then_inc(zeroed, 1)
                for m in range(1, 3):
                    for c in range(KC):
                        split_w(m, c)
                pool.wait_ge(proj_done, 2 * FILLS)
                nc.gpsimd.memset(Vmask[:], 0.0).then_inc(zeroed, 1)
                pool.wait_ge(small_loaded, 16 * n_small)
                if mixed:
                    pool.wait_ge(x_loaded, 16 * NT)
                else:
                    pool.wait_ge(norm_in.turned, NT)
                for T in range(NT):
                    nc.gpsimd.tensor_tensor(S.x[:, T], S.x[:, T], bo[:], ALU.add).then_inc(x_biased, 1)
                for c in range(KC):
                    split_w(3, c)

                def divide(j, w):
                    n = W * j + w
                    pool.wait_ge(inv_done, n + 1)
                    nc.gpsimd.tensor_tensor(prob[:, w % 4], prob[:, w % 4], softmax_rows(inv[:, w % 4]),
                                            ALU.mult).then_inc(prob_ready, 1)

                divide(0, 0)
                divide(0, 1)

                def body(i):
                    for e in range(2):
                        for w in range(W):
                            exists, nj, slot, nw = step_ahead(i, e, w, AHEAD - 1)
                            if exists:
                                divide(nj, nw)

                loop(pool, body)
        ph.close()


def lora_phase(nc, name, S, d, next_loads):
    E, R = 8, 16
    S.begin_phase()
    with ExitStack() as ctx:
        ph = Phase(nc, ctx, name)
        sb, ps, sem = ph.sb, ph.ps, ph.sem
        raw = S.raw[:, 0:7 * DM].rearrange("p (k n) -> p k n", k=7)
        w_hi = sb("w_hi", [P, 7, DM], F32R)
        w_lo = sb("w_lo", [P, 7, DM], F32R)
        A, ROUTER, B, BASE = 0, 1, 2, 3
        base_bias = sb("base_bias", [P, DM])
        router_bias = sb("router_bias", [P, 1])
        inv_k = sb("inv_k", [P, E])
        hT = sb("hT", [P, TOK])
        gT = sb("gT", [P, TOK])
        z = sb("z", [P, NT, E])
        top = sb("top", [P, NT, E])
        run = sb("run", [P, NT, E])
        tau = sb("tau", [P, NT])
        weight = sb("weight", [P, NT, E, R])
        hw = sb("hw", [P, TOK])
        hw_hi = sb("hw_hi", [P, TOK], F32R)
        hw_lo = sb("hw_lo", [P, TOK], F32R)
        banks = ps("banks", [P, 4, DM])
        pA = banks[:, 0:2, :]
        pL = banks[:, 2:4, :].rearrange("p a (t n) -> p (a t) n", n=P)
        pB = ps("pB", [P, 4, DM])
        names = ("small_loaded", "w_hi_done", "w_lo_done", "x_biased", "proj_done", "h_read", "logits_turned",
                 "z_done", "sorted_done", "step", "weight_turned", "hw_done", "hw_hi_done", "hw_lo_done", "out_done", "summed")
        (small_loaded, w_hi_done, w_lo_done, x_biased, proj_done, h_read, logits_turned,
         z_done, sorted_done, step, weight_turned, hw_done, hw_hi_done, hw_lo_done, out_done, summed) = map(sem, names)
        norm = Norm(nc, ph, "out", S, [(T, T + 2) for T in range(0, NT, 2)],
                    lambda T: banks[:, T % 4, :].rearrange("p (k n) -> p k n", k=KC))

        with nc.Block() as block:

            @block.sync
            def _(sp):
                sp.dma_start(base_bias[:], d["base_bias"].broadcast_to([P, DM])).then_inc(small_loaded, 16)
                sp.dma_start(router_bias[:], d["router_bias"]).then_inc(small_loaded, 16)
                sp.dma_start(inv_k[:], d["inv_k"].broadcast_to([P, E])).then_inc(small_loaded, 16)
                sp.wait_ge(w_hi_done, 7)
                sp.wait_ge(w_lo_done, 7)
                S.prefetch(sp, next_loads)

            @block.tensor
            def _(pe):
                for i, w in enumerate((ROUTER, A)):
                    for hf in range(2):
                        pe.wait_ge(w_lo_done, 2)
                        if i == 1:
                            pe.wait_ge(h_read, hf + 1)
                        tok = slice(hf * HALF, (hf + 1) * HALF)
                        for k in range(KC):
                            wk = slice(k * P, (k + 1) * P)
                            mm = three_pass(pe, pA[:, hf, :], w_hi[:, w, wk], w_lo[:, w, wk],
                                            S.xT_hi[:, k, tok], S.xT_lo[:, k, tok], k == 0, k == KC - 1)
                        mm.then_inc(proj_done, 1)
                pe.wait_ge(h_read, 2)
                for T in range(NT):
                    mm = pe.transpose(pL[:, T, :], gT[:, T * P:(T + 1) * P], S.ident[:])
                mm.then_inc(logits_turned, 1)

                def base(T):
                    wait(pe, summed, T - 3)
                    cols = slice(T * P, (T + 1) * P)
                    for k in range(KC):
                        pe.wait_ge(w_lo_done, BASE + k + 1)
                        three_pass(pe, pB[:, T % 4, :], S.xT_hi[:, k, cols], S.xT_lo[:, k, cols],
                                   w_hi[:, BASE + k, :], w_lo[:, BASE + k, :], k == 0, False)

                def lora(T):
                    if T % 4 == 0:
                        pe.wait_ge(hw_lo_done, T // 4 + 1)
                    cols = slice(T * P, (T + 1) * P)
                    three_pass(pe, pB[:, T % 4, :], hw_hi[:, cols], hw_lo[:, cols], w_hi[:, B, :], w_lo[:, B, :],
                               False, True).then_inc(out_done, 1)

                for T in range(4):
                    base(T)
                pe.wait_ge(step, E + 4)
                for T in range(NT):
                    mm = pe.transpose(pL[:, T, :], weight[:, T].rearrange("p e r -> p (e r)"), S.ident[:])
                mm.then_inc(weight_turned, 1)
                for T in range(4):
                    lora(T)
                for T in range(4, NT):
                    base(T)
                    lora(T)
                    for turned in {5: (0, 1), 6: (2, 3), 7: (4, 5, 6, 7)}.get(T, ()):
                        norm.turn(pe, turned)

            @block.scalar
            def _(act):
                S.wait_prefetched(act)
                for i in (ROUTER, A, B, BASE, BASE + 1, BASE + 2, BASE + 3):
                    nc.scalar.copy(w_hi[:, i], raw[:, i]).then_inc(w_hi_done, 1)
                act.wait_ge(small_loaded, 48)
                for hf in range(2):
                    act.wait_ge(proj_done, hf + 1)
                    nc.scalar.activation(gT[:, hf * HALF:(hf + 1) * HALF], pA[:, hf, :], ACT.Identity,
                                         bias=router_bias[:, 0:1]).then_inc(h_read, 1)
                for hf in range(2):
                    act.wait_ge(proj_done, 3 + hf)
                    nc.scalar.copy(hT[:, hf * HALF:(hf + 1) * HALF], pA[:, hf, :]).then_inc(h_read, 1)
                for hf in range(2):
                    act.wait_ge(hw_done, hf + 1)
                    nc.scalar.copy(hw_hi[:, hf * HALF:(hf + 1) * HALF], hw[:, hf * HALF:(hf + 1) * HALF]).then_inc(hw_hi_done, 1)
                for i in range(NT // 2):
                    norm.root(act, i)
                    if i > 0:
                        norm.high(act, 2 * i - 2)
                        norm.high(act, 2 * i - 1)
                for T in range(NT - 2, NT):
                    norm.high(act, T)

            @block.vector
            def _(dve):
                dve.wait_ge(small_loaded, 48)
                dve.wait_ge(logits_turned, 1)
                nc.vector.tensor_copy(z[:], pL[:, :, :].rearrange("p t (e r) -> p t e r", r=R)[:, :, :, 0]).then_inc(z_done, 1)
                dve.wait_ge(z_done, 1)
                for T in range(NT):
                    nc.vector.max(top[:, T], z[:, T]).then_inc(sorted_done, 1)
                dve.wait_ge(sorted_done, NT)

                def link(n, instruction):
                    instruction.then_inc(step, 1)
                    dve.wait_ge(step, n)

                link(1, nc.vector.tensor_scalar(run[:, :, 0:1], top[:, :, 0:1], -1.0, None, ALU.add))
                for k in range(1, E):
                    link(k + 1, nc.vector.tensor_tensor(run[:, :, k:k + 1], run[:, :, k - 1:k], top[:, :, k:k + 1], ALU.add))
                link(E + 1, nc.vector.tensor_tensor(run[:], run[:], inv_k[:].unsqueeze(1).broadcast_to([P, NT, E]), ALU.mult))
                link(E + 2, nc.vector.tensor_reduce(tau[:], run[:], AX.X, ALU.max))
                link(E + 3, nc.vector.tensor_tensor(z[:], z[:], tau[:].unsqueeze(2).broadcast_to([P, NT, E]), ALU.subtract))
                link(E + 4, nc.vector.tensor_scalar(weight[:], z[:].unsqueeze(3).broadcast_to([P, NT, E, R]), 0.0, None, ALU.max))
                dve.wait_ge(h_read, 4)
                dve.wait_ge(weight_turned, 1)
                for hf in range(2):
                    tok = slice(hf * HALF, (hf + 1) * HALF)
                    nc.vector.tensor_tensor(hw[:, tok], hT[:, tok], pL[:, 4 * hf:4 * hf + 4, :].rearrange("p t n -> p (t n)"),
                                            ALU.mult).then_inc(hw_done, 1)
                for hf in range(2):
                    tok = slice(hf * HALF, (hf + 1) * HALF)
                    dve.wait_ge(hw_hi_done, hf + 1)
                    nc.vector.tensor_tensor(hw_lo[:, tok], hw[:, tok], hw_hi[:, tok].bitcast(F32),
                                            ALU.subtract).then_inc(hw_lo_done, 1)
                for T in range(NT + 2):
                    if T < NT:
                        dve.wait_ge(out_done, T + 1)
                        dve.wait_ge(x_biased, T + 1)
                        nc.vector.tensor_tensor(S.x[:, T], pB[:, T % 4, :], S.x[:, T], ALU.add).then_inc(summed, 1)
                        dve.wait_ge(summed, T + 1)
                    if T % 2 == 1 and T < NT:
                        norm.variances(dve, T // 2)
                    if T % 2 == 0 and T >= 2:
                        norm.scale_rows(dve, T // 2 - 1)
                    if T >= 6:
                        for low in range(2 * (T - 6), 2 * (T - 5)):
                            norm.low(dve, low)

            @block.gpsimd
            def _(pool):
                for n, i in enumerate((ROUTER, A, B, BASE, BASE + 1, BASE + 2, BASE + 3)):
                    pool.wait_ge(w_hi_done, n + 1)
                    nc.gpsimd.tensor_tensor(w_lo[:, i], raw[:, i], w_hi[:, i].bitcast(F32), ALU.subtract).then_inc(w_lo_done, 1)
                pool.wait_ge(small_loaded, 48)
                for T in range(NT):
                    nc.gpsimd.tensor_tensor(S.x[:, T], S.x[:, T], base_bias[:], ALU.add).then_inc(x_biased, 1)
        ph.close()


def experts_phase(nc, name, S, d, out):
    E, G, X = 16, 4, 18
    S.begin_phase()
    with ExitStack() as ctx:
        ph = Phase(nc, ctx, name)
        sb, ps, sem = ph.sb, ph.ps, ph.sem
        raw = S.raw[:, 0:2 * EW].rearrange("p (s n) -> p s n", s=2)
        w12_hi = sb("w12_hi", [P, 2, 2 * DM], F32R)
        w12_lo = sb("w12_lo", [P, 2, 2 * DM], F32R)
        w3_hi = sb("w3_hi", [P, 2, DM], F32R)
        w3_lo = sb("w3_lo", [P, 2, DM], F32R)
        r_raw = sb("r_raw", [P, DM])
        r_hi = sb("r_hi", [P, DM], F32R)
        r_lo = sb("r_lo", [P, DM], F32R)
        r_bias = sb("r_bias", [P, 1])
        s_bias = sb("s_bias", [P, E])
        before = sb("before", [P, E, E])
        b3 = sb("b3", [X, DM])
        gT = sb("gT", [P, TOK])
        score = sb("score", [P, NT, E])
        masked = sb("masked", [P, NT, E])
        stat = sb("stat", [P, NT])
        gmax = sb("gmax", [P, NT, G])
        keep = sb("keep", [P, NT, G])
        cmp = sb("cmp", [P, NT, E, E])
        same = sb("same", [P, NT, E, E])
        rank = sb("rank", [P, NT, E])
        gate = sb("gate", [P, NT, X])
        gateT = sb("gateT", [X, TOK])
        act_out = sb("act_out", [P, 2, HALF])
        hid = sb("hid", [P, 2, HALF])
        hid_hi = sb("hid_hi", [P, 2, 2, HALF], F32R)
        hid_lo = sb("hid_lo", [P, 2, 2, HALF], F32R)
        pH = ps("pH", [P, 2, 2, HALF])
        pY = ps("pY", [P, 4, DM])
        names = ("small_loaded", "r_hi_done", "r_lo_done", "r_done", "r_read", "r_turned", "step", "exp_done", "gate_set",
                 "gate_turned", "gateT_read", "b3_done", "w12_hi_done", "w12_lo_done", "w3_hi_done", "w3_lo_done",
                 "hid_done", "silu_done", "hid_ready", "hid_hi_done", "hid_lo_done", "y_done", "summed")
        (small_loaded, r_hi_done, r_lo_done, r_done, r_read, r_turned, step, exp_done, gate_set,
         gate_turned, gateT_read, b3_done, w12_hi_done, w12_lo_done, w3_hi_done, w3_lo_done,
         hid_done, silu_done, hid_ready, hid_hi_done, hid_lo_done, y_done, summed) = map(sem, names)
        w_loaded = [sem(f"w_loaded{i}") for i in range(2)]
        stored = sem("stored")
        norm = Norm(nc, ph, "out", S, [(0, 4), (4, 6), (6, 8)])
        STEPS = 18

        def bcast(ap, dim, n):
            shape = list(ap.shape)
            shape.insert(dim, n)
            return ap.unsqueeze(dim).broadcast_to(shape)

        def loop(engine, body):
            body(0)
            with engine.Fori(1, X // 2 - 1) as i:
                body(i)
            body(X // 2 - 1)

        def exists(i, e2, ahead):
            return not (isinstance(i, int) and 2 * i + e2 + ahead >= X)

        with nc.Block() as block:

            @block.sync
            def _(sp):
                for dst, src in ((r_raw, d["r_w"]), (r_bias, d["r_bias"]), (s_bias, d["s_bias"].broadcast_to([P, E])),
                                 (before, d["before"].broadcast_to([P, E * E])), (b3, d["b3"])):
                    to = dst[:].rearrange("p i j -> p (i j)") if dst is before else dst[:]
                    sp.dma_start(to, src).then_inc(small_loaded, 16)

                def body(i):
                    for e2 in range(2):
                        e = 2 * i + e2
                        sp.wait_ge(hid_ready, 2 * (e - 1))
                        sp.wait_ge(w3_hi_done, e - 1)
                        sp.wait_ge(w3_lo_done, e - 1)
                        sp.dma_start(raw[:, e2], d["w"][e]).then_inc(w_loaded[e2], 16)

                with sp.Fori(1, X // 2) as i:
                    body(i)
                for T in range(NT):
                    sp.wait_ge(norm.normed, T + 1)
                    sp.dma_start(out[T], S.x[:, T]).then_inc(stored, 16)
                sp.wait_ge(stored, 16 * NT)

            @block.tensor
            def _(pe):
                pe.wait_ge(r_hi_done, 1)
                pe.wait_ge(r_lo_done, 1)
                for hf in range(2):
                    tok = slice(hf * HALF, (hf + 1) * HALF)
                    for k in range(KC):
                        wk = slice(k * P, (k + 1) * P)
                        mm = three_pass(pe, pY[:, hf, :], r_hi[:, wk], r_lo[:, wk],
                                        S.xT_hi[:, k, tok], S.xT_lo[:, k, tok], k == 0, k == KC - 1)
                    mm.then_inc(r_done, 1)
                pe.wait_ge(r_read, 2)
                for T in range(NT):
                    mm = pe.transpose(pY[:, 2 + T // 4, (T % 4) * P:(T % 4 + 1) * P], gT[:, T * P:(T + 1) * P], S.ident[:])
                mm.then_inc(r_turned, 1)

                def hidden(e, slot, hf):
                    if hf == 0:
                        pe.wait_ge(w12_hi_done, e + 1)
                        pe.wait_ge(w12_lo_done, e + 1)
                    wait(pe, silu_done, 2 * e - 1 + hf)
                    wait(pe, hid_ready, 2 * e - 1 + hf)
                    tok = slice(hf * HALF, (hf + 1) * HALF)
                    for m in range(2):
                        for k in range(KC):
                            wk = slice(m * DM + k * P, m * DM + (k + 1) * P)
                            mm = three_pass(pe, pH[:, m, hf, :], w12_hi[:, slot, wk], w12_lo[:, slot, wk],
                                            S.xT_hi[:, k, tok], S.xT_lo[:, k, tok], k == 0, k == KC - 1)
                    mm.then_inc(hid_done, 1)

                def output(e, slot, hf):
                    pe.wait_ge(hid_lo_done, 2 * e + hf + 1)
                    if hf == 0:
                        pe.wait_ge(w3_hi_done, e + 1)
                        pe.wait_ge(w3_lo_done, e + 1)
                    for t in range(4):
                        wait(pe, summed, 8 * (e + 1) + 4 * hf + t - 3)
                        cols = slice(t * P, (t + 1) * P)
                        three_pass(pe, pY[:, t, :], hid_hi[:, slot, hf, cols], hid_lo[:, slot, hf, cols],
                                   w3_hi[:, slot, :], w3_lo[:, slot, :], True, True).then_inc(y_done, 1)

                for hf in range(2):
                    hidden(0, 0, hf)
                pe.wait_ge(step, STEPS)
                for T in range(NT):
                    bank = pY[0:X, T // 4, (T % 4) * P:(T % 4 + 1) * P]
                    mm = pe.transpose(bank, gate[:, T, :], S.ident[:])
                mm.then_inc(gate_turned, 1)
                pe.wait_ge(gateT_read, 1)
                for T in range(NT):
                    wait(pe, summed, T - 3)
                    pe.matmul(pY[:, T % 4, :], gateT[:, T * P:(T + 1) * P], b3[:, :],
                              start=True, stop=True, skip_group_check=True).then_inc(b3_done, 1)

                def body(i):
                    for e2 in range(2):
                        e = 2 * i + e2
                        for hf in range(2):
                            if exists(i, e2, 1):
                                hidden(e + 1, 1 - e2, hf)
                            output(e, e2, hf)

                loop(pe, body)

            @block.scalar
            def _(act):
                act.wait_ge(small_loaded, 80)
                nc.scalar.copy(r_hi[:], r_raw[:]).then_inc(r_hi_done, 1)

                def split(e, slot, i, n12):
                    if isinstance(i, int) and i == 0:
                        S.wait_prefetched(act)
                    else:
                        act.wait_ge(w_loaded[slot], 16 * i)
                    if n12:
                        wait(act, hid_done, 2 * (e - 1))
                        nc.scalar.copy(w12_hi[:, slot], raw[:, slot, 0:2 * DM]).then_inc(w12_hi_done, 1)
                    else:
                        wait(act, y_done, 8 * (e - 1))
                        nc.scalar.copy(w3_hi[:, slot], raw[:, slot, 2 * DM:3 * DM]).then_inc(w3_hi_done, 1)

                def silu(e, slot, hf):
                    act.wait_ge(hid_done, 2 * e + hf + 1)
                    wait(act, hid_ready, 2 * e - 1 + hf)
                    nc.scalar.activation(act_out[:, hf], pH[:, 0, hf, :], ACT.Silu,
                                         bias=raw[:, slot, 3 * DM:3 * DM + 1]).then_inc(silu_done, 1)

                def high(e, slot, hf):
                    act.wait_ge(hid_ready, 2 * e + hf + 1)
                    wait(act, y_done, 8 * (e - 1))
                    nc.scalar.copy(hid_hi[:, slot, hf], hid[:, hf]).then_inc(hid_hi_done, 1)

                split(0, 0, 0, True)
                for hf in range(2):
                    act.wait_ge(r_done, hf + 1)
                    nc.scalar.activation(gT[:, hf * HALF:(hf + 1) * HALF], pY[:, hf, :], ACT.Identity,
                                         bias=r_bias[:, 0:1]).then_inc(r_read, 1)
                split(1, 1, 0, True)
                split(0, 0, 0, False)
                act.wait_ge(step, 2)
                nc.scalar.activation(score[:], score[:], ACT.Exp).then_inc(exp_done, 1)
                for hf in range(2):
                    silu(0, 0, hf)
                    high(0, 0, hf)
                act.wait_ge(gate_turned, 1)
                nc.scalar.copy(gateT[:], pY[0:X, 0:2, :].rearrange("p t n -> p (t n)")).then_inc(gateT_read, 1)

                def body(i):
                    for e2 in range(2):
                        e = 2 * i + e2
                        if exists(i, e2, 1):
                            split(e + 1, 1 - e2, i + e2, False)
                            silu(e + 1, 1 - e2, 0)
                            high(e + 1, 1 - e2, 0)
                        if exists(i, e2, 2):
                            split(e + 2, e2, i + 1, True)
                        if exists(i, e2, 1):
                            silu(e + 1, 1 - e2, 1)
                            high(e + 1, 1 - e2, 1)

                loop(act, body)
                for i in range(len(norm.groups)):
                    norm.root(act, i)

            @block.vector
            def _(dve):
                dve.wait_ge(small_loaded, 80)

                def link(n, instruction):
                    instruction.then_inc(step, 1)
                    dve.wait_ge(step, n)

                def hidden_product(e, slot, hf):
                    dve.wait_ge(silu_done, 2 * e + hf + 1)
                    wait(dve, hid_lo_done, 2 * e - 1 + hf)
                    nc.vector.scalar_tensor_tensor(out=hid[:, hf], in0=pH[:, 1, hf, :], scalar=raw[:, slot, 3 * DM + 1:3 * DM + 2],
                                                   in1=act_out[:, hf], op0=ALU.add, op1=ALU.mult).then_inc(hid_ready, 1)

                def low(e, slot, hf):
                    dve.wait_ge(hid_hi_done, 2 * e + hf + 1)
                    nc.vector.tensor_tensor(hid_lo[:, slot, hf], hid[:, hf], hid_hi[:, slot, hf].bitcast(F32),
                                            ALU.subtract).then_inc(hid_lo_done, 1)

                def add_output(e, hf):
                    for t in range(4):
                        T = 4 * hf + t
                        dve.wait_ge(y_done, 8 * e + T + 1)
                        dve.wait_ge(summed, 8 * e + T + 1)
                        nc.vector.scalar_tensor_tensor(out=S.x[:, T], in0=pY[:, t, :], scalar=gate[:, T, bass.ds(e, 1)],
                                                       in1=S.x[:, T], op0=ALU.mult, op1=ALU.add).then_inc(summed, 1)

                dve.wait_ge(r_turned, 1)
                logits = pY[:, 2:4, :].rearrange("p a (t e r) -> p (a t) e r", t=4, r=P // E)[:, :, :, 0]
                link(1, nc.vector.tensor_reduce(stat[:], logits, AX.X, ALU.max))
                link(2, nc.vector.tensor_tensor(score[:], logits, bcast(stat[:], 2, E), ALU.subtract))
                dve.wait_ge(exp_done, 1)
                link(3, nc.vector.tensor_reduce(stat[:], score[:], AX.X, ALU.add))
                link(4, nc.vector.reciprocal(stat[:], stat[:]))
                link(5, nc.vector.tensor_tensor(score[:], score[:], bcast(stat[:], 2, E), ALU.mult))
                link(6, nc.vector.tensor_tensor(score[:], score[:], bcast(s_bias[:], 1, NT), ALU.add))

                def ranks(n, values, m, out):
                    c, s = cmp[:, :, 0:m, 0:m], same[:, :, 0:m, 0:m]
                    mine, other = bcast(values, 3, m), bcast(values, 2, m)
                    nc.vector.tensor_tensor(c, other, mine, ALU.is_gt)
                    link(n, nc.vector.tensor_tensor(s, other, mine, ALU.is_equal))
                    link(n + 1, nc.vector.tensor_tensor(s, s, bcast(before[:, 0:m, 0:m], 1, NT), ALU.mult))
                    link(n + 2, nc.vector.tensor_tensor(c, c, s, ALU.add))
                    link(n + 3, nc.vector.tensor_reduce(out, c, AX.X, ALU.add))

                link(7, nc.vector.tensor_reduce(gmax[:], score[:].rearrange("p t (g i) -> p t g i", g=G), AX.X, ALU.max))
                ranks(8, gmax[:], G, keep[:])
                link(12, nc.vector.tensor_scalar(keep[:], keep[:], 1.5, None, ALU.is_lt))
                grouped = lambda a: a[:].rearrange("p t (g i) -> p t g i", g=G)
                nc.vector.tensor_tensor(grouped(masked), grouped(score), bcast(keep[:], 3, G), ALU.mult)
                link(13, nc.vector.tensor_scalar(gmax[:], keep[:], -MASKED, MASKED, ALU.mult, ALU.add))
                nc.vector.tensor_tensor(grouped(masked), grouped(masked), bcast(gmax[:], 3, G), ALU.add).then_inc(gate_set, 1)
                dve.wait_ge(gate_set, 1)
                ranks(14, masked[:], E, rank[:])
                nc.vector.memset(gate[:, :, 0:2], 1.0)
                nc.vector.scalar_tensor_tensor(out=gate[:, :, 2:X], in0=rank[:], scalar=1.5, in1=score[:],
                                               op0=ALU.is_lt, op1=ALU.mult).then_inc(step, 1)
                for hf in range(2):
                    hidden_product(0, 0, hf)
                    low(0, 0, hf)
                for T in range(NT):
                    dve.wait_ge(b3_done, T + 1)
                    nc.vector.tensor_tensor(S.x[:, T], pY[:, T % 4, :], S.x[:, T], ALU.add).then_inc(summed, 1)

                def body(i):
                    for e2 in range(2):
                        e = 2 * i + e2
                        for hf in range(2):
                            if exists(i, e2, 1):
                                hidden_product(e + 1, 1 - e2, hf)
                                low(e + 1, 1 - e2, hf)
                            add_output(e, hf)
                            if isinstance(e, int) and e == X - 1:
                                if hf == 0:
                                    dve.wait_ge(summed, 8 * X + 4)
                                    norm.variances(dve, 0)
                                    norm.scale_rows(dve, 0)

                loop(dve, body)
                dve.wait_ge(summed, 8 * X + 8)
                for i in (1, 2):
                    norm.variances(dve, i)
                    norm.scale_rows(dve, i)

            @block.gpsimd
            def _(pool):
                pool.wait_ge(r_hi_done, 1)
                nc.gpsimd.tensor_tensor(r_lo[:], r_raw[:], r_hi[:].bitcast(F32), ALU.subtract).then_inc(r_lo_done, 1)

                def split(e, slot, n12):
                    if n12:
                        pool.wait_ge(w12_hi_done, e + 1)
                        wait(pool, hid_done, 2 * (e - 1))
                        nc.gpsimd.tensor_tensor(w12_lo[:, slot], raw[:, slot, 0:2 * DM], w12_hi[:, slot].bitcast(F32),
                                                ALU.subtract).then_inc(w12_lo_done, 1)
                    else:
                        pool.wait_ge(w3_hi_done, e + 1)
                        wait(pool, y_done, 8 * (e - 1))
                        nc.gpsimd.tensor_tensor(w3_lo[:, slot], raw[:, slot, 2 * DM:3 * DM], w3_hi[:, slot].bitcast(F32),
                                                ALU.subtract).then_inc(w3_lo_done, 1)

                split(0, 0, True)
                split(1, 1, True)
                split(0, 0, False)

                def body(i):
                    for e2 in range(2):
                        e = 2 * i + e2
                        if exists(i, e2, 1):
                            split(e + 1, 1 - e2, False)
                        if exists(i, e2, 2):
                            split(e + 2, e2, True)

                loop(pool, body)
        ph.close()


def decoder(nc, d, out):
    with ExitStack() as ctx:
        S = State(nc, ctx)
        run_phases(nc, d, out, S)


def run_phases(nc, d, out, S):
    scratch = nc.dram_tensor("x_natural", (NT, P, DM), F32).ap()
    sub = lambda prefix: {k[len(prefix):]: v for k, v in d.items() if k.startswith(prefix)}
    attention_first = lambda layer: [(S.raw[:, 0:CH * DM], d[f"l{layer}_wqkv"][0]),
                                     (S.raw[:, CH * DM:(CH + QPG) * DM], d[f"l{layer}_wo"][0])]
    cross_first = lambda layer: [(S.raw[:, 0:KC * DM], d[f"x{layer}_w"][0]),
                                 (S.raw[:, KC * DM:2 * KC * DM], d["ctxT"][0])]
    lora_first = [(S.raw[:, 0:7 * DM], d["f0_w"])]
    experts_first = [(S.raw[:, e * EW:(e + 1) * EW], d["f1_w"][e]) for e in range(2)]
    steps = [
        lambda: attention_phase(nc, "l0a", S, d["l0_wqkv"], d["l0_wo"], d["mask0"], True, cross_first(0),
                                xT_raw_dram=d["xT_perm"], x_rows_dram=d["x_rows"], ident_dram=d["ident"]),
        lambda: cross_attention_phase(nc, "l0x", S, sub("x0_"), 32, d["ctxT"][1], lora_first, scratch),
        lambda: lora_phase(nc, "l0f", S, sub("f0_"), attention_first(1)),
        lambda: attention_phase(nc, "l1a", S, d["l1_wqkv"], d["l1_wo"], d["mask1"], False, cross_first(1),
                                rope_dram=d["rope"]),
        lambda: cross_attention_phase(nc, "l1x", S, sub("x1_"), 64, d["ctxT"][1], experts_first),
        lambda: experts_phase(nc, "l1f", S, sub("f1_"), out),
    ]
    for step in steps:
        step()


def _rows(a):
    return a.reshape(4, 4, 2, 32, -1).transpose(2, 0, 1, 3, 4).reshape(NT, P, -1)


def _k_major(w):
    K, n = w.shape
    return w.reshape(K // P, P, n).transpose(1, 0, 2).reshape(P, -1)


def _group_weights(w):
    return w.reshape(GROUPS, CH, P, KC, P).transpose(0, 4, 1, 3, 2).reshape(GROUPS, P, -1)


def _out_weights(w):
    return w.reshape(DM, GROUPS, QPG, HD).transpose(1, 3, 2, 0).reshape(GROUPS, P, -1)


def _constants():
    bf = np.dtype("bfloat16")
    i = np.arange(P)
    causal = i[:, None] >= i[None, :]
    mask0 = causal & (i[:, None] // SEQ_A == i[None, :] // SEQ_A)
    mask1 = causal & (i[:, None] // SEQ_B == i[None, :] // SEQ_B)
    inv = 1.0 / 500000.0 ** (np.arange(0, HD, 2, dtype=np.float32) / HD)
    wavelen = 2.0 * np.pi / inv
    low, high = 1024 / 1.0, 1024 / 4.0
    scaled = np.where(wavelen > low, inv / 8.0, inv)
    smooth = (1024 / wavelen - 1.0) / (4.0 - 1.0)
    smoothed = (1.0 - smooth) / 8.0 * inv + smooth * inv
    freq = np.where((wavelen <= low) & (wavelen >= high), smoothed, scaled).astype(np.float32)
    angle = (np.arange(SEQ_B, dtype=np.float32)[None, :] * np.concatenate([freq, freq])[:, None]).astype(np.float32)
    sign = np.where(i[:, None] < HD // 2, 1.0, -1.0)
    rope = np.stack([np.cos(angle.astype(np.float64)), sign * np.sin(angle.astype(np.float64))]).astype(np.float32)
    return {
        "ident": np.eye(P, dtype=np.float32),
        "mask0": np.where(mask0, 0.0, MASKED).astype(np.float32).astype(bf),
        "mask1": np.where(mask1, 0.0, MASKED).astype(np.float32).astype(bf),
        "rope": rope,
        "f0_inv_k": (1.0 / np.arange(1, 9, dtype=np.float32)).reshape(1, 8),
        "f1_before": (np.arange(16)[:, None] > np.arange(16)[None, :]).astype(np.float32).reshape(1, 256),
        "x0_row_mask": (i[:, None] % 4 == np.arange(4)).astype(np.float32),
        "x1_row_mask": (i[:, None] // 16 % 4 == np.arange(4)).astype(np.float32),
        "x0_same": (i[:, None] // 4 == np.arange(32)).astype(np.float32),
    }


def _lay_out(i):
    n = {k: np.asarray(v) for k, v in i.items()}
    a = _constants()
    x = n["x"]
    a["x_rows"] = _rows(x)
    halves = lambda xT: np.stack([_k_major(xT[:, :HALF]), _k_major(xT[:, HALF:])])
    a["xT_perm"] = halves(x.transpose(2, 1, 0).reshape(DM, TOK))
    a["ctxT"] = halves(n["ctx_4096"].reshape(TOK, DM).T)
    w = n["L0_attn_weight_qkv"].reshape(GROUPS, CH, P, DM)
    a["l0_wqkv"] = _group_weights(np.concatenate([w[:, 4:6], w[:, 0:4]], axis=1))
    a["l0_wo"] = _out_weights(n["L0_attn_weight_proj"])
    w = np.concatenate([n["L1_attn_Wk"].reshape(GROUPS, 1, P, DM), n["L1_attn_Wv"].reshape(GROUPS, 1, P, DM),
                        n["L1_attn_Wq"].reshape(GROUPS, QPG, P, DM)], axis=1)
    a["l1_wqkv"] = _group_weights(w)
    a["l1_wo"] = _out_weights(n["L1_attn_Wo"])
    for layer in range(2):
        o, x = f"L{layer}_xattn_", f"x{layer}_"
        if layer == 0:
            wk, wv, wq, wo = [n[o + k].T for k in ("Wk", "Wv", "Wq", "Wo")]
            bk, bv, bq = n[o + "bk"], n[o + "bv"], n[o + "bq"]
            a[x + "inter"] = np.repeat(n[o + "interference"].reshape(KC, 4, 1, 4, 4), 8, axis=2).reshape(KC, P, 4).transpose(1, 0, 2)
            a[x + "amp"] = n[o + "amp"].reshape(1, 1)
        else:
            share = lambda w: np.repeat(w.reshape(-1, 8, 1, 16), 4, axis=2).reshape(w.shape[0] if w.ndim > 1 else 1, DM)
            wk, wv, wq, wo = share(n[o + "Wk"]), share(n[o + "Wv"]), n[o + "Wq"], n[o + "Wo"]
            bk, bv, bq = share(n[o + "bk"]), share(n[o + "bv"]), n[o + "bq"]
        by_chunk = lambda w: w.reshape(KC, P, KC, P).transpose(1, 2, 0, 3).reshape(P, -1)
        a[x + "w"] = np.stack([by_chunk(wk), by_chunk(wv), by_chunk(wq), _k_major(wo)])
        a[x + "biases"] = np.stack([b.reshape(KC, P).T for b in (bk, bv, bq)], axis=1)
        a[x + "bo"] = n[o + "bo"].reshape(1, DM)
    f = "L0_ffn_"
    lora_a = n[f + "lora_A"].transpose(1, 0, 2).reshape(DM, P)
    router = np.repeat(n[f + "W_router"].T, P // 8, axis=1)
    a["f0_w"] = np.concatenate([_k_major(lora_a), _k_major(router), n[f + "lora_B"].reshape(P, DM),
                                _k_major(n[f + "W_base"].T)], axis=1)
    a["f0_base_bias"] = n[f + "b_base"].reshape(1, DM)
    a["f0_router_bias"] = np.repeat(n[f + "b_router"], P // 8).reshape(P, 1)
    f = "L1_ffn_"
    two = lambda w: w.reshape(DM, 2, P).transpose(1, 0, 2)
    w1 = np.concatenate([two(n[f + "sw1"]), n[f + "ew1"]])
    w2 = np.concatenate([two(n[f + "sw2"]), n[f + "ew2"]])
    w3 = np.concatenate([n[f + "sw3"].reshape(2, P, DM), n[f + "ew3"]])
    b1 = np.concatenate([n[f + "sb1"].reshape(2, P), n[f + "eb1"]])
    b2 = np.concatenate([n[f + "sb2"].reshape(2, P), n[f + "eb2"]])
    a["f1_w"] = np.concatenate([np.stack([_k_major(w) for w in w1]), np.stack([_k_major(w) for w in w2]), w3,
                                b1[:, :, None], b2[:, :, None]], axis=2)
    a["f1_b3"] = np.concatenate([n[f + "sb3"].reshape(1, DM), np.zeros((1, DM), np.float32), n[f + "eb3"]])
    a["f1_r_w"] = _k_major(np.repeat(n[f + "router_w"], P // 16, axis=1))
    a["f1_r_bias"] = np.repeat(n[f + "router_b"], P // 16).reshape(P, 1)
    a["f1_s_bias"] = n[f + "router_bias"].reshape(1, 16)
    return {k: np.ascontiguousarray(v) for k, v in a.items()}


def kernel(**inputs):
    import concourse.bacc as _bacc
    from concourse.bass_utils import run_bass_kernel_spmd as _run

    nc = _bacc.Bacc("TRN2", target_bir_lowering=False, num_devices=1)
    arrays = _lay_out(inputs)
    d = {k: nc.dram_tensor(f"in_{k}_dram", v.shape, mybir.dt.from_np(v.dtype), kind="ExternalInput").ap()
         for k, v in arrays.items()}
    out = nc.dram_tensor("out_0_dram", (NT, P, DM), F32, kind="ExternalOutput").ap()
    decoder(nc, d, out)
    r = _run(nc, [{f"in_{k}_dram": v for k, v in arrays.items()}], core_ids=[0])
    rows = r.results[0]["out_0_dram"]
    return rows.reshape(SEQ_A, SEQ_B, DM)
```

```python
from contextlib import ExitStack

import numpy as np

import concourse.bass as bass
from concourse import mybir

F32 = mybir.dt.float32
F32R = mybir.dt.float32r
BF16 = mybir.dt.bfloat16
ALU = mybir.AluOpType
ACT = mybir.ActivationFunctionType
AX = mybir.AxisListType

P = 128
SEQ_A, SEQ_B, DM = 16, 64, 512
TOK = SEQ_A * SEQ_B
KC = DM // P
NT = TOK // P
HALF = TOK // 2
GROUPS, QPG, HD = 8, 4, 128
CH = QPG + 2
EPS = 1e-5
EW = 3 * DM + 2
MASKED = -1e30




def wait(engine, semaphore, value):
    if isinstance(value, int) and value <= 0:
        return
    engine.wait_ge(semaphore, value)


def three_pass(pe, out, w_hi, w_lo, x_hi, x_lo, start, stop):
    pe.matmul(out, w_hi, x_hi, start=start, stop=False, skip_group_check=True)
    pe.matmul(out, w_hi, x_lo, start=False, stop=False, skip_group_check=True)
    return pe.matmul(out, w_lo, x_hi, start=False, stop=stop, skip_group_check=True)


class Phase:

    def __init__(self, nc, ctx, name):
        self.nc, self.ctx, self.name = nc, ctx, name
        self.semaphores = []

    def sb(self, name, shape, dt=F32):
        return self.ctx.enter_context(self.nc.sbuf_tensor(f"{self.name}_{name}", shape, dt))

    def ps(self, name, shape, dt=F32):
        return self.ctx.enter_context(self.nc.psum_tensor(f"{self.name}_{name}", shape, dt))

    def sem(self, name):
        self.semaphores.append(self.nc.alloc_semaphore(name=f"{self.name}_{name}"))
        return self.semaphores[-1]

    def close(self):
        self.nc.clear_and_free_semaphores(self.semaphores)
        self.nc.all_engine_barrier()


def attention_phase(nc, name, S, w_dram, wo_dram, mask_dram, layer0, next_loads, xT_raw_dram=None, rope_dram=None,
                    x_rows_dram=None, ident_dram=None):
    scale = float(HD) ** -0.5
    n_small = 32 if layer0 else 48
    S.begin_phase()
    with ExitStack() as ctx:
        ph = Phase(nc, ctx, name)
        sb, ps, sem = ph.sb, ph.ps, ph.sem
        QT = sb("QT", [P, 2, QPG, HALF])
        KT = sb("KT", [P, 2, HALF])
        VT = sb("VT", [P, HALF])
        V_hi = sb("V_hi", [P, 2, 4, HD], F32R)
        V_lo = sb("V_lo", [P, 2, 4, HD], F32R)
        W_raw = S.raw[:, 0:CH * DM].rearrange("p (c k n) -> p c k n", c=CH, k=KC)
        W_hi = sb("W_hi", [P, CH, KC, P], F32R)
        W_lo = sb("W_lo", [P, CH, KC, P], F32R)
        Wo_raw = S.raw[:, CH * DM:(CH + QPG) * DM].rearrange("p (h n) -> p h n", h=QPG)
        Wo_hi = sb("Wo_hi", [P, QPG, DM], F32R)
        Wo_lo = sb("Wo_lo", [P, QPG, DM], F32R)
        O_hi = sb("O_hi", [P, 2, QPG, HALF], F32R)
        O_lo = sb("O_lo", [P, 2, QPG, HALF], F32R)
        prob = sb("prob", [P, 2, QPG, P])
        probT_hi = sb("probT_hi", [P, 2, QPG, P], F32R)
        probT_lo = sb("probT_lo", [P, 2, QPG, P], F32R)
        top = sb("top", [P, 2, QPG])
        total = sb("total", [P, 2, QPG])
        inv = sb("inv", [P, 2, QPG])
        mask = sb("mask", [P, P], BF16)
        if not layer0:
            cos = sb("cos", [P, SEQ_B])
            sin = sb("sin", [P, SEQ_B])
            r_cos = sb("r_cos", [P, 2, HALF])
            r_sin = sb("r_sin", [P, 2, HALF])
        pA = ps("pA", [P, 2, HALF])
        pS = ps("pS", [P, QPG, P])
        pP = ps("pP", [P, QPG, P])
        pV = ps("pV", [P, 4, HD])
        pO = ps("pO", [P, QPG, P])
        pC = ps("pC", [P, 2, DM])
        mask_loaded = sem("mask_loaded")
        x_loaded = sem("x_loaded")
        first_loaded = [sem(f"first_loaded{i}") for i in range(3 if layer0 else 0)]
        xT_loaded = [sem(f"xT_loaded{hf}") for hf in range(2)]
        xT_hi_done = sem("xT_hi_done")
        xT_lo_done = sem("xT_lo_done")
        w_loaded = sem("w_loaded")
        wo_loaded = sem("wo_loaded")
        w_hi_done = sem("w_hi_done")
        w_lo_done = sem("w_lo_done")
        wo_hi_done = sem("wo_hi_done")
        wo_lo_done = sem("wo_lo_done")
        proj_done = sem("proj_done")
        chunk_read = [sem("chunk_read0"), sem("chunk_read1")]
        rope_done = sem("rope_done")
        v_turned = sem("v_turned")
        v_hi_done = sem("v_hi_done")
        v_lo_done = sem("v_lo_done")
        scores_done = sem("scores_done")
        masked = sem("masked")
        top_done = sem("top_done")
        shifted = sem("shifted")
        exp_done = sem("exp_done")
        total_done = sem("total_done")
        inv_done = sem("inv_done")
        prob_ready = sem("prob_ready")
        prob_turned = sem("prob_turned")
        probT_hi_done = sem("probT_hi_done")
        probT_lo_done = sem("probT_lo_done")
        av_done = sem("av_done")
        o_hi_done = sem("o_hi_done")
        o_lo_done = sem("o_lo_done")
        out_done = sem("out_done")
        summed = sem("summed")

        AHEAD = ((0, 1, 2), (3, 4), (5,), ())

        def o_tile(O, u2, t):
            if layer0:
                return O[:, u2].rearrange("p h (a t b) -> p h t b a", t=4, b=8)[:, :, t]
            return O[:, u2, :, t * P:(t + 1) * P]

        def po_view():
            if layer0:
                return pO[:, :, :].rearrange("p h (b a) -> p h b a", a=SEQ_A)
            return pO[:, :, :]

        def o_columns(O, u2, h, t):
            return O[:, u2, h, t * P:(t + 1) * P]

        def head_sum(ap):
            return ap.unsqueeze(2).broadcast_to([P, QPG, P])

        def loop(engine, body):
            body(0)
            with engine.Fori(1, GROUPS - 1) as g:
                body(g)
            body(GROUPS - 1)

        def is_last(g, hf):
            return isinstance(g, int) and g == GROUPS - 1 and hf == 1

        def is_first(g, hf):
            return isinstance(g, int) and g == 0 and hf == 0

        with nc.Block() as block:

            @block.sync
            def _(sp):
                if layer0:
                    half = lambda hf: QT[:, hf].rearrange("p k n -> p (k n)")
                    sp.dma_start(S.raw[:, 0:DM], w_dram[0][:, 0:DM]).then_inc(first_loaded[0], 16)
                    sp.dma_start(half(0), xT_raw_dram[0]).then_inc(xT_loaded[0], 16)
                    sp.dma_start(S.raw[:, DM:CH * DM], w_dram[0][:, DM:CH * DM]).then_inc(first_loaded[1], 16)
                    sp.dma_start(half(1), xT_raw_dram[1]).then_inc(xT_loaded[1], 16)
                    sp.dma_start(S.ident[:], ident_dram).then_inc(mask_loaded, 16)
                sp.dma_start(mask[:], mask_dram).then_inc(mask_loaded, 16)
                if not layer0:
                    sp.dma_start(cos[:], rope_dram[0]).then_inc(mask_loaded, 16)
                    sp.dma_start(sin[:], rope_dram[1]).then_inc(mask_loaded, 16)
                if layer0:
                    sp.dma_start(S.raw[:, CH * DM:(CH + QPG) * DM], wo_dram[0]).then_inc(first_loaded[2], 16)
                    for T in range(NT):
                        sp.dma_start(S.x[:, T], x_rows_dram[T]).then_inc(x_loaded, 16)

                with sp.Fori(1, GROUPS) as g:
                    sp.wait_ge(w_hi_done, CH * g)
                    sp.wait_ge(w_lo_done, CH * g)
                    sp.dma_start(W_raw.rearrange("p c k n -> p (c k n)"), w_dram[g]).then_inc(w_loaded, 16)
                    sp.wait_ge(wo_hi_done, QPG * g)
                    sp.wait_ge(wo_lo_done, QPG * g)
                    sp.dma_start(Wo_raw.rearrange("p h n -> p (h n)"), wo_dram[g]).then_inc(wo_loaded, 16)
                sp.wait_ge(w_lo_done, CH * GROUPS)
                sp.wait_ge(wo_lo_done, QPG * GROUPS)
                S.prefetch(sp, next_loads)

            @block.tensor
            def _(pe):
                def project(u, g, hf, c):
                    pe.wait_ge(w_hi_done, CH * g + c + 1)
                    pe.wait_ge(w_lo_done, CH * g + c + 1)
                    wait(pe, chunk_read[c % 2], 3 * u + c // 2)
                    if layer0 and c == 0 and isinstance(u, int) and u < 2:
                        pe.wait_ge(xT_lo_done, KC * (u + 1))
                    tok = slice(hf * HALF, (hf + 1) * HALF)
                    for k in range(KC):
                        mm = three_pass(pe, pA[:, c % 2, :], W_hi[:, c, k, :], W_lo[:, c, k, :],
                                        S.xT_hi[:, k, tok], S.xT_lo[:, k, tok], k == 0, k == KC - 1)
                    mm.then_inc(proj_done, 1)

                def turn_v(u, hf):
                    wait(pe, v_lo_done, u)
                    pe.wait_ge(chunk_read[1], 3 * u + 1)
                    for t in range(4):
                        mm = pe.transpose(pV[:, t, :], VT[:, t * P:(t + 1) * P], S.ident[:])
                    mm.then_inc(v_turned, 1)

                def scores(u, hf, t):
                    wait(pe, masked, 4 * u + t)
                    if t == 0:
                        if layer0:
                            pe.wait_ge(chunk_read[0], 3 * u + 3)
                            pe.wait_ge(chunk_read[1], 3 * u + 3)
                        else:
                            pe.wait_ge(rope_done, 5 * u + 5)
                    cols = slice(t * P, (t + 1) * P)
                    for h in range(QPG):
                        mm = pe.matmul(pS[:, h, :], QT[:, hf, h, cols], KT[:, hf, cols],
                                       start=True, stop=True, skip_group_check=True)
                    mm.then_inc(scores_done, 1)

                def turn_probs(u, t):
                    n = 4 * u + t
                    pe.wait_ge(prob_ready, n + 1)
                    wait(pe, probT_lo_done, n)
                    for h in range(QPG):
                        mm = pe.transpose(pP[:, h, :], prob[:, t % 2, h, :], S.ident[:])
                    mm.then_inc(prob_turned, 1)

                def attend(u, hf, t):
                    n = 4 * u + t
                    pe.wait_ge(probT_lo_done, n + 1)
                    if t == 0:
                        pe.wait_ge(v_lo_done, u + 1)
                    wait(pe, o_lo_done, n)
                    three_pass(pe, pO[:, :, :], V_hi[:, hf, t, :], V_lo[:, hf, t, :], probT_hi[:, t % 2, :, :],
                               probT_lo[:, t % 2, :, :], True, True).then_inc(av_done, 1)

                def out_project(u, g, hf, t):
                    n = 4 * u + t
                    if t == 0:
                        pe.wait_ge(o_lo_done, 4 * u + 4)
                        if hf == 0:
                            pe.wait_ge(wo_hi_done, QPG * (g + 1))
                            pe.wait_ge(wo_lo_done, QPG * (g + 1))
                    wait(pe, summed, n - 1)
                    for h in range(QPG):
                        mm = three_pass(pe, pC[:, t % 2, :], o_columns(O_hi, hf, h, t), o_columns(O_lo, hf, h, t),
                                        Wo_hi[:, h, :], Wo_lo[:, h, :], h == 0, h == QPG - 1)
                    mm.then_inc(out_done, 1)

                for c in range(CH):
                    project(0, 0, 0, c)
                pe.wait_ge(mask_loaded, n_small)
                turn_v(0, 0)
                scores(0, 0, 0)

                def body(g):
                    for hf in range(2):
                        u = 2 * g + hf
                        last = is_last(g, hf)
                        for t in range(4):
                            if t < 3:
                                scores(u, hf, t + 1)
                            elif not last:
                                scores(u + 1, 1 - hf, 0)
                            turn_probs(u, t)
                            if not last:
                                for c in AHEAD[t]:
                                    project(u + 1, g + hf, 1 - hf, c)
                                if t == 3:
                                    turn_v(u + 1, 1 - hf)
                            if t == 3 and not is_first(g, hf):
                                out_project(u - 1, g - 1 + hf, 1 - hf, t)
                            attend(u, hf, t)
                            if t < 3 and not is_first(g, hf):
                                out_project(u - 1, g - 1 + hf, 1 - hf, t)

                loop(pe, body)
                for t in range(4):
                    out_project(2 * GROUPS - 1, GROUPS - 1, 1, t)

            @block.scalar
            def _(act):
                def split_w(g, c):
                    if isinstance(g, int) and g == 0:
                        if not layer0:
                            S.wait_prefetched(act)
                        elif c < 2:
                            act.wait_ge(first_loaded[c], 16)
                    elif c == 0:
                        act.wait_ge(w_loaded, 16 * g)
                    if not (isinstance(g, int) and g == 0):
                        act.wait_ge(proj_done, CH * (2 * g - 1) + c + 1)
                    nc.scalar.copy(W_hi[:, c], W_raw[:, c]).then_inc(w_hi_done, 1)

                def split_wo(g):
                    if layer0 and isinstance(g, int) and g == 0:
                        act.wait_ge(first_loaded[2], 16)
                    wait(act, wo_loaded, 16 * g)
                    if not (isinstance(g, int) and g == 0):
                        act.wait_ge(out_done, 8 * g)
                    for h in range(QPG):
                        nc.scalar.copy(Wo_hi[:, h], Wo_raw[:, h]).then_inc(wo_hi_done, 1)

                def read_chunk(u, hf, c):
                    if not layer0 and c != 1:
                        return
                    act.wait_ge(proj_done, CH * u + c + 1)
                    if c == 1:
                        wait(act, v_turned, u)
                        dst = VT[:, :]
                    else:
                        wait(act, scores_done, 4 * u - 4)
                        dst = KT[:, hf, :] if c == 0 else QT[:, hf, c - 2, :]
                    nc.scalar.copy(dst, pA[:, c % 2, :]).then_inc(chunk_read[c % 2], 1)

                def read_v(u, hf):
                    act.wait_ge(v_turned, u + 1)
                    wait(act, av_done, 4 * u - 4)
                    nc.scalar.copy(V_hi[:, hf], pV[:, :, :]).then_inc(v_hi_done, 1)

                def exponent(u, t):
                    n = 4 * u + t
                    act.wait_ge(shifted, n + 1)
                    nc.scalar.activation(prob[:, t % 2], prob[:, t % 2], ACT.Exp, scale=scale).then_inc(exp_done, 1)

                def read_probT(u, t):
                    n = 4 * u + t
                    act.wait_ge(prob_turned, n + 1)
                    wait(act, av_done, n - 1)
                    nc.scalar.copy(probT_hi[:, t % 2], pP[:, :, :]).then_inc(probT_hi_done, 1)

                def read_o(u, hf, t):
                    n = 4 * u + t
                    act.wait_ge(av_done, n + 1)
                    wait(act, out_done, 4 * u - 4)
                    nc.scalar.copy(o_tile(O_hi, hf, t), po_view()).then_inc(o_hi_done, 1)

                split_w(0, 0)
                if layer0:
                    for hf in range(2):
                        act.wait_ge(xT_loaded[hf], 16)
                        for k in range(KC):
                            nc.scalar.copy(S.xT_hi[:, k, hf * HALF:(hf + 1) * HALF], QT[:, hf, k, :]).then_inc(xT_hi_done, 1)
                        if hf == 0:
                            for c in range(1, CH):
                                split_w(0, c)
                    act.wait_ge(xT_lo_done, 2 * KC)
                else:
                    for c in range(1, CH):
                        split_w(0, c)
                for c in range(CH):
                    read_chunk(0, 0, c)
                read_v(0, 0)
                exponent(0, 0)

                def body(g):
                    for hf in range(2):
                        u = 2 * g + hf
                        last = is_last(g, hf)
                        for t in range(4):
                            read_probT(u, t)
                            if t < 3:
                                exponent(u, t + 1)
                            elif not last:
                                exponent(u + 1, 0)
                            if not last:
                                for c in AHEAD[t]:
                                    read_chunk(u + 1, 1 - hf, c)
                                    if hf == 0 and not (isinstance(g, int) and g == GROUPS - 1):
                                        split_w(g + 1, c)
                                if t == 3:
                                    read_v(u + 1, 1 - hf)
                            read_o(u, hf, t)
                        if hf == 0:
                            split_wo(g)

                loop(act, body)

            @block.vector
            def _(dve):
                def soften(u, t):
                    n = 4 * u + t
                    dve.wait_ge(scores_done, n + 1)
                    wait(dve, prob_turned, n - 1)
                    nc.vector.tensor_tensor(prob[:, t % 2], pS[:, :, :], mask[:].unsqueeze(1).broadcast_to([P, QPG, P]),
                                            ALU.add).then_inc(masked, 1)
                    dve.wait_ge(masked, n + 1)
                    nc.vector.tensor_reduce(top[:, t % 2], prob[:, t % 2], AX.X, ALU.max).then_inc(top_done, 1)
                    dve.wait_ge(top_done, n + 1)
                    nc.vector.tensor_tensor(prob[:, t % 2], prob[:, t % 2], head_sum(top[:, t % 2]),
                                            ALU.subtract).then_inc(shifted, 1)

                def row_totals(u, t):
                    n = 4 * u + t
                    dve.wait_ge(exp_done, n + 1)
                    nc.vector.tensor_reduce(total[:, t % 2], prob[:, t % 2], AX.X, ALU.add).then_inc(total_done, 1)
                    dve.wait_ge(total_done, n + 1)
                    wait(dve, prob_ready, n - 1)
                    nc.vector.reciprocal(inv[:, t % 2], total[:, t % 2]).then_inc(inv_done, 1)

                def low_v(u, hf):
                    dve.wait_ge(v_hi_done, u + 1)
                    nc.vector.tensor_tensor(V_lo[:, hf], pV[:, :, :], V_hi[:, hf].bitcast(F32),
                                            ALU.subtract).then_inc(v_lo_done, 1)

                def low_probT(u, t):
                    dve.wait_ge(probT_hi_done, 4 * u + t + 1)
                    nc.vector.tensor_tensor(probT_lo[:, t % 2], pP[:, :, :], probT_hi[:, t % 2].bitcast(F32),
                                            ALU.subtract).then_inc(probT_lo_done, 1)

                def rope(u, c):
                    if layer0 or c == 1:
                        return
                    i = 0 if c == 0 else c - 1
                    m = 5 * u + i
                    slot = RS[0]
                    RS[0] = 1 - RS[0]
                    dve.wait_ge(proj_done, CH * u + c + 1)
                    wait(dve, rope_done, m - 1)
                    src = pA[:, c % 2, :].rearrange("p (a b) -> p a b", b=SEQ_B)
                    rc = r_cos[:, slot].rearrange("p (a b) -> p a b", b=SEQ_B)
                    rs = r_sin[:, slot].rearrange("p (a b) -> p a b", b=SEQ_B)
                    n_a = HALF // SEQ_B
                    h = HD // 2
                    nc.vector.tensor_tensor(rc, src, cos[:].unsqueeze(1).broadcast_to([P, n_a, SEQ_B]), ALU.mult)
                    nc.vector.tensor_tensor(rs[0:h], src[h:P], sin[h:P].unsqueeze(1).broadcast_to([h, n_a, SEQ_B]), ALU.mult)
                    nc.vector.tensor_tensor(rs[h:P], src[0:h], sin[0:h].unsqueeze(1).broadcast_to([h, n_a, SEQ_B]),
                                            ALU.mult).then_inc(chunk_read[c % 2], 1)

                def read_o_lo(u, hf, t):
                    n = 4 * u + t
                    dve.wait_ge(o_hi_done, n + 1)
                    nc.vector.tensor_tensor(o_tile(O_lo, hf, t), po_view(), o_tile(O_hi, hf, t).bitcast(F32),
                                            ALU.subtract).then_inc(o_lo_done, 1)

                def add_out(u, hf, t):
                    n = 4 * u + t
                    dve.wait_ge(out_done, n + 1)
                    wait(dve, summed, n - 3)
                    T = 4 * hf + t
                    nc.vector.tensor_tensor(S.x[:, T], pC[:, t % 2, :], S.x[:, T], ALU.add).then_inc(summed, 1)

                RS = [0]
                if layer0:
                    for hf in range(2):
                        for k in range(KC):
                            tok = slice(hf * HALF, (hf + 1) * HALF)
                            dve.wait_ge(xT_hi_done, KC * hf + k + 1)
                            nc.vector.tensor_tensor(S.xT_lo[:, k, tok], QT[:, hf, k, :], S.xT_hi[:, k, tok].bitcast(F32),
                                                    ALU.subtract).then_inc(xT_lo_done, 1)
                    dve.wait_ge(x_loaded, 16 * NT)
                dve.wait_ge(mask_loaded, n_small)
                for c in range(CH):
                    rope(0, c)
                soften(0, 0)
                low_v(0, 0)
                row_totals(0, 0)

                def body(g):
                    for hf in range(2):
                        u = 2 * g + hf
                        last = is_last(g, hf)
                        for t in range(4):
                            nu, nt = (u, t + 1) if t < 3 else (u + 1, 0)
                            todo = t < 3 or not last
                            if todo:
                                soften(nu, nt)
                            low_probT(u, t)
                            if not last:
                                for c in AHEAD[t][:1]:
                                    rope(u + 1, c)
                            if todo:
                                row_totals(nu, nt)
                            if not last:
                                for c in AHEAD[t][1:]:
                                    rope(u + 1, c)
                                if t == 3:
                                    low_v(u + 1, 1 - hf)
                            if t == 3 and not is_first(g, hf):
                                add_out(u - 1, 1 - hf, t)
                            read_o_lo(u, hf, t)
                            if t < 3 and not is_first(g, hf):
                                add_out(u - 1, 1 - hf, t)

                loop(dve, body)
                for t in range(4):
                    add_out(2 * GROUPS - 1, 1, t)

            @block.gpsimd
            def _(pool):
                def split_w(g, c):
                    pool.wait_ge(w_hi_done, CH * g + c + 1)
                    if not (isinstance(g, int) and g == 0):
                        pool.wait_ge(proj_done, CH * (2 * g - 1) + c + 1)
                    nc.gpsimd.tensor_tensor(W_lo[:, c], W_raw[:, c], W_hi[:, c].bitcast(F32),
                                            ALU.subtract).then_inc(w_lo_done, 1)

                def split_wo(g):
                    if not (isinstance(g, int) and g == 0):
                        pool.wait_ge(out_done, 8 * g)
                    for h in range(QPG):
                        pool.wait_ge(wo_hi_done, QPG * g + h + 1)
                        nc.gpsimd.tensor_tensor(Wo_lo[:, h], Wo_raw[:, h], Wo_hi[:, h].bitcast(F32),
                                                ALU.subtract).then_inc(wo_lo_done, 1)

                def divide(u, t):
                    n = 4 * u + t
                    pool.wait_ge(inv_done, n + 1)
                    nc.gpsimd.tensor_tensor(prob[:, t % 2], prob[:, t % 2], head_sum(inv[:, t % 2]),
                                            ALU.mult).then_inc(prob_ready, 1)

                def rope_add(u, hf, c):
                    if layer0 or c == 1:
                        return
                    slot = RS[0]
                    RS[0] = 1 - RS[0]
                    pool.wait_ge(chunk_read[c % 2], 3 * u + c // 2 + 1)
                    wait(pool, scores_done, 4 * u - 4)
                    dst = KT[:, hf, :] if c == 0 else QT[:, hf, c - 2, :]
                    nc.gpsimd.tensor_tensor(dst, r_cos[:, slot], r_sin[:, slot], ALU.add).then_inc(rope_done, 1)

                RS = [0]
                for c in range(CH):
                    split_w(0, c)
                for c in range(CH):
                    rope_add(0, 0, c)
                divide(0, 0)

                def body(g):
                    for hf in range(2):
                        u = 2 * g + hf
                        last = is_last(g, hf)
                        for t in range(4):
                            if not last:
                                for c in AHEAD[t][:1]:
                                    rope_add(u + 1, 1 - hf, c)
                            if t < 3:
                                divide(u, t + 1)
                            elif not last:
                                divide(u + 1, 0)
                            if not last:
                                for c in AHEAD[t][1:]:
                                    rope_add(u + 1, 1 - hf, c)
                                if hf == 0 and not (isinstance(g, int) and g == GROUPS - 1):
                                    for c in AHEAD[t]:
                                        split_w(g + 1, c)
                        if hf == 0:
                            split_wo(g)

                loop(pool, body)
        ph.close()


class State:

    def __init__(self, nc, ctx):
        sb = lambda name, shape, dt=F32: ctx.enter_context(nc.sbuf_tensor(name, shape, dt))
        self.x = sb("x", [P, NT, DM])
        self.xT_hi = sb("xT_hi", [P, KC, TOK], F32R)
        self.xT_lo = sb("xT_lo", [P, KC, TOK], F32R)
        self.ident = sb("ident", [P, P])
        self.raw = sb("raw", [P, (CH + QPG) * DM])
        self.prefetched = ctx.enter_context(nc.semaphore("prefetched"))
        self.loads = 0

    def prefetch(self, sp, loads):
        for dst, src in loads:
            sp.dma_start(dst, src).then_inc(self.prefetched, 16)
        self.loads += len(loads)

    def wait_prefetched(self, engine):
        engine.wait_ge(self.prefetched, 16 * self.loads_before)

    def begin_phase(self):
        self.loads_before = self.loads


class Norm:

    def __init__(self, nc, ph, tag, S, groups, banks=None, ring=4, split_rows=False):
        self.nc, self.S, self.groups, self.banks, self.ring, self.split_rows = nc, S, groups, banks, ring, split_rows
        self.stats = ph.sb(tag + "_stats", [P, NT, 6])
        self.mv = ph.sb(tag + "_mv", [P, NT, 2])
        self.var, self.dev, self.rstd, self.newton = [ph.sb(f"{tag}_{n}", [P, NT]) for n in ("var", "dev", "rstd", "newton")]
        names = ("stats_done", "mv_done", "var_done", "dev_done", "newton_step", "normed", "turned", "x_hi_done", "x_lo_done")
        (self.stats_done, self.mv_done, self.var_done, self.dev_done, self.newton_step,
         self.normed, self.turned, self.x_hi_done, self.x_lo_done) = [ph.sem(f"{tag}_{n}") for n in names]

    def statistics(self, T):
        self.nc.vector.bn_stats(self.stats[:, T], self.S.x[:, T]).then_inc(self.stats_done, 1)

    def variances(self, dve, i):
        nc, (a, b) = self.nc, self.groups[i]
        for T in range(a, b):
            dve.wait_ge(self.stats_done, T + 1)
            nc.vector.bn_aggr(self.mv[:, T], self.stats[:, T]).then_inc(self.mv_done, 1)
        dve.wait_ge(self.mv_done, b)
        nc.vector.tensor_scalar(self.var[:, a:b], self.mv[:, a:b, 1], EPS, None, ALU.add).then_inc(self.var_done, 1)

    def scale_rows(self, dve, i):
        nc, (a, b) = self.nc, self.groups[i]
        var, dev, r, t = self.var[:, a:b], self.dev[:, a:b], self.rstd[:, a:b], self.newton[:, a:b]
        dve.wait_ge(self.dev_done, i + 1)
        dve.wait_ge(self.var_done, i + 1)
        steps = (lambda: nc.vector.reciprocal(r, dev),
                 lambda: nc.vector.tensor_tensor(t, r, r, ALU.mult),
                 lambda: nc.vector.tensor_tensor(t, t, var, ALU.mult),
                 lambda: nc.vector.tensor_scalar(t, t, -0.5, 1.5, ALU.mult, ALU.add),
                 lambda: nc.vector.tensor_tensor(r, r, t, ALU.mult))
        for n, step in enumerate(steps):
            step().then_inc(self.newton_step, 1)
            dve.wait_ge(self.newton_step, len(steps) * i + n + 1)
        for T in range(a, b):
            nc.vector.tensor_scalar(self.S.x[:, T], self.S.x[:, T], self.mv[:, T, 0:1], self.rstd[:, T:T + 1],
                                    ALU.subtract, ALU.mult).then_inc(self.normed, 1)

    def low(self, dve, T):
        dve.wait_ge(self.x_hi_done, T + 1)
        for (lo, bank), (hi, _) in zip(self.parts(self.S.xT_lo, T), self.parts(self.S.xT_hi, T)):
            ins = self.nc.vector.tensor_tensor(lo, bank, hi.bitcast(F32), ALU.subtract)
        ins.then_inc(self.x_lo_done, 1)

    def root(self, act, i):
        a, b = self.groups[i]
        act.wait_ge(self.var_done, i + 1)
        self.nc.scalar.activation(self.dev[:, a:b], self.var[:, a:b], ACT.Sqrt).then_inc(self.dev_done, 1)

    def high(self, act, T):
        act.wait_ge(self.turned, T + 1)
        for hi, bank in self.parts(self.S.xT_hi, T):
            ins = self.nc.scalar.copy(hi, bank)
        ins.then_inc(self.x_hi_done, 1)

    def turn(self, pe, T):
        pe.wait_ge(self.normed, T + 1)
        wait(pe, self.x_lo_done, T - self.ring + 1)
        for k in range(KC):
            mm = pe.transpose(self.banks(T)[:, k], self.S.x[:, T, k * P:(k + 1) * P], self.S.ident[:])
        mm.then_inc(self.turned, 1)

    def parts(self, xT, T):
        if not self.split_rows:
            return [(xT[:, :, T * P:(T + 1) * P], self.banks(T))]
        hb, r = divmod(T, 4)
        to = xT[:].rearrange("p k (r a h b) -> p k r h a b", r=4, a=4, h=2)[:, :, r, hb]
        return [(to[:, k], self.banks(T)[:, k].rearrange("p (a b) -> p a b", a=4)) for k in range(KC)]


def cross_attention_phase(nc, name, S, d, rows_per_unit, ctx_half, next_loads, x_dram=None):
    mixed = rows_per_unit == 32
    W = DM // rows_per_unit // 2
    U = P // rows_per_unit
    D = 1 if mixed else 16
    scale = float(8 if mixed else 16) ** -0.5
    SB = SEQ_B
    K, V, Q, O = range(4)
    VC = KC if mixed else 1
    chunks = (KC, VC, KC, KC)
    fills = [(m, hf, c) for m in (K, V, Q) for hf in range(2) for c in range(chunks[m])]
    fill_at = {fill: n for n, fill in enumerate(fills)}
    chunk_at = {chunk: n for n, chunk in enumerate((m, c) for m in range(4) for c in range(chunks[m]))}
    V_END, Q_HALF, Q_END = fill_at[Q, 0, 0], fill_at[Q, 1, 0], len(fills)
    LEFT = Q_END // 2
    if mixed:
        turns = {fill_at[V, 0, 0] + T: (T,) for T in range(NT)}
        splits = {fill_at[m, 1, c]: [(m + 1, c)] for m in (K, V, Q) for c in range(KC)}
    else:
        turns = {V_END - 4 + i: (2 * i, 2 * i + 1) for i in range(4)}
        splits = {fill_at[Q, 1, c]: [(O, c)] for c in range(KC)}
        splits |= {fill_at[K, 1, 0]: [(V, 0)], fill_at[V, 0, 0]: [(Q, 0), (Q, 1)], fill_at[V, 1, 0]: [(Q, 2), (Q, 3)]}
    S.begin_phase()
    with ExitStack() as ctx:
        ph = Phase(nc, ctx, name)
        sb, ps, sem = ph.sb, ph.ps, ph.sem
        with ExitStack() as early:
            ph_early = Phase(nc, early, name)
            ctx_hi = ph_early.sb("ctx_hi", [P, KC, TOK], F32R)
            ctx_lo = ph_early.sb("ctx_lo", [P, KC, TOK], F32R)
        Kmask = sb("Kmask", [P, 2, KC, 4, P])
        Vmask = sb("Vmask", [P, 2, 2, 2 * DM + 5 * D])
        W_raw = S.raw[:, 0:KC * DM].rearrange("p (k n) -> p k n", k=KC)
        slots = KC if mixed else KC + 1
        W_hi = sb("W_hi", [P, slots, DM], F32R)
        W_lo = sb("W_lo", [P, slots, DM], F32R)
        QT = sb("QT", [P, KC, TOK])
        KT = sb("KT", [P, KC, TOK])
        VT = sb("VT", [P, VC, TOK])
        ctx_raw = [S.raw[:, KC * DM:2 * KC * DM].rearrange("p (k n) -> p k n", k=KC),
                   QT[:, 0:2, :].rearrange("p a (b n) -> p (a b) n", n=HALF)]
        Qunit = sb("Qunit", [P, 2, KC, U, P])
        Ktile = sb("Ktile", [P, KC, P])
        Vtile = sb("Vtile", [P, VC, P])
        prob = sb("prob", [P, 4, 8, SB])
        probT = sb("probT", [P, 2, 4, P])
        top = sb("top", [P, 4, 8])
        total = sb("total", [P, 4, 8])
        inv = sb("inv", [P, 4, 8])
        row_mask = sb("row_mask", [P, 4])
        unit_mask = sb("unit_mask", [P, U])
        biases = sb("biases", [P, 3, KC])
        bo = sb("bo", [P, DM])
        if mixed:
            inter = sb("inter", [P, KC, 4])
            amp = sb("amp", [P, 1])
            same = sb("same", [P, 32])
            mix = sb("mix", [P, KC, P])
        pM = ps("pM", [P, 2, DM])
        pN = ps("pN", [P, 4, DM])
        pS = pN[:, 0:2, :]
        pO = pN[:, 2:4, :].rearrange("p e (c n) -> p e c n", c=KC)
        pP = ps("pP", [P, 4, P])
        pV = ps("pV", [P, DM])
        pX = [pP[:, :, :].rearrange("p i n -> p (i n)"), pV[:, :]]
        norm_bank = lambda T: pN[:, T % 4, :].rearrange("p (k n) -> p k n", k=KC)
        norm_in = Norm(nc, ph, "in", S, [(0, NT)], norm_bank, split_rows=mixed)
        norm_out = Norm(nc, ph, "out", S, [(T, T + 2) for T in range(0, NT, 2)], norm_bank)
        small_loaded = sem("small_loaded")
        ctx_loaded = sem("ctx_loaded")
        x_stored = sem("x_stored")
        x_loaded = sem("x_loaded")
        x_biased = sem("x_biased")
        ctx_hi_done = sem("ctx_hi_done")
        ctx_lo_done = sem("ctx_lo_done")
        w_loaded = sem("w_loaded")
        w_hi_done = sem("w_hi_done")
        w_lo_done = sem("w_lo_done")
        mix_step = sem("mix_step")
        proj_done = sem("proj_done")
        bank_read = [sem("bank_read0"), sem("bank_read1")]
        mixed_done = sem("mixed_done")
        mixed_read = sem("mixed_read")
        k_copied = sem("k_copied")
        v_copied = sem("v_copied")
        v_turned = sem("v_turned")
        zeroed = sem("zeroed")
        v_masked = sem("v_masked")
        q_ready = sem("q_ready")
        k_ready = sem("k_ready")
        scores_done = sem("scores_done")
        top_done = sem("top_done")
        shifted = sem("shifted")
        exp_done = sem("exp_done")
        total_done = sem("total_done")
        inv_done = sem("inv_done")
        prob_ready = sem("prob_ready")
        prob_turned = sem("prob_turned")
        probT_ready = sem("probT_ready")
        av_done = sem("av_done")
        o_hi_done = sem("o_hi_done")
        o_lo_done = sem("o_lo_done")
        out_done = sem("out_done")
        n_small = 7 if mixed else 4
        PAIRS = NT // 2
        AHEAD = 3

        def softmax_rows(ap):
            return ap.unsqueeze(2).broadcast_to([P, 8, SB])

        def half(hf):
            return slice(hf * HALF, (hf + 1) * HALF)

        def w_slot(m, c):
            return KC if m == V and not mixed else c

        def split_after(m, c):
            users = [n + 1 for n, (m2, hf, c2) in enumerate(fills) if m2 < m and w_slot(m2, c2) == w_slot(m, c)]
            return max(users, default=0)

        def loop(engine, body):
            body(0)
            with engine.Fori(1, PAIRS - 1) as i:
                body(i)
            body(PAIRS - 1)

        def is_first(i, e):
            return isinstance(i, int) and i == 0 and e == 0

        def is_last(i, e):
            return isinstance(i, int) and i == PAIRS - 1 and e == 1

        def two_ahead(i):
            return not (isinstance(i, int) and i == PAIRS - 1)

        def wait_chunks(engine, n):
            if mixed:
                engine.wait_ge(mixed_read, n)
            else:
                for bank in bank_read:
                    engine.wait_ge(bank, n // 2)

        def step_ahead(i, e, w, n):
            j = 2 * i + e
            if w + n < W:
                return True, j, e, w + n
            return not is_last(i, e), j + 1, 1 - e, w + n - W

        def masked_v(slot, b, m2):
            width = DM + 2 * D
            rows = Vmask[m2 * SB:(m2 + 1) * SB, slot, b, D * m2:D * m2 + 2 * width]
            to = rows.rearrange("p (pair q) -> p pair q", pair=2)[:, :, 0:DM].rearrange("p pair (k r) -> p pair k r", r=4 * D)
            v = pV[b * SB:(b + 1) * SB, :]
            if mixed:
                src = v.rearrange("p (k pair m d) -> p pair k m d", pair=2, m=2, d=D)[:, :, :, m2]
            else:
                src = v[:, 0:P].rearrange("p (k d) -> p k d", d=D).unsqueeze(1).broadcast_to([SB, 2, P // D, D])
            return to[:, :, :, 0:D], src

        with nc.Block() as block:

            @block.sync
            def _(sp):
                sp.dma_start(QT[:, 0:2, :].rearrange("p a n -> p (a n)"), ctx_half).then_inc(ctx_loaded, 16)
                sp.dma_start(biases[:], d["biases"]).then_inc(small_loaded, 16)
                sp.dma_start(row_mask[:], d["row_mask"]).then_inc(small_loaded, 16)
                sp.dma_start(unit_mask[:], d["unit_mask"]).then_inc(small_loaded, 16)
                sp.dma_start(bo[:], d["bo"].broadcast_to([P, DM])).then_inc(small_loaded, 16)
                if mixed:
                    sp.dma_start(inter[:], d["inter"]).then_inc(small_loaded, 16)
                    sp.dma_start(amp[:], d["amp"].broadcast_to([P, 1])).then_inc(small_loaded, 16)
                    sp.dma_start(same[:], d["same"]).then_inc(small_loaded, 16)

                def load_w(m):
                    sp.wait_ge(w_hi_done, chunk_at[m, 0])
                    sp.wait_ge(w_lo_done, chunk_at[m, 0])
                    sp.dma_start(S.raw[:, 0:chunks[m] * DM], d[("w_k", "w_v", "w_q", "w_o")[m]]).then_inc(w_loaded, 16)

                load_w(V)
                if mixed:
                    rows = x_dram.rearrange("t (a h b) n -> h t a b n", a=2, h=2)
                    for T in range(NT):
                        sp.wait_ge(norm_in.normed, T + 1)
                        hb, r = divmod(T, 4)
                        for a4 in range(4):
                            sp.dma_start(rows[hb, 2 * r + a4 // 2, a4 % 2], S.x[32 * a4:32 * a4 + 32, T]).then_inc(x_stored, 16)
                load_w(Q)
                if mixed:
                    sp.wait_ge(x_stored, 16 * NT * 4)
                    sp.wait_ge(norm_in.turned, NT)
                    for T in range(NT):
                        sp.dma_start(S.x[:, T], x_dram[T]).then_inc(x_loaded, 16)
                load_w(O)
                sp.wait_ge(w_hi_done, len(chunk_at))
                sp.wait_ge(w_lo_done, len(chunk_at))
                S.prefetch(sp, next_loads)

            @block.tensor
            def _(pe):
                def mix_chunk(n):
                    m, hf, c = fills[n]
                    if n == 0:
                        pe.wait_ge(mix_step, 1 + 2 * KC)
                    pe.wait_ge(bank_read[n % 2], n // 2 + 1)
                    wait(pe, mixed_read, n - 1)
                    pe.matmul(pX[n % 2], mix[:, c, :], (KT, VT, QT)[m][:, c, half(hf)],
                              start=True, stop=True, skip_group_check=True).then_inc(mixed_done, 1)

                for n, (m, hf, c) in enumerate(fills):
                    hi, lo = (S.xT_hi, S.xT_lo) if m == Q else (ctx_hi, ctx_lo)
                    if n == V_END:
                        pe.wait_ge(norm_in.x_lo_done, NT)
                    if hf == 0:
                        pe.wait_ge(w_hi_done, chunk_at[m, c] + 1)
                        pe.wait_ge(w_lo_done, chunk_at[m, c] + 1)
                    wait(pe, bank_read[n % 2], n // 2)
                    for k in range(KC):
                        if m == K and c == 0:
                            pe.wait_ge(ctx_lo_done, KC * hf + k + 1)
                        wk = slice(k * P, (k + 1) * P)
                        mm = three_pass(pe, pM[:, n % 2, :], W_hi[:, w_slot(m, c), wk], W_lo[:, w_slot(m, c), wk],
                                        hi[:, k, half(hf)], lo[:, k, half(hf)], k == 0, k == KC - 1)
                    mm.then_inc(proj_done, 1)
                    if mixed and n > 0:
                        mix_chunk(n - 1)
                    for T in turns.get(n, ()):
                        norm_in.turn(pe, T)

                def turn_v(j):
                    pe.wait_ge(v_copied, j + 1)
                    wait(pe, v_masked, j)
                    for c in range(VC):
                        mm = pe.transpose(pV[:, c * P:(c + 1) * P], Vtile[:, c, :], S.ident[:])
                    mm.then_inc(v_turned, 1)

                def unit(w, i):
                    return w // 2, slice(w // 2 * rows_per_unit, (w // 2 + 1) * rows_per_unit), 2 * (w % 2) + i

                def wait_qk(j):
                    pe.wait_ge(q_ready, j + 1)
                    pe.wait_ge(k_ready, j + 1)

                def scores(j, slot, w):
                    for i in range(2):
                        place, _, c = unit(w, i)
                        for b in range(2):
                            mm = pe.matmul(pS[b * SB:(b + 1) * SB, w % 2, i * 4 * SB:(i + 1) * 4 * SB],
                                           Qunit[:, slot, c, place, b * SB:(b + 1) * SB],
                                           Kmask[:, slot, c, :, b * SB:(b + 1) * SB],
                                           start=True, stop=True, skip_group_check=True)
                    mm.then_inc(scores_done, 1)

                def turn_probs(j, w):
                    n = W * j + w
                    pe.wait_ge(prob_ready, n + 1)
                    wait(pe, probT_ready, n)
                    for i in range(4):
                        mm = pe.transpose(pP[:, i, :], prob[:, w % 4, 2 * i:2 * i + 2, :], S.ident[:])
                    mm.then_inc(prob_turned, 1)

                def attend(j, slot, w):
                    n = W * j + w
                    pe.wait_ge(probT_ready, n + 1)
                    if w == 0:
                        pe.wait_ge(v_masked, j + 1)
                        wait(pe, o_lo_done, j - 1)
                    for i in range(2):
                        _, r, c = unit(w, i)
                        for b in range(2):
                            for pair in range(2):
                                col = pair * DM + c * P
                                mm = pe.matmul(pO[r, slot, c, b * SB:(b + 1) * SB],
                                               Vmask[:, slot, b, col + r.start:col + r.stop],
                                               probT[:, w % 2, 2 * i + pair, b * SB:(b + 1) * SB],
                                               start=pair == 0, stop=pair == 1, skip_group_check=True,
                                               tile_position=(0, r.start))
                    mm.then_inc(av_done, 1)

                if mixed:
                    mix_chunk(Q_END - 1)
                    pe.wait_ge(mixed_read, Q_END)
                turn_v(0)
                wait_qk(0)
                for w in range(AHEAD):
                    if w == 2:
                        pe.wait_ge(shifted, 1)
                    scores(0, 0, w)

                def body(i):
                    for e in range(2):
                        j = 2 * i + e
                        for w in range(W):
                            exists, nj, slot, nw = step_ahead(i, e, w, AHEAD)
                            if exists:
                                if nw == 0:
                                    wait_qk(nj)
                                pe.wait_ge(shifted, W * j + w + 2)
                                scores(nj, slot, nw)
                            turn_probs(j, w)
                            if w == 1 and not is_last(i, e):
                                turn_v(j + 1)
                            if w > 0:
                                attend(j, e, w - 1)
                            elif not is_first(i, e):
                                attend(j - 1, 1 - e, W - 1)

                loop(pe, body)
                attend(NT - 1, 1, W - 1)
                pe.wait_ge(w_hi_done, len(chunk_at))
                pe.wait_ge(w_lo_done, len(chunk_at))
                for T in range(NT):
                    if T in (0, NT - 1):
                        pe.wait_ge(o_lo_done, NT - 1 if T == 0 else NT)
                    pe.wait_ge(bank_read[T % 2], LEFT + T // 2)
                    cols = slice(T * P, (T + 1) * P)
                    for c in range(KC):
                        mm = three_pass(pe, pM[:, T % 2, :], S.xT_hi[:, c, cols], S.xT_lo[:, c, cols],
                                        W_hi[:, c, :], W_lo[:, c, :], c == 0, c == KC - 1)
                    mm.then_inc(out_done, 1)
                    for turned in {5: (0, 1), 6: (2, 3), 7: (4, 5, 6, 7)}.get(T, ()):
                        norm_out.turn(pe, turned)

            @block.scalar
            def _(act):
                def split_w(m, c):
                    if m == K:
                        S.wait_prefetched(act)
                    elif c == 0:
                        act.wait_ge(w_loaded, 16 * m)
                    wait(act, proj_done, split_after(m, c))
                    nc.scalar.copy(W_hi[:, w_slot(m, c)], W_raw[:, c]).then_inc(w_hi_done, 1)

                def ctx_high(hf, k):
                    nc.scalar.copy(ctx_hi[:, k, half(hf)], ctx_raw[hf][:, k]).then_inc(ctx_hi_done, 1)

                split_w(K, 0)
                for k in range(KC):
                    ctx_high(0, k)
                for c in range(1, KC):
                    split_w(K, c)
                act.wait_ge(small_loaded, 16 * n_small)

                def read_mixed(n):
                    m, hf, c = fills[n]
                    act.wait_ge(mixed_done, n + 1)
                    nc.scalar.copy((KT, VT, QT)[m][:, c, half(hf)], pX[n % 2]).then_inc(mixed_read, 1)

                def mask_k(j, slot, softmaxes):
                    act.wait_ge(k_copied, j + 1)
                    wait(act, scores_done, W * (j - 1))
                    for m in softmaxes:
                        ins = nc.scalar.activation(Kmask[:, slot, :, m, :], Ktile[:], ACT.Copy, scale=row_mask[:, m:m + 1])
                    if m == 3:
                        ins.then_inc(k_ready, 1)

                for n, (m, hf, c) in enumerate(fills):
                    act.wait_ge(proj_done, n + 1)
                    if n == V_END:
                        act.wait_ge(ctx_lo_done, 2 * KC)
                    nc.scalar.activation((KT, VT, QT)[m][:, c, half(hf)], pM[:, n % 2, :], ACT.Identity,
                                         bias=biases[:, m, c:c + 1]).then_inc(bank_read[n % 2], 1)
                    if n == 1:
                        act.wait_ge(ctx_loaded, 16)
                        for k in range(KC):
                            ctx_high(1, k)
                    if n == 3:
                        norm_in.root(act, 0)
                    for T in turns.get(n - 1, ()) + (turns[n] if n == V_END - 1 else ()):
                        norm_in.high(act, T)
                    for chunk in splits.get(n, ()):
                        split_w(*chunk)
                    if mixed and n > 0:
                        read_mixed(n - 1)
                    if n >= Q_HALF:
                        mask_k(c // 2, c // 2, ((0, 1), (2, 3))[c % 2])
                if mixed:
                    read_mixed(Q_END - 1)

                def read_probT(j, w):
                    n = W * j + w
                    act.wait_ge(prob_turned, n + 1)
                    wait(act, av_done, n - 1)
                    nc.scalar.copy(probT[:, w % 2], pP[:, :, :]).then_inc(probT_ready, 1)

                def high_o(j, slot):
                    nc.scalar.copy(S.xT_hi[:, :, bass.ds(j * P, P)], pO[:, slot]).then_inc(o_hi_done, 1)

                def exponent(j, w):
                    n = W * j + w
                    act.wait_ge(shifted, n + 1)
                    nc.scalar.activation(prob[:, w % 4], prob[:, w % 4], ACT.Exp, scale=scale).then_inc(exp_done, 1)

                def mask_v(j, slot):
                    act.wait_ge(v_turned, j + 1)
                    wait(act, av_done, W * (j - 1))
                    for b in range(2):
                        for m2 in range(2):
                            to, src = masked_v(slot, b, m2)
                            ins = nc.scalar.copy(to, src)
                    ins.then_inc(v_masked, 1)

                exponent(0, 0)
                act.wait_ge(zeroed, 1)
                mask_v(0, 0)
                exponent(0, 1)
                exponent(0, 2)

                def body(i):
                    for e in range(2):
                        j = 2 * i + e
                        for w in range(W):
                            read_probT(j, w)
                            if w == 1 and not is_first(i, e):
                                high_o(j - 1, 1 - e)
                            exists, nj, slot, nw = step_ahead(i, e, w, AHEAD)
                            if exists:
                                exponent(nj, nw)
                            if w == W - 3 and two_ahead(i):
                                mask_k(j + 2, e, (0, 1))
                            if w == W - 2 and two_ahead(i):
                                mask_k(j + 2, e, (2, 3))
                            if w == 3 and not is_last(i, e):
                                mask_v(j + 1, 1 - e)

                loop(act, body)
                act.wait_ge(av_done, W * NT)
                high_o(NT - 1, 1)
                for i in range(PAIRS):
                    norm_out.root(act, i)
                    for T in range(2 * (i - 1), 2 * i):
                        if T >= 0:
                            norm_out.high(act, T)
                for T in range(NT - 2, NT):
                    norm_out.high(act, T)

            @block.vector
            def _(dve):
                def ctx_low(hf):
                    for k in range(KC):
                        dve.wait_ge(ctx_hi_done, KC * hf + k + 1)
                        nc.vector.tensor_tensor(ctx_lo[:, k, half(hf)], ctx_raw[hf][:, k], ctx_hi[:, k, half(hf)].bitcast(F32),
                                                ALU.subtract).then_inc(ctx_lo_done, 1)

                def build_mix():
                    nc.vector.tensor_scalar(inter[:], inter[:], amp[:, 0:1], 0.1, ALU.mult, ALU.mult).then_inc(mix_step, 1)
                    dve.wait_ge(mix_step, 1)
                    for c in range(KC):
                        nc.vector.tensor_tensor(mix[:, c, :].rearrange("p (h j) -> p h j", j=4),
                                                same[:].unsqueeze(2).broadcast_to([P, 32, 4]),
                                                inter[:, c].unsqueeze(1).broadcast_to([P, 32, 4]),
                                                ALU.mult).then_inc(mix_step, 1)
                        dve.wait_ge(mix_step, 2 + 2 * c)
                        nc.vector.tensor_tensor(mix[:, c, :], mix[:, c, :], S.ident[:], ALU.add).then_inc(mix_step, 1)

                ctx_low(0)
                dve.wait_ge(small_loaded, 16 * n_small)
                if mixed:
                    build_mix()
                for T in range(NT):
                    norm_in.statistics(T)
                norm_in.variances(dve, 0)
                ctx_low(1)
                norm_in.scale_rows(dve, 0)
                for T in range(NT):
                    norm_in.low(dve, T)
                def copy_v(j):
                    wait(dve, v_turned, j)
                    nc.vector.tensor_scalar(Vtile[:], VT[:, :, bass.ds(j * P, P)], 1.0, None, ALU.mult).then_inc(v_copied, 1)

                def soften(ahead, behind):
                    if ahead is not None:
                        j, w = ahead
                        n = W * j + w
                        bank = pS[:, w % 2, :].rearrange("p (u k) -> p u k", u=8)
                        dve.wait_ge(scores_done, n + 1)
                        nc.vector.tensor_reduce(top[:, w % 4], bank, AX.X, ALU.max).then_inc(top_done, 1)
                    if behind is not None:
                        j2, w2 = behind
                        n2 = W * j2 + w2
                        dve.wait_ge(exp_done, n2 + 1)
                        nc.vector.tensor_reduce(total[:, w2 % 4], prob[:, w2 % 4], AX.X, ALU.add).then_inc(total_done, 1)
                    if ahead is not None:
                        dve.wait_ge(top_done, n + 1)
                        wait(dve, prob_turned, n - 3)
                        nc.vector.tensor_tensor(prob[:, w % 4], bank, softmax_rows(top[:, w % 4]),
                                                ALU.subtract).then_inc(shifted, 1)
                    if behind is not None:
                        dve.wait_ge(total_done, n2 + 1)
                        wait(dve, prob_ready, n2 - 3)
                        nc.vector.reciprocal(inv[:, w2 % 4], total[:, w2 % 4]).then_inc(inv_done, 1)

                def low_o(j, slot):
                    dve.wait_ge(o_hi_done, j + 1)
                    nc.vector.tensor_tensor(S.xT_lo[:, :, bass.ds(j * P, P)], pO[:, slot],
                                            S.xT_hi[:, :, bass.ds(j * P, P)].bitcast(F32), ALU.subtract).then_inc(o_lo_done, 1)

                wait_chunks(dve, V_END)
                copy_v(0)
                soften((0, 0), None)
                soften((0, 1), (0, 0))
                copy_v(1)
                soften((0, 2), (0, 1))
                dve.wait_ge(proj_done, Q_END)

                def body(i):
                    for e in range(2):
                        j = 2 * i + e
                        for w in range(W):
                            steps = [step_ahead(i, e, w, n) for n in (AHEAD, AHEAD - 1)]
                            soften(*[(nj, nw) if exists else None for exists, nj, _, nw in steps])
                            if w == 1 and not is_first(i, e):
                                low_o(j - 1, 1 - e)
                            if w == 3 and two_ahead(i):
                                copy_v(j + 2)

                loop(dve, body)
                low_o(NT - 1, 1)
                for T in range(NT + 2):
                    if T < NT:
                        dve.wait_ge(out_done, T + 1)
                        dve.wait_ge(x_biased, T + 1)
                        nc.vector.tensor_tensor(S.x[:, T], pM[:, T % 2, :], S.x[:, T], ALU.add).then_inc(bank_read[T % 2], 1)
                        dve.wait_ge(bank_read[T % 2], LEFT + T // 2 + 1)
                        norm_out.statistics(T)
                    if T % 2 == 1 and T < NT:
                        norm_out.variances(dve, T // 2)
                    if T % 2 == 0 and T >= 2:
                        norm_out.scale_rows(dve, T // 2 - 1)
                    if T >= 6:
                        for low in range(2 * (T - 6), 2 * (T - 5)):
                            norm_out.low(dve, low)

            @block.gpsimd
            def _(pool):
                def split_w(m, c):
                    pool.wait_ge(w_hi_done, chunk_at[m, c] + 1)
                    wait(pool, proj_done, split_after(m, c))
                    nc.gpsimd.tensor_tensor(W_lo[:, w_slot(m, c)], W_raw[:, c], W_hi[:, w_slot(m, c)].bitcast(F32),
                                            ALU.subtract).then_inc(w_lo_done, 1)

                for m, c in chunk_at:
                    if m < O:
                        split_w(m, c)
                pool.wait_ge(proj_done, V_END)
                nc.gpsimd.memset(Vmask[:], 0.0).then_inc(zeroed, 1)
                pool.wait_ge(small_loaded, 16 * n_small)
                if mixed:
                    pool.wait_ge(x_loaded, 16 * NT)
                else:
                    pool.wait_ge(norm_in.turned, NT)
                for T in range(NT):
                    nc.gpsimd.tensor_tensor(S.x[:, T], S.x[:, T], bo[:], ALU.add).then_inc(x_biased, 1)

                def copy_k(j):
                    nc.gpsimd.tensor_copy(Ktile[:], KT[:, :, bass.ds(j * P, P)]).then_inc(k_copied, 1)

                def place_q(j, slot, places):
                    for place in places:
                        ins = nc.gpsimd.tensor_tensor(Qunit[:, slot, :, place, :], QT[:, :, bass.ds(j * P, P)],
                                                      unit_mask[:, place:place + 1].unsqueeze(2).broadcast_to([P, KC, P]), ALU.mult)
                    if place == U - 1:
                        ins.then_inc(q_ready, 1)

                wait_chunks(pool, Q_HALF)
                for j in range(2):
                    wait(pool, k_ready, j)
                    copy_k(j)
                    place_q(j, j, range(U))
                    for c in range(2 * j, 2 * j + 2):
                        split_w(O, c)

                def divide(j, w):
                    n = W * j + w
                    pool.wait_ge(inv_done, n + 1)
                    nc.gpsimd.tensor_tensor(prob[:, w % 4], prob[:, w % 4], softmax_rows(inv[:, w % 4]),
                                            ALU.mult).then_inc(prob_ready, 1)

                divide(0, 0)
                divide(0, 1)

                def body(i):
                    for e in range(2):
                        for w in range(W):
                            exists, nj, slot, nw = step_ahead(i, e, w, AHEAD - 1)
                            if exists:
                                divide(nj, nw)
                            places = [p for p in {W - 3: (0,), W - 2: (1,), W - 1: (2, 3)}.get(w, ()) if p < U]
                            if w == W - 4 and two_ahead(i):
                                copy_k(2 * i + e + 2)
                            if places and two_ahead(i):
                                place_q(2 * i + e + 2, e, places)

                loop(pool, body)
        ph.close()


def lora_phase(nc, name, S, d, next_loads):
    E, R = 8, 16
    S.begin_phase()
    with ExitStack() as ctx:
        ph = Phase(nc, ctx, name)
        sb, ps, sem = ph.sb, ph.ps, ph.sem
        raw = S.raw[:, 0:7 * DM].rearrange("p (k n) -> p k n", k=7)
        w_hi = sb("w_hi", [P, 7, DM], F32R)
        w_lo = sb("w_lo", [P, 7, DM], F32R)
        A, ROUTER, B, BASE = 0, 1, 2, 3
        base_bias = sb("base_bias", [P, DM])
        router_bias = sb("router_bias", [P, 1])
        inv_k = sb("inv_k", [P, E])
        hT = sb("hT", [P, TOK])
        gT = sb("gT", [P, TOK])
        z = sb("z", [P, NT, E])
        top = sb("top", [P, NT, E])
        run = sb("run", [P, NT, E])
        tau = sb("tau", [P, NT])
        weight = sb("weight", [P, NT, E, R])
        hw = sb("hw", [P, TOK])
        hw_hi = sb("hw_hi", [P, TOK], F32R)
        hw_lo = sb("hw_lo", [P, TOK], F32R)
        banks = ps("banks", [P, 4, DM])
        pA = banks[:, 0:2, :]
        pL = banks[:, 2:4, :].rearrange("p a (t n) -> p (a t) n", n=P)
        pB = ps("pB", [P, 4, DM])
        names = ("small_loaded", "w_hi_done", "w_lo_done", "x_biased", "proj_done", "h_read", "logits_turned",
                 "z_done", "sorted_done", "step", "weight_turned", "hw_done", "hw_hi_done", "hw_lo_done", "out_done", "summed")
        (small_loaded, w_hi_done, w_lo_done, x_biased, proj_done, h_read, logits_turned,
         z_done, sorted_done, step, weight_turned, hw_done, hw_hi_done, hw_lo_done, out_done, summed) = map(sem, names)
        norm = Norm(nc, ph, "out", S, [(T, T + 2) for T in range(0, NT, 2)],
                    lambda T: banks[:, T % 4, :].rearrange("p (k n) -> p k n", k=KC))

        with nc.Block() as block:

            @block.sync
            def _(sp):
                sp.dma_start(base_bias[:], d["base_bias"].broadcast_to([P, DM])).then_inc(small_loaded, 16)
                sp.dma_start(router_bias[:], d["router_bias"]).then_inc(small_loaded, 16)
                sp.dma_start(inv_k[:], d["inv_k"].broadcast_to([P, E])).then_inc(small_loaded, 16)
                sp.wait_ge(w_hi_done, 7)
                sp.wait_ge(w_lo_done, 7)
                S.prefetch(sp, next_loads)

            @block.tensor
            def _(pe):
                for i, w in enumerate((ROUTER, A)):
                    for hf in range(2):
                        pe.wait_ge(w_lo_done, i + 1)
                        if i == 1:
                            pe.wait_ge(h_read, hf + 1)
                        tok = slice(hf * HALF, (hf + 1) * HALF)
                        for k in range(KC):
                            wk = slice(k * P, (k + 1) * P)
                            mm = three_pass(pe, pA[:, hf, :], w_hi[:, w, wk], w_lo[:, w, wk],
                                            S.xT_hi[:, k, tok], S.xT_lo[:, k, tok], k == 0, k == KC - 1)
                        mm.then_inc(proj_done, 1)
                pe.wait_ge(h_read, 2)
                for T in range(NT):
                    mm = pe.transpose(pL[:, T, :], gT[:, T * P:(T + 1) * P], S.ident[:])
                mm.then_inc(logits_turned, 1)

                def base(T):
                    wait(pe, summed, T - 3)
                    cols = slice(T * P, (T + 1) * P)
                    for k in range(KC):
                        pe.wait_ge(w_lo_done, BASE + k + 1)
                        three_pass(pe, pB[:, T % 4, :], S.xT_hi[:, k, cols], S.xT_lo[:, k, cols],
                                   w_hi[:, BASE + k, :], w_lo[:, BASE + k, :], k == 0, False)

                def lora(T):
                    if T % 4 == 0:
                        pe.wait_ge(hw_lo_done, T // 4 + 1)
                    cols = slice(T * P, (T + 1) * P)
                    three_pass(pe, pB[:, T % 4, :], hw_hi[:, cols], hw_lo[:, cols], w_hi[:, B, :], w_lo[:, B, :],
                               False, True).then_inc(out_done, 1)

                for T in range(4):
                    base(T)
                pe.wait_ge(step, E + 4)
                for T in range(NT):
                    mm = pe.transpose(pL[:, T, :], weight[:, T].rearrange("p e r -> p (e r)"), S.ident[:])
                mm.then_inc(weight_turned, 1)
                for T in range(4):
                    lora(T)
                for T in range(4, NT):
                    base(T)
                    lora(T)
                    for turned in {5: (0, 1), 6: (2, 3), 7: (4, 5, 6, 7)}.get(T, ()):
                        norm.turn(pe, turned)

            @block.scalar
            def _(act):
                S.wait_prefetched(act)
                for i in (ROUTER, A, B, BASE, BASE + 1, BASE + 2, BASE + 3):
                    nc.scalar.copy(w_hi[:, i], raw[:, i]).then_inc(w_hi_done, 1)
                act.wait_ge(small_loaded, 48)
                for hf in range(2):
                    act.wait_ge(proj_done, hf + 1)
                    nc.scalar.activation(gT[:, hf * HALF:(hf + 1) * HALF], pA[:, hf, :], ACT.Identity,
                                         bias=router_bias[:, 0:1]).then_inc(h_read, 1)
                for hf in range(2):
                    act.wait_ge(proj_done, 3 + hf)
                    nc.scalar.copy(hT[:, hf * HALF:(hf + 1) * HALF], pA[:, hf, :]).then_inc(h_read, 1)
                for hf in range(2):
                    act.wait_ge(hw_done, hf + 1)
                    nc.scalar.copy(hw_hi[:, hf * HALF:(hf + 1) * HALF], hw[:, hf * HALF:(hf + 1) * HALF]).then_inc(hw_hi_done, 1)
                for i in range(NT // 2):
                    norm.root(act, i)
                    if i > 0:
                        norm.high(act, 2 * i - 2)
                        norm.high(act, 2 * i - 1)
                for T in range(NT - 2, NT):
                    norm.high(act, T)

            @block.vector
            def _(dve):
                dve.wait_ge(small_loaded, 48)
                dve.wait_ge(logits_turned, 1)
                nc.vector.tensor_copy(z[:], pL[:, :, :].rearrange("p t (e r) -> p t e r", r=R)[:, :, :, 0]).then_inc(z_done, 1)
                dve.wait_ge(z_done, 1)
                for T in range(NT):
                    nc.vector.max(top[:, T], z[:, T]).then_inc(sorted_done, 1)
                dve.wait_ge(sorted_done, NT)

                def link(n, instruction):
                    instruction.then_inc(step, 1)
                    dve.wait_ge(step, n)

                link(1, nc.vector.tensor_scalar(run[:, :, 0:1], top[:, :, 0:1], -1.0, None, ALU.add))
                for k in range(1, E):
                    link(k + 1, nc.vector.tensor_tensor(run[:, :, k:k + 1], run[:, :, k - 1:k], top[:, :, k:k + 1], ALU.add))
                link(E + 1, nc.vector.tensor_tensor(run[:], run[:], inv_k[:].unsqueeze(1).broadcast_to([P, NT, E]), ALU.mult))
                link(E + 2, nc.vector.tensor_reduce(tau[:], run[:], AX.X, ALU.max))
                link(E + 3, nc.vector.tensor_tensor(z[:], z[:], tau[:].unsqueeze(2).broadcast_to([P, NT, E]), ALU.subtract))
                link(E + 4, nc.vector.tensor_scalar(weight[:], z[:].unsqueeze(3).broadcast_to([P, NT, E, R]), 0.0, None, ALU.max))
                dve.wait_ge(h_read, 4)
                dve.wait_ge(weight_turned, 1)
                for hf in range(2):
                    tok = slice(hf * HALF, (hf + 1) * HALF)
                    nc.vector.tensor_tensor(hw[:, tok], hT[:, tok], pL[:, 4 * hf:4 * hf + 4, :].rearrange("p t n -> p (t n)"),
                                            ALU.mult).then_inc(hw_done, 1)
                for hf in range(2):
                    tok = slice(hf * HALF, (hf + 1) * HALF)
                    dve.wait_ge(hw_hi_done, hf + 1)
                    nc.vector.tensor_tensor(hw_lo[:, tok], hw[:, tok], hw_hi[:, tok].bitcast(F32),
                                            ALU.subtract).then_inc(hw_lo_done, 1)
                for T in range(NT + 2):
                    if T < NT:
                        dve.wait_ge(out_done, T + 1)
                        dve.wait_ge(x_biased, T + 1)
                        nc.vector.tensor_tensor(S.x[:, T], pB[:, T % 4, :], S.x[:, T], ALU.add).then_inc(summed, 1)
                        dve.wait_ge(summed, T + 1)
                        norm.statistics(T)
                    if T % 2 == 1 and T < NT:
                        norm.variances(dve, T // 2)
                    if T % 2 == 0 and T >= 2:
                        norm.scale_rows(dve, T // 2 - 1)
                    if T >= 6:
                        for low in range(2 * (T - 6), 2 * (T - 5)):
                            norm.low(dve, low)

            @block.gpsimd
            def _(pool):
                for n, i in enumerate((ROUTER, A, B, BASE, BASE + 1, BASE + 2, BASE + 3)):
                    pool.wait_ge(w_hi_done, n + 1)
                    nc.gpsimd.tensor_tensor(w_lo[:, i], raw[:, i], w_hi[:, i].bitcast(F32), ALU.subtract).then_inc(w_lo_done, 1)
                pool.wait_ge(small_loaded, 48)
                for T in range(NT):
                    nc.gpsimd.tensor_tensor(S.x[:, T], S.x[:, T], base_bias[:], ALU.add).then_inc(x_biased, 1)
        ph.close()


def experts_phase(nc, name, S, d, out):
    E, G, X = 16, 4, 18
    S.begin_phase()
    with ExitStack() as ctx:
        ph = Phase(nc, ctx, name)
        sb, ps, sem = ph.sb, ph.ps, ph.sem
        raw = S.raw[:, 0:2 * EW].rearrange("p (s n) -> p s n", s=2)
        w12_hi = sb("w12_hi", [P, 2, 2 * DM], F32R)
        w12_lo = sb("w12_lo", [P, 2, 2 * DM], F32R)
        w3_hi = sb("w3_hi", [P, 2, DM], F32R)
        w3_lo = sb("w3_lo", [P, 2, DM], F32R)
        r_raw = S.raw[:, 2 * EW:2 * EW + DM]
        r_hi = sb("r_hi", [P, DM], F32R)
        r_lo = sb("r_lo", [P, DM], F32R)
        r_bias = sb("r_bias", [P, 1])
        s_bias = sb("s_bias", [P, E])
        before = sb("before", [P, E, E])
        b3 = sb("b3", [X, DM])
        gT = sb("gT", [P, TOK])
        score = sb("score", [P, NT, E])
        masked = sb("masked", [P, NT, E])
        stat = sb("stat", [P, NT])
        gmax = sb("gmax", [P, NT, G])
        keep = sb("keep", [P, NT, G])
        cmp = sb("cmp", [P, NT, E, E])
        same = sb("same", [P, NT, E, E])
        rank = sb("rank", [P, NT, E])
        gate = sb("gate", [P, NT, X])
        gateT = sb("gateT", [X, TOK])
        act_out = sb("act_out", [P, 2, HALF])
        hid = sb("hid", [P, 2, HALF])
        hid_hi = sb("hid_hi", [P, 2, 2, HALF], F32R)
        hid_lo = sb("hid_lo", [P, 2, 2, HALF], F32R)
        pH = ps("pH", [P, 2, 2, HALF])
        pY = ps("pY", [P, 4, DM])
        names = ("small_loaded", "r_hi_done", "r_lo_done", "r_done", "r_read", "r_turned", "step", "exp_done", "gate_set",
                 "gate_turned", "gateT_read", "b3_done", "w12_hi_done", "w12_lo_done", "w3_hi_done", "w3_lo_done",
                 "hid_done", "silu_done", "hid_ready", "hid_hi_done", "hid_lo_done", "y_done", "summed")
        (small_loaded, r_hi_done, r_lo_done, r_done, r_read, r_turned, step, exp_done, gate_set,
         gate_turned, gateT_read, b3_done, w12_hi_done, w12_lo_done, w3_hi_done, w3_lo_done,
         hid_done, silu_done, hid_ready, hid_hi_done, hid_lo_done, y_done, summed) = map(sem, names)
        w_loaded = [sem(f"w_loaded{i}") for i in range(2)]
        stored = sem("stored")
        norm = Norm(nc, ph, "out", S, [(0, 4), (4, 8)])
        STEPS = 18

        def bcast(ap, dim, n):
            shape = list(ap.shape)
            shape.insert(dim, n)
            return ap.unsqueeze(dim).broadcast_to(shape)

        def loop(engine, body):
            body(0)
            with engine.Fori(1, X // 2 - 1) as i:
                body(i)
            body(X // 2 - 1)

        def exists(i, e2, ahead):
            return not (isinstance(i, int) and 2 * i + e2 + ahead >= X)

        with nc.Block() as block:

            @block.sync
            def _(sp):
                for dst, src in ((r_bias, d["r_bias"]), (s_bias, d["s_bias"].broadcast_to([P, E])),
                                 (before, d["before"].broadcast_to([P, E * E])), (b3, d["b3"])):
                    to = dst[:].rearrange("p i j -> p (i j)") if dst is before else dst[:]
                    sp.dma_start(to, src).then_inc(small_loaded, 16)

                def body(i):
                    for e2 in range(2):
                        e = 2 * i + e2
                        sp.wait_ge(hid_ready, 2 * (e - 1))
                        sp.wait_ge(w3_hi_done, e - 1)
                        sp.wait_ge(w3_lo_done, e - 1)
                        sp.dma_start(raw[:, e2], d["w"][e]).then_inc(w_loaded[e2], 16)

                with sp.Fori(1, X // 2) as i:
                    body(i)
                for T in range(NT):
                    sp.wait_ge(norm.normed, T + 1)
                    sp.dma_start(out[T], S.x[:, T]).then_inc(stored, 16)
                sp.wait_ge(stored, 16 * NT)

            @block.tensor
            def _(pe):
                pe.wait_ge(r_hi_done, 1)
                pe.wait_ge(r_lo_done, 1)
                for hf in range(2):
                    tok = slice(hf * HALF, (hf + 1) * HALF)
                    for k in range(KC):
                        wk = slice(k * P, (k + 1) * P)
                        mm = three_pass(pe, pY[:, hf, :], r_hi[:, wk], r_lo[:, wk],
                                        S.xT_hi[:, k, tok], S.xT_lo[:, k, tok], k == 0, k == KC - 1)
                    mm.then_inc(r_done, 1)
                pe.wait_ge(r_read, 2)
                for T in range(NT):
                    mm = pe.transpose(pY[:, 2 + T // 4, (T % 4) * P:(T % 4 + 1) * P], gT[:, T * P:(T + 1) * P], S.ident[:])
                mm.then_inc(r_turned, 1)

                def hidden(e, slot, hf):
                    if hf == 0:
                        pe.wait_ge(w12_hi_done, e + 1)
                        pe.wait_ge(w12_lo_done, e + 1)
                    wait(pe, silu_done, 2 * e - 1 + hf)
                    wait(pe, hid_ready, 2 * e - 1 + hf)
                    tok = slice(hf * HALF, (hf + 1) * HALF)
                    for m in range(2):
                        for k in range(KC):
                            wk = slice(m * DM + k * P, m * DM + (k + 1) * P)
                            mm = three_pass(pe, pH[:, m, hf, :], w12_hi[:, slot, wk], w12_lo[:, slot, wk],
                                            S.xT_hi[:, k, tok], S.xT_lo[:, k, tok], k == 0, k == KC - 1)
                    mm.then_inc(hid_done, 1)

                def output(e, slot, hf):
                    pe.wait_ge(hid_lo_done, 2 * e + hf + 1)
                    if hf == 0:
                        pe.wait_ge(w3_hi_done, e + 1)
                        pe.wait_ge(w3_lo_done, e + 1)
                    for t in range(4):
                        wait(pe, summed, 8 * (e + 1) + 4 * hf + t - 3)
                        cols = slice(t * P, (t + 1) * P)
                        three_pass(pe, pY[:, t, :], hid_hi[:, slot, hf, cols], hid_lo[:, slot, hf, cols],
                                   w3_hi[:, slot, :], w3_lo[:, slot, :], True, True).then_inc(y_done, 1)

                for hf in range(2):
                    hidden(0, 0, hf)
                def shared_biases():
                    pe.wait_ge(step, STEPS)
                    for T in range(NT):
                        bank = pY[0:X, T // 4, (T % 4) * P:(T % 4 + 1) * P]
                        mm = pe.transpose(bank, gate[:, T, :], S.ident[:])
                    mm.then_inc(gate_turned, 1)
                    pe.wait_ge(gateT_read, 1)
                    for T in range(NT):
                        wait(pe, summed, T - 3)
                        pe.matmul(pY[:, T % 4, :], gateT[:, T * P:(T + 1) * P], b3[:, :],
                                  start=True, stop=True, skip_group_check=True).then_inc(b3_done, 1)

                def body(i):
                    for e2 in range(2):
                        e = 2 * i + e2
                        for hf in range(2):
                            if exists(i, e2, 1):
                                hidden(e + 1, 1 - e2, hf)
                            if isinstance(e, int) and e == 0 and hf == 0:
                                shared_biases()
                            output(e, e2, hf)

                loop(pe, body)

            @block.scalar
            def _(act):
                S.wait_prefetched(act)
                nc.scalar.copy(r_hi[:], r_raw[:]).then_inc(r_hi_done, 1)

                def split(e, slot, i, n12):
                    if isinstance(i, int) and i == 0:
                        S.wait_prefetched(act)
                    else:
                        act.wait_ge(w_loaded[slot], 16 * i)
                    if n12:
                        wait(act, hid_done, 2 * (e - 1))
                        nc.scalar.copy(w12_hi[:, slot], raw[:, slot, 0:2 * DM]).then_inc(w12_hi_done, 1)
                    else:
                        wait(act, y_done, 8 * (e - 1))
                        nc.scalar.copy(w3_hi[:, slot], raw[:, slot, 2 * DM:3 * DM]).then_inc(w3_hi_done, 1)

                def silu(e, slot, hf):
                    act.wait_ge(hid_done, 2 * e + hf + 1)
                    wait(act, hid_ready, 2 * e - 1 + hf)
                    nc.scalar.activation(act_out[:, hf], pH[:, 0, hf, :], ACT.Silu,
                                         bias=raw[:, slot, 3 * DM:3 * DM + 1]).then_inc(silu_done, 1)

                def high(e, slot, hf):
                    act.wait_ge(hid_ready, 2 * e + hf + 1)
                    wait(act, y_done, 8 * (e - 1))
                    nc.scalar.copy(hid_hi[:, slot, hf], hid[:, hf]).then_inc(hid_hi_done, 1)

                split(0, 0, 0, True)
                act.wait_ge(small_loaded, 64)
                for hf in range(2):
                    act.wait_ge(r_done, hf + 1)
                    nc.scalar.activation(gT[:, hf * HALF:(hf + 1) * HALF], pY[:, hf, :], ACT.Identity,
                                         bias=r_bias[:, 0:1]).then_inc(r_read, 1)
                split(1, 1, 0, True)
                split(0, 0, 0, False)
                act.wait_ge(step, 2)
                nc.scalar.activation(score[:], score[:], ACT.Exp).then_inc(exp_done, 1)
                for hf in range(2):
                    silu(0, 0, hf)
                    high(0, 0, hf)
                act.wait_ge(gate_turned, 1)
                nc.scalar.copy(gateT[:], pY[0:X, 0:2, :].rearrange("p t n -> p (t n)")).then_inc(gateT_read, 1)

                def body(i):
                    for e2 in range(2):
                        e = 2 * i + e2
                        if exists(i, e2, 1):
                            split(e + 1, 1 - e2, i + e2, False)
                            silu(e + 1, 1 - e2, 0)
                            high(e + 1, 1 - e2, 0)
                        if exists(i, e2, 2):
                            split(e + 2, e2, i + 1, True)
                        if exists(i, e2, 1):
                            silu(e + 1, 1 - e2, 1)
                            high(e + 1, 1 - e2, 1)

                loop(act, body)
                for i in range(len(norm.groups)):
                    norm.root(act, i)

            @block.vector
            def _(dve):
                dve.wait_ge(small_loaded, 64)

                def link(n, instruction):
                    instruction.then_inc(step, 1)
                    dve.wait_ge(step, n)

                def hidden_product(e, slot, hf):
                    dve.wait_ge(silu_done, 2 * e + hf + 1)
                    wait(dve, hid_lo_done, 2 * e - 1 + hf)
                    nc.vector.scalar_tensor_tensor(out=hid[:, hf], in0=pH[:, 1, hf, :], scalar=raw[:, slot, 3 * DM + 1:3 * DM + 2],
                                                   in1=act_out[:, hf], op0=ALU.add, op1=ALU.mult).then_inc(hid_ready, 1)

                def low(e, slot, hf):
                    dve.wait_ge(hid_hi_done, 2 * e + hf + 1)
                    nc.vector.tensor_tensor(hid_lo[:, slot, hf], hid[:, hf], hid_hi[:, slot, hf].bitcast(F32),
                                            ALU.subtract).then_inc(hid_lo_done, 1)

                def add_output(e, hf):
                    for t in range(4):
                        T = 4 * hf + t
                        dve.wait_ge(y_done, 8 * e + T + 1)
                        dve.wait_ge(summed, 8 * e + T + 1)
                        nc.vector.scalar_tensor_tensor(out=S.x[:, T], in0=pY[:, t, :], scalar=gate[:, T, bass.ds(e, 1)],
                                                       in1=S.x[:, T], op0=ALU.mult, op1=ALU.add).then_inc(summed, 1)

                dve.wait_ge(r_turned, 1)
                logits = pY[:, 2:4, :].rearrange("p a (t e r) -> p (a t) e r", t=4, r=P // E)[:, :, :, 0]
                link(1, nc.vector.tensor_reduce(stat[:], logits, AX.X, ALU.max))
                link(2, nc.vector.tensor_tensor(score[:], logits, bcast(stat[:], 2, E), ALU.subtract))
                dve.wait_ge(exp_done, 1)
                link(3, nc.vector.tensor_reduce(stat[:], score[:], AX.X, ALU.add))
                link(4, nc.vector.reciprocal(stat[:], stat[:]))
                link(5, nc.vector.tensor_tensor(score[:], score[:], bcast(stat[:], 2, E), ALU.mult))
                link(6, nc.vector.tensor_tensor(score[:], score[:], bcast(s_bias[:], 1, NT), ALU.add))

                def ranks(n, values, m, out):
                    c, s = cmp[:, :, 0:m, 0:m], same[:, :, 0:m, 0:m]
                    mine, other = bcast(values, 3, m), bcast(values, 2, m)
                    nc.vector.tensor_tensor(c, other, mine, ALU.is_gt)
                    link(n, nc.vector.tensor_tensor(s, other, mine, ALU.is_equal))
                    link(n + 1, nc.vector.tensor_tensor(s, s, bcast(before[:, 0:m, 0:m], 1, NT), ALU.mult))
                    link(n + 2, nc.vector.tensor_tensor(c, c, s, ALU.add))
                    link(n + 3, nc.vector.tensor_reduce(out, c, AX.X, ALU.add))

                link(7, nc.vector.tensor_reduce(gmax[:], score[:].rearrange("p t (g i) -> p t g i", g=G), AX.X, ALU.max))
                ranks(8, gmax[:], G, keep[:])
                link(12, nc.vector.tensor_scalar(keep[:], keep[:], 1.5, None, ALU.is_lt))
                grouped = lambda a: a[:].rearrange("p t (g i) -> p t g i", g=G)
                nc.vector.tensor_tensor(grouped(masked), grouped(score), bcast(keep[:], 3, G), ALU.mult)
                link(13, nc.vector.tensor_scalar(gmax[:], keep[:], -MASKED, MASKED, ALU.mult, ALU.add))
                nc.vector.tensor_tensor(grouped(masked), grouped(masked), bcast(gmax[:], 3, G), ALU.add).then_inc(gate_set, 1)
                dve.wait_ge(gate_set, 1)
                hidden_product(0, 0, 0)
                low(0, 0, 0)
                ranks(14, masked[:], E, rank[:])
                nc.vector.memset(gate[:, :, 0:2], 1.0)
                nc.vector.scalar_tensor_tensor(out=gate[:, :, 2:X], in0=rank[:], scalar=1.5, in1=score[:],
                                               op0=ALU.is_lt, op1=ALU.mult).then_inc(step, 1)
                hidden_product(0, 0, 1)
                low(0, 0, 1)
                for T in range(NT):
                    dve.wait_ge(b3_done, T + 1)
                    nc.vector.tensor_tensor(S.x[:, T], pY[:, T % 4, :], S.x[:, T], ALU.add).then_inc(summed, 1)

                def body(i):
                    for e2 in range(2):
                        e = 2 * i + e2
                        for hf in range(2):
                            if exists(i, e2, 1):
                                hidden_product(e + 1, 1 - e2, hf)
                                low(e + 1, 1 - e2, hf)
                            add_output(e, hf)
                            if isinstance(e, int) and e == X - 1:
                                if hf == 0:
                                    dve.wait_ge(summed, 8 * X + 4)
                                    for T in range(4):
                                        norm.statistics(T)
                                    norm.variances(dve, 0)

                loop(dve, body)
                dve.wait_ge(summed, 8 * X + 8)
                for T in range(4, NT):
                    norm.statistics(T)
                norm.variances(dve, 1)
                for i in range(2):
                    norm.scale_rows(dve, i)

            @block.gpsimd
            def _(pool):
                pool.wait_ge(r_hi_done, 1)
                nc.gpsimd.tensor_tensor(r_lo[:], r_raw[:], r_hi[:].bitcast(F32), ALU.subtract).then_inc(r_lo_done, 1)

                def split(e, slot, n12):
                    if n12:
                        pool.wait_ge(w12_hi_done, e + 1)
                        wait(pool, hid_done, 2 * (e - 1))
                        nc.gpsimd.tensor_tensor(w12_lo[:, slot], raw[:, slot, 0:2 * DM], w12_hi[:, slot].bitcast(F32),
                                                ALU.subtract).then_inc(w12_lo_done, 1)
                    else:
                        pool.wait_ge(w3_hi_done, e + 1)
                        wait(pool, y_done, 8 * (e - 1))
                        nc.gpsimd.tensor_tensor(w3_lo[:, slot], raw[:, slot, 2 * DM:3 * DM], w3_hi[:, slot].bitcast(F32),
                                                ALU.subtract).then_inc(w3_lo_done, 1)

                split(0, 0, True)
                split(1, 1, True)
                split(0, 0, False)

                def body(i):
                    for e2 in range(2):
                        e = 2 * i + e2
                        if exists(i, e2, 1):
                            split(e + 1, 1 - e2, False)
                        if exists(i, e2, 2):
                            split(e + 2, e2, True)

                loop(pool, body)
        ph.close()


def decoder(nc, d, out):
    with ExitStack() as ctx:
        S = State(nc, ctx)
        run_phases(nc, d, out, S)


def run_phases(nc, d, out, S):
    scratch = nc.dram_tensor("x_natural", (NT, P, DM), F32).ap()
    sub = lambda prefix: {k[len(prefix):]: v for k, v in d.items() if k.startswith(prefix)}
    attention_first = lambda layer: [(S.raw[:, 0:CH * DM], d[f"l{layer}_wqkv"][0]),
                                     (S.raw[:, CH * DM:(CH + QPG) * DM], d[f"l{layer}_wo"][0])]
    cross_first = lambda layer: [(S.raw[:, 0:KC * DM], d[f"x{layer}_w_k"]),
                                 (S.raw[:, KC * DM:2 * KC * DM], d["ctxT"][0])]
    lora_first = [(S.raw[:, 0:7 * DM], d["f0_w"])]
    experts_first = [(S.raw[:, 2 * EW:2 * EW + DM], d["f1_r_w"])]
    experts_first += [(S.raw[:, e * EW:(e + 1) * EW], d["f1_w"][e]) for e in range(2)]
    steps = [
        lambda: attention_phase(nc, "l0a", S, d["l0_wqkv"], d["l0_wo"], d["mask0"], True, cross_first(0),
                                xT_raw_dram=d["xT_perm"], x_rows_dram=d["x_rows"], ident_dram=d["ident"]),
        lambda: cross_attention_phase(nc, "l0x", S, sub("x0_"), 32, d["ctxT"][1], lora_first, scratch),
        lambda: lora_phase(nc, "l0f", S, sub("f0_"), attention_first(1)),
        lambda: attention_phase(nc, "l1a", S, d["l1_wqkv"], d["l1_wo"], d["mask1"], False, cross_first(1),
                                rope_dram=d["rope"]),
        lambda: cross_attention_phase(nc, "l1x", S, sub("x1_"), 64, d["ctxT"][1], experts_first),
        lambda: experts_phase(nc, "l1f", S, sub("f1_"), out),
    ]
    for step in steps:
        step()


def _rows(a):
    return a.reshape(4, 4, 2, 32, -1).transpose(2, 0, 1, 3, 4).reshape(NT, P, -1)


def _k_major(w):
    K, n = w.shape
    return w.reshape(K // P, P, n).transpose(1, 0, 2).reshape(P, -1)


def _group_weights(w):
    return w.reshape(GROUPS, CH, P, KC, P).transpose(0, 4, 1, 3, 2).reshape(GROUPS, P, -1)


def _out_weights(w):
    return w.reshape(DM, GROUPS, QPG, HD).transpose(1, 3, 2, 0).reshape(GROUPS, P, -1)


def _constants():
    bf = np.dtype("bfloat16")
    i = np.arange(P)
    causal = i[:, None] >= i[None, :]
    mask0 = causal & (i[:, None] // SEQ_A == i[None, :] // SEQ_A)
    mask1 = causal & (i[:, None] // SEQ_B == i[None, :] // SEQ_B)
    inv = 1.0 / 500000.0 ** (np.arange(0, HD, 2, dtype=np.float32) / HD)
    wavelen = 2.0 * np.pi / inv
    low, high = 1024 / 1.0, 1024 / 4.0
    scaled = np.where(wavelen > low, inv / 8.0, inv)
    smooth = (1024 / wavelen - 1.0) / (4.0 - 1.0)
    smoothed = (1.0 - smooth) / 8.0 * inv + smooth * inv
    freq = np.where((wavelen <= low) & (wavelen >= high), smoothed, scaled).astype(np.float32)
    angle = (np.arange(SEQ_B, dtype=np.float32)[None, :] * np.concatenate([freq, freq])[:, None]).astype(np.float32)
    sign = np.where(i[:, None] < HD // 2, 1.0, -1.0)
    rope = np.stack([np.cos(angle.astype(np.float64)), sign * np.sin(angle.astype(np.float64))]).astype(np.float32)
    return {
        "ident": np.eye(P, dtype=np.float32),
        "mask0": np.where(mask0, 0.0, MASKED).astype(np.float32).astype(bf),
        "mask1": np.where(mask1, 0.0, MASKED).astype(np.float32).astype(bf),
        "rope": rope,
        "f0_inv_k": (1.0 / np.arange(1, 9, dtype=np.float32)).reshape(1, 8),
        "f1_before": (np.arange(16)[:, None] > np.arange(16)[None, :]).astype(np.float32).reshape(1, 256),
        "x0_row_mask": (i[:, None] % 4 == np.arange(4)).astype(np.float32),
        "x1_row_mask": (i[:, None] // 16 % 4 == np.arange(4)).astype(np.float32),
        "x0_unit_mask": (i[:, None] // 32 == np.arange(4)).astype(np.float32),
        "x1_unit_mask": (i[:, None] // 64 == np.arange(2)).astype(np.float32),
        "x0_same": (i[:, None] // 4 == np.arange(32)).astype(np.float32),
    }


def _lay_out(i):
    n = {k: np.asarray(v) for k, v in i.items()}
    a = _constants()
    x = n["x"]
    a["x_rows"] = _rows(x)
    halves = lambda xT: np.stack([_k_major(xT[:, :HALF]), _k_major(xT[:, HALF:])])
    a["xT_perm"] = halves(x.transpose(2, 1, 0).reshape(DM, TOK))
    a["ctxT"] = halves(n["ctx_4096"].reshape(TOK, DM).T)
    w = n["L0_attn_weight_qkv"].reshape(GROUPS, CH, P, DM)
    a["l0_wqkv"] = _group_weights(np.concatenate([w[:, 4:6], w[:, 0:4]], axis=1))
    a["l0_wo"] = _out_weights(n["L0_attn_weight_proj"])
    w = np.concatenate([n["L1_attn_Wk"].reshape(GROUPS, 1, P, DM), n["L1_attn_Wv"].reshape(GROUPS, 1, P, DM),
                        n["L1_attn_Wq"].reshape(GROUPS, QPG, P, DM)], axis=1)
    a["l1_wqkv"] = _group_weights(w)
    a["l1_wo"] = _out_weights(n["L1_attn_Wo"])
    for layer in range(2):
        o, x = f"L{layer}_xattn_", f"x{layer}_"
        if layer == 0:
            wk, wv, wq, wo = [n[o + k].T for k in ("Wk", "Wv", "Wq", "Wo")]
            bk, bv, bq = n[o + "bk"], n[o + "bv"], n[o + "bq"]
            a[x + "inter"] = np.repeat(n[o + "interference"].reshape(KC, 4, 1, 4, 4), 8, axis=2).reshape(KC, P, 4).transpose(1, 0, 2)
            a[x + "amp"] = n[o + "amp"].reshape(1, 1)
        else:
            share = lambda w: np.repeat(w.reshape(-1, 8, 1, 16), 4, axis=2).reshape(w.shape[0] if w.ndim > 1 else 1, DM)
            wk, wv, wq, wo = share(n[o + "Wk"]), n[o + "Wv"], n[o + "Wq"], n[o + "Wo"]
            bk, bv, bq = share(n[o + "bk"]), n[o + "bv"], n[o + "bq"]
        by_chunk = lambda w: w.reshape(KC, P, -1, P).transpose(1, 2, 0, 3).reshape(P, -1)
        for name, w in (("k", by_chunk(wk)), ("v", by_chunk(wv)), ("q", by_chunk(wq)), ("o", _k_major(wo))):
            a[x + "w_" + name] = w
        a[x + "biases"] = np.stack([np.resize(b, DM).reshape(KC, P).T for b in (bk, bv, bq)], axis=1)
        a[x + "bo"] = n[o + "bo"].reshape(1, DM)
    f = "L0_ffn_"
    lora_a = n[f + "lora_A"].transpose(1, 0, 2).reshape(DM, P)
    router = np.repeat(n[f + "W_router"].T, P // 8, axis=1)
    a["f0_w"] = np.concatenate([_k_major(lora_a), _k_major(router), n[f + "lora_B"].reshape(P, DM),
                                _k_major(n[f + "W_base"].T)], axis=1)
    a["f0_base_bias"] = n[f + "b_base"].reshape(1, DM)
    a["f0_router_bias"] = np.repeat(n[f + "b_router"], P // 8).reshape(P, 1)
    f = "L1_ffn_"
    two = lambda w: w.reshape(DM, 2, P).transpose(1, 0, 2)
    w1 = np.concatenate([two(n[f + "sw1"]), n[f + "ew1"]])
    w2 = np.concatenate([two(n[f + "sw2"]), n[f + "ew2"]])
    w3 = np.concatenate([n[f + "sw3"].reshape(2, P, DM), n[f + "ew3"]])
    b1 = np.concatenate([n[f + "sb1"].reshape(2, P), n[f + "eb1"]])
    b2 = np.concatenate([n[f + "sb2"].reshape(2, P), n[f + "eb2"]])
    a["f1_w"] = np.concatenate([np.stack([_k_major(w) for w in w1]), np.stack([_k_major(w) for w in w2]), w3,
                                b1[:, :, None], b2[:, :, None]], axis=2)
    a["f1_b3"] = np.concatenate([n[f + "sb3"].reshape(1, DM), np.zeros((1, DM), np.float32), n[f + "eb3"]])
    a["f1_r_w"] = _k_major(np.repeat(n[f + "router_w"], P // 16, axis=1))
    a["f1_r_bias"] = np.repeat(n[f + "router_b"], P // 16).reshape(P, 1)
    a["f1_s_bias"] = n[f + "router_bias"].reshape(1, 16)
    return {k: np.ascontiguousarray(v) for k, v in a.items()}


def kernel(**inputs):
    import concourse.bacc as _bacc
    from concourse.bass_utils import run_bass_kernel_spmd as _run

    nc = _bacc.Bacc("TRN2", target_bir_lowering=False, num_devices=1)
    arrays = _lay_out(inputs)
    d = {k: nc.dram_tensor(f"in_{k}_dram", v.shape, mybir.dt.from_np(v.dtype), kind="ExternalInput").ap()
         for k, v in arrays.items()}
    out = nc.dram_tensor("out_0_dram", (NT, P, DM), F32, kind="ExternalOutput").ap()
    decoder(nc, d, out)
    r = _run(nc, [{f"in_{k}_dram": v for k, v in arrays.items()}], core_ids=[0])
    rows = r.results[0]["out_0_dram"]
    return rows.reshape(SEQ_A, SEQ_B, DM)
```
